# Optimizing a Trainium2 kernel written in Bass

```python
import numpy as np
import jax
import jax.numpy as jnp

def _softmax(x, axis=-1):
    return jax.nn.softmax(x, axis=axis)

def _gelu(x):
    return jax.nn.gelu(x, approximate=True)

def _silu(x):
    return jax.nn.silu(x)

def _sigmoid(x):
    return jax.nn.sigmoid(x)

def _layernorm(x, axis=-1, eps=1e-05):
    m = jnp.mean(x, axis=axis, keepdims=True)
    v = jnp.var(x, axis=axis, keepdims=True)
    return (x - m) / jnp.sqrt(v + eps)

def _scatter_add(tgt, idx, src, axis=0):
    return tgt.at[idx].add(src)

def _segment_sum(src, seg, n):
    return jax.ops.segment_sum(src, seg, n)
kernel_name = 'mk_adaln_d2_jaxref_r8_23abb9'

def setup_inputs(seed: int=0):
    np.random.seed(seed)
    _w = jnp.asarray

    def _L0_attn_setup():
        import jax, jax.numpy as jnp
        import numpy as np
        D_MODEL = 256
        D_STATE = 128
        HEADDIM = 64
        EXPAND = 2
        D_CONV = 4
        NGROUPS = 1
        CHUNK = 32
        EPS = 1e-05
        D_INNER = EXPAND * D_MODEL
        NHEADS = D_INNER // HEADDIM
        CONV_DIM = D_INNER + 2 * NGROUPS * D_STATE
        D_IN_PROJ = 2 * D_INNER + 2 * NGROUPS * D_STATE + NHEADS

        def _segsum(a):
            T = a.shape[-1]
            cs = jnp.cumsum(a, axis=-1)
            d = cs[..., :, None] - cs[..., None, :]
            mask = jnp.tril(jnp.ones((T, T), dtype=bool))
            return jnp.where(mask, d, -jnp.inf)

        def _ssd(X, A, Bm, Cm):
            b, l, h, p = X.shape
            n = Bm.shape[-1]
            c = l // CHUNK
            X = X.reshape(b, c, CHUNK, h, p)
            A = A.reshape(b, c, CHUNK, h).transpose(0, 3, 1, 2)
            Bm = Bm.reshape(b, c, CHUNK, n)
            Cm = Cm.reshape(b, c, CHUNK, n)
            A_cs = jnp.cumsum(A, axis=-1)
            Lmat = jnp.exp(_segsum(A))
            Y_diag = jnp.einsum('bcln,bcsn,bhcls,bcshp->bclhp', Cm, Bm, Lmat, X)
            decay_states = jnp.exp(A_cs[..., -1:] - A_cs)
            states = jnp.einsum('bcln,bhcl,bclhp->bchpn', Bm, decay_states, X)
            A_last = jnp.pad(A_cs[..., -1], ((0, 0), (0, 0), (1, 0)))
            decay_chunk = jnp.exp(_segsum(A_last))
            states = jnp.concatenate([jnp.zeros_like(states[:, :1]), states], axis=1)
            states = jnp.einsum('bhzc,bchpn->bzhpn', decay_chunk, states)[:, :-1]
            Y_off = jnp.einsum('bchpn,bcln,bhcl->bclhp', states, Cm, jnp.exp(A_cs))
            return (Y_diag + Y_off).reshape(b, l, h, p)

        def _mamba2(x, w_in, conv_w, conv_b, dt_bias, A_log, D, norm_w, w_out):
            B, L, _ = x.shape
            zxbcdt = jnp.einsum('bld,de->ble', x, w_in)
            z = zxbcdt[..., :D_INNER]
            xBC = zxbcdt[..., D_INNER:D_INNER + CONV_DIM]
            dt = zxbcdt[..., D_INNER + CONV_DIM:]
            dt = jax.nn.softplus(dt + dt_bias)
            xp = jnp.pad(xBC, ((0, 0), (D_CONV - 1, 0), (0, 0)))
            acc = conv_b
            xBC = sum((conv_w[:, k] * xp[:, k:k + L, :] for k in range(D_CONV))) + conv_b
            xBC = jax.nn.silu(xBC)
            xh = xBC[..., :D_INNER].reshape(B, L, NHEADS, HEADDIM)
            Bm = xBC[..., D_INNER:D_INNER + NGROUPS * D_STATE]
            Cm = xBC[..., D_INNER + NGROUPS * D_STATE:]
            A = -jnp.exp(A_log)
            y = _ssd(xh * dt[..., None], dt * A, Bm, Cm)
            y = y + xh * D[None, None, :, None]
            y = y.reshape(B, L, D_INNER)
            y = y * jax.nn.silu(z)
            y = y * jax.lax.rsqrt(jnp.mean(y * y, axis=-1, keepdims=True) + EPS) * norm_w
            return jnp.einsum('ble,ed->bld', y, w_out)
        key = jax.random.key(seed)
        ks = jax.random.split(key, 9)
        B, L = (2, 256)
        x = jax.random.normal(ks[0], (B, L, D_MODEL), jnp.float32)
        w_in = jax.random.normal(ks[1], (D_MODEL, D_IN_PROJ), jnp.float32) * D_MODEL ** (-0.5)
        conv_w = jax.random.normal(ks[2], (CONV_DIM, D_CONV), jnp.float32) * 0.2
        conv_b = jnp.zeros((CONV_DIM,), jnp.float32)
        dt_bias = jax.random.uniform(ks[3], (NHEADS,), jnp.float32, -4.0, -1.0)
        A_log = jnp.log(jax.random.uniform(ks[4], (NHEADS,), jnp.float32, 1.0, 16.0))
        D = jnp.ones((NHEADS,), jnp.float32)
        norm_w = jnp.ones((D_INNER,), jnp.float32)
        w_out = jax.random.normal(ks[5], (D_INNER, D_MODEL), jnp.float32) * D_INNER ** (-0.5)
        return {'x': x, 'w_in': w_in, 'conv_w': conv_w, 'conv_b': conv_b, 'dt_bias': dt_bias, 'A_log': A_log, 'D': D, 'norm_w': norm_w, 'w_out': w_out}
    _L0_attn_in = _L0_attn_setup()

    def _L0_ffn_setup():
        import jax, jax.numpy as jnp
        import numpy as np
        COST_LAMBDA = 1e-07
        HID = [128, 256, 384, 512, 128, 256, 384, 512]
        TOP_K = 2

        def _gelu(v):
            return jax.nn.gelu(v, approximate=False)

        def _forward(x, down_w, down_b, up_w, up_b, router_w, router_b, shared_w1, shared_b1, shared_w2, shared_b2, core_w, core_b, expert_params):
            E = len(expert_params)
            h = x @ down_w + down_b
            cost = jnp.array([w1.shape[0] * w1.shape[1] + w2.shape[0] * w2.shape[1] for w1, _, w2, _ in expert_params], jnp.float32)
            logits = x @ router_w + router_b - COST_LAMBDA * cost
            probs = jax.nn.softmax(logits, axis=-1)
            topv, topi = jax.lax.top_k(probs, TOP_K)
            gate = jax.nn.softmax(topv, axis=-1)
            out = jnp.zeros_like(h)
            for k in range(TOP_K):
                mask = jax.nn.one_hot(topi[..., k], E, dtype=h.dtype)
                acc = jnp.zeros_like(h)
                for e, (w1, b1, w2, b2) in enumerate(expert_params):
                    hm = h * mask[..., e:e + 1]
                    acc = acc + (_gelu(_gelu(hm) @ w1 + b1) @ w2 + b2)
                out = out + acc * gate[..., k:k + 1]
            out = out + 0.1 * (_gelu(_gelu(h) @ shared_w1 + shared_b1) @ shared_w2 + shared_b2)
            out = out @ up_w + up_b
            out = out + (_gelu(x) @ core_w + core_b)
            return out
        key = jax.random.key(seed)
        ks = iter(jax.random.split(key, 80))

        def W(shape):
            return jax.random.normal(next(ks), shape, jnp.float32) * 0.02
        B, T, D, L = (4, 256, 256, 128)
        inp = {'x': jax.random.normal(next(ks), (B, T, D), jnp.float32)}
        inp['down_w'] = W((D, L))
        inp['down_b'] = jnp.zeros((L,), jnp.float32)
        inp['up_w'] = W((L, D))
        inp['up_b'] = jnp.zeros((D,), jnp.float32)
        inp['router_w'] = W((D, len(HID)))
        inp['router_b'] = jnp.zeros((len(HID),), jnp.float32)
        inp['shared_w1'] = W((L, L))
        inp['shared_b1'] = jnp.zeros((L,), jnp.float32)
        inp['shared_w2'] = W((L, L))
        inp['shared_b2'] = jnp.zeros((L,), jnp.float32)
        inp['core_w'] = W((D, D))
        inp['core_b'] = jnp.zeros((D,), jnp.float32)
        for e, h in enumerate(HID):
            inp[f'e{e}_w1'] = W((L, h))
            inp[f'e{e}_b1'] = jnp.zeros((h,), jnp.float32)
            inp[f'e{e}_w2'] = W((h, L))
            inp[f'e{e}_b2'] = jnp.zeros((L,), jnp.float32)
        return inp
    _L0_ffn_in = _L0_ffn_setup()
    _L0_c = _w((lambda *s: np.random.randn(*s).astype(np.float32) * 0.05)(4, 256))
    _L0_wmod = _w((lambda *s: np.random.randn(*s).astype(np.float32) * 0.05)(256, 6 * 256) * 256 ** (-0.5))

    def _L1_attn_setup():
        import math
        import jax, jax.numpy as jnp
        import numpy as np
        B, L, HID = (2, 256, 256)
        H = 16
        D = HID // H
        EPS = 1e-06
        ROPE_BASE = 10000.0
        BETA_MIN, BETA_MAX = (0.8, 0.9995)

        def _rope_cache(seq_len, dim):
            half = dim // 2
            inv_freq = 1.0 / ROPE_BASE ** (jnp.arange(half, dtype=jnp.float32) / float(half))
            t = jnp.arange(seq_len, dtype=jnp.float32)
            freqs = t[:, None] * inv_freq[None, :]
            return (jnp.cos(freqs), jnp.sin(freqs))

        def _apply_rope(x, cos, sin):
            half = x.shape[-1] // 2
            xe, xo = (x[..., :half], x[..., half:])
            c = cos[None, None]
            s = sin[None, None]
            return jnp.concatenate([xe * c - xo * s, xe * s + xo * c], axis=-1)

        def _deltanet(x, Wq, Wk, Wv, Wg, bg, Wo, bo):
            Bb, Ll, _ = x.shape
            split = lambda t: t.reshape(Bb, Ll, H, D).transpose(0, 2, 1, 3)
            q = split(x @ Wq)
            k = split(x @ Wk)
            v = split(x @ Wv)
            cos, sin = _rope_cache(Ll, D)
            q = _apply_rope(q, cos, sin)
            k = _apply_rope(k, cos, sin)
            beta = jax.nn.sigmoid(x @ Wg + bg)
            beta = jnp.clip(beta, BETA_MIN, BETA_MAX).transpose(0, 2, 1)
            phi_q = jax.nn.elu(q) + 1.0
            phi_k = jax.nn.elu(k) + 1.0
            pq = phi_q.transpose(2, 0, 1, 3)
            pk = phi_k.transpose(2, 0, 1, 3)
            vt = v.transpose(2, 0, 1, 3)
            bt = beta.transpose(2, 0, 1)
            S0 = jnp.zeros((Bb, H, D, D), jnp.float32)
            z0 = jnp.zeros((Bb, H, D), jnp.float32)

            def step(carry, inp):
                S, z = carry
                pq_t, pk_t, v_t, b_t = inp
                S = S * b_t[..., None, None] + pk_t[..., :, None] * v_t[..., None, :]
                z = z * b_t[..., None] + pk_t
                numer = jnp.einsum('bhd,bhde->bhe', pq_t, S)
                denom = jnp.sum(pq_t * z, axis=-1, keepdims=True) + EPS
                return ((S, z), numer / denom)
            (_, _), y = jax.lax.scan(step, (S0, z0), (pq, pk, vt, bt))
            y = y.transpose(1, 0, 2, 3).reshape(Bb, Ll, HID)
            return y @ Wo + bo
        key = jax.random.key(seed)
        ks = jax.random.split(key, 6)
        sc = 1.0 / math.sqrt(HID)
        return {'x': jax.random.normal(ks[0], (B, L, HID), jnp.float32), 'Wq': jax.random.normal(ks[1], (HID, HID), jnp.float32) * sc, 'Wk': jax.random.normal(ks[2], (HID, HID), jnp.float32) * sc, 'Wv': jax.random.normal(ks[3], (HID, HID), jnp.float32) * sc, 'Wg': jax.random.normal(ks[4], (HID, H), jnp.float32) * sc, 'bg': jnp.full((H,), math.log(0.98 / (1.0 - 0.98)), jnp.float32), 'Wo': jax.random.normal(ks[5], (HID, HID), jnp.float32) * sc, 'bo': jnp.zeros((HID,), jnp.float32)}
    _L1_attn_in = _L1_attn_setup()

    def _L1_ffn_setup():
        import jax, jax.numpy as jnp
        import numpy as np
        COST_LAMBDA = 1e-07
        HID = [128, 256, 384, 512, 128, 256, 384, 512]
        TOP_K = 2

        def _gelu(v):
            return jax.nn.gelu(v, approximate=False)

        def _forward(x, down_w, down_b, up_w, up_b, router_w, router_b, shared_w1, shared_b1, shared_w2, shared_b2, core_w, core_b, expert_params):
            E = len(expert_params)
            h = x @ down_w + down_b
            cost = jnp.array([w1.shape[0] * w1.shape[1] + w2.shape[0] * w2.shape[1] for w1, _, w2, _ in expert_params], jnp.float32)
            logits = x @ router_w + router_b - COST_LAMBDA * cost
            probs = jax.nn.softmax(logits, axis=-1)
            topv, topi = jax.lax.top_k(probs, TOP_K)
            gate = jax.nn.softmax(topv, axis=-1)
            out = jnp.zeros_like(h)
            for k in range(TOP_K):
                mask = jax.nn.one_hot(topi[..., k], E, dtype=h.dtype)
                acc = jnp.zeros_like(h)
                for e, (w1, b1, w2, b2) in enumerate(expert_params):
                    hm = h * mask[..., e:e + 1]
                    acc = acc + (_gelu(_gelu(hm) @ w1 + b1) @ w2 + b2)
                out = out + acc * gate[..., k:k + 1]
            out = out + 0.1 * (_gelu(_gelu(h) @ shared_w1 + shared_b1) @ shared_w2 + shared_b2)
            out = out @ up_w + up_b
            out = out + (_gelu(x) @ core_w + core_b)
            return out
        key = jax.random.key(seed)
        ks = iter(jax.random.split(key, 80))

        def W(shape):
            return jax.random.normal(next(ks), shape, jnp.float32) * 0.02
        B, T, D, L = (4, 256, 256, 128)
        inp = {'x': jax.random.normal(next(ks), (B, T, D), jnp.float32)}
        inp['down_w'] = W((D, L))
        inp['down_b'] = jnp.zeros((L,), jnp.float32)
        inp['up_w'] = W((L, D))
        inp['up_b'] = jnp.zeros((D,), jnp.float32)
        inp['router_w'] = W((D, len(HID)))
        inp['router_b'] = jnp.zeros((len(HID),), jnp.float32)
        inp['shared_w1'] = W((L, L))
        inp['shared_b1'] = jnp.zeros((L,), jnp.float32)
        inp['shared_w2'] = W((L, L))
        inp['shared_b2'] = jnp.zeros((L,), jnp.float32)
        inp['core_w'] = W((D, D))
        inp['core_b'] = jnp.zeros((D,), jnp.float32)
        for e, h in enumerate(HID):
            inp[f'e{e}_w1'] = W((L, h))
            inp[f'e{e}_b1'] = jnp.zeros((h,), jnp.float32)
            inp[f'e{e}_w2'] = W((h, L))
            inp[f'e{e}_b2'] = jnp.zeros((L,), jnp.float32)
        return inp
    _L1_ffn_in = _L1_ffn_setup()
    _L1_c = _w((lambda *s: np.random.randn(*s).astype(np.float32) * 0.05)(4, 256))
    _L1_wmod = _w((lambda *s: np.random.randn(*s).astype(np.float32) * 0.05)(256, 6 * 256) * 256 ** (-0.5))
    _d = {'L0_attn_x': _L0_attn_in['x'], 'L0_attn_w_in': _L0_attn_in['w_in'], 'L0_attn_conv_w': _L0_attn_in['conv_w'], 'L0_attn_conv_b': _L0_attn_in['conv_b'], 'L0_attn_dt_bias': _L0_attn_in['dt_bias'], 'L0_attn_A_log': _L0_attn_in['A_log'], 'L0_attn_D': _L0_attn_in['D'], 'L0_attn_norm_w': _L0_attn_in['norm_w'], 'L0_attn_w_out': _L0_attn_in['w_out'], 'L0_ffn_down_w': _L0_ffn_in['down_w'], 'L0_ffn_down_b': _L0_ffn_in['down_b'], 'L0_ffn_up_w': _L0_ffn_in['up_w'], 'L0_ffn_up_b': _L0_ffn_in['up_b'], 'L0_ffn_router_w': _L0_ffn_in['router_w'], 'L0_ffn_router_b': _L0_ffn_in['router_b'], 'L0_ffn_shared_w1': _L0_ffn_in['shared_w1'], 'L0_ffn_shared_b1': _L0_ffn_in['shared_b1'], 'L0_ffn_shared_w2': _L0_ffn_in['shared_w2'], 'L0_ffn_shared_b2': _L0_ffn_in['shared_b2'], 'L0_ffn_core_w': _L0_ffn_in['core_w'], 'L0_ffn_core_b': _L0_ffn_in['core_b'], 'L0_ffn_e0_w1': _L0_ffn_in['e0_w1'], 'L0_ffn_e0_b1': _L0_ffn_in['e0_b1'], 'L0_ffn_e0_w2': _L0_ffn_in['e0_w2'], 'L0_ffn_e0_b2': _L0_ffn_in['e0_b2'], 'L0_ffn_e1_w1': _L0_ffn_in['e1_w1'], 'L0_ffn_e1_b1': _L0_ffn_in['e1_b1'], 'L0_ffn_e1_w2': _L0_ffn_in['e1_w2'], 'L0_ffn_e1_b2': _L0_ffn_in['e1_b2'], 'L0_ffn_e2_w1': _L0_ffn_in['e2_w1'], 'L0_ffn_e2_b1': _L0_ffn_in['e2_b1'], 'L0_ffn_e2_w2': _L0_ffn_in['e2_w2'], 'L0_ffn_e2_b2': _L0_ffn_in['e2_b2'], 'L0_ffn_e3_w1': _L0_ffn_in['e3_w1'], 'L0_ffn_e3_b1': _L0_ffn_in['e3_b1'], 'L0_ffn_e3_w2': _L0_ffn_in['e3_w2'], 'L0_ffn_e3_b2': _L0_ffn_in['e3_b2'], 'L0_ffn_e4_w1': _L0_ffn_in['e4_w1'], 'L0_ffn_e4_b1': _L0_ffn_in['e4_b1'], 'L0_ffn_e4_w2': _L0_ffn_in['e4_w2'], 'L0_ffn_e4_b2': _L0_ffn_in['e4_b2'], 'L0_ffn_e5_w1': _L0_ffn_in['e5_w1'], 'L0_ffn_e5_b1': _L0_ffn_in['e5_b1'], 'L0_ffn_e5_w2': _L0_ffn_in['e5_w2'], 'L0_ffn_e5_b2': _L0_ffn_in['e5_b2'], 'L0_ffn_e6_w1': _L0_ffn_in['e6_w1'], 'L0_ffn_e6_b1': _L0_ffn_in['e6_b1'], 'L0_ffn_e6_w2': _L0_ffn_in['e6_w2'], 'L0_ffn_e6_b2': _L0_ffn_in['e6_b2'], 'L0_ffn_e7_w1': _L0_ffn_in['e7_w1'], 'L0_ffn_e7_b1': _L0_ffn_in['e7_b1'], 'L0_ffn_e7_w2': _L0_ffn_in['e7_w2'], 'L0_ffn_e7_b2': _L0_ffn_in['e7_b2'], 'L0_c': _L0_c, 'L0_wmod': _L0_wmod, 'L1_attn_Wq': _L1_attn_in['Wq'], 'L1_attn_Wk': _L1_attn_in['Wk'], 'L1_attn_Wv': _L1_attn_in['Wv'], 'L1_attn_Wg': _L1_attn_in['Wg'], 'L1_attn_bg': _L1_attn_in['bg'], 'L1_attn_Wo': _L1_attn_in['Wo'], 'L1_attn_bo': _L1_attn_in['bo'], 'L1_ffn_down_w': _L1_ffn_in['down_w'], 'L1_ffn_down_b': _L1_ffn_in['down_b'], 'L1_ffn_up_w': _L1_ffn_in['up_w'], 'L1_ffn_up_b': _L1_ffn_in['up_b'], 'L1_ffn_router_w': _L1_ffn_in['router_w'], 'L1_ffn_router_b': _L1_ffn_in['router_b'], 'L1_ffn_shared_w1': _L1_ffn_in['shared_w1'], 'L1_ffn_shared_b1': _L1_ffn_in['shared_b1'], 'L1_ffn_shared_w2': _L1_ffn_in['shared_w2'], 'L1_ffn_shared_b2': _L1_ffn_in['shared_b2'], 'L1_ffn_core_w': _L1_ffn_in['core_w'], 'L1_ffn_core_b': _L1_ffn_in['core_b'], 'L1_ffn_e0_w1': _L1_ffn_in['e0_w1'], 'L1_ffn_e0_b1': _L1_ffn_in['e0_b1'], 'L1_ffn_e0_w2': _L1_ffn_in['e0_w2'], 'L1_ffn_e0_b2': _L1_ffn_in['e0_b2'], 'L1_ffn_e1_w1': _L1_ffn_in['e1_w1'], 'L1_ffn_e1_b1': _L1_ffn_in['e1_b1'], 'L1_ffn_e1_w2': _L1_ffn_in['e1_w2'], 'L1_ffn_e1_b2': _L1_ffn_in['e1_b2'], 'L1_ffn_e2_w1': _L1_ffn_in['e2_w1'], 'L1_ffn_e2_b1': _L1_ffn_in['e2_b1'], 'L1_ffn_e2_w2': _L1_ffn_in['e2_w2'], 'L1_ffn_e2_b2': _L1_ffn_in['e2_b2'], 'L1_ffn_e3_w1': _L1_ffn_in['e3_w1'], 'L1_ffn_e3_b1': _L1_ffn_in['e3_b1'], 'L1_ffn_e3_w2': _L1_ffn_in['e3_w2'], 'L1_ffn_e3_b2': _L1_ffn_in['e3_b2'], 'L1_ffn_e4_w1': _L1_ffn_in['e4_w1'], 'L1_ffn_e4_b1': _L1_ffn_in['e4_b1'], 'L1_ffn_e4_w2': _L1_ffn_in['e4_w2'], 'L1_ffn_e4_b2': _L1_ffn_in['e4_b2'], 'L1_ffn_e5_w1': _L1_ffn_in['e5_w1'], 'L1_ffn_e5_b1': _L1_ffn_in['e5_b1'], 'L1_ffn_e5_w2': _L1_ffn_in['e5_w2'], 'L1_ffn_e5_b2': _L1_ffn_in['e5_b2'], 'L1_ffn_e6_w1': _L1_ffn_in['e6_w1'], 'L1_ffn_e6_b1': _L1_ffn_in['e6_b1'], 'L1_ffn_e6_w2': _L1_ffn_in['e6_w2'], 'L1_ffn_e6_b2': _L1_ffn_in['e6_b2'], 'L1_ffn_e7_w1': _L1_ffn_in['e7_w1'], 'L1_ffn_e7_b1': _L1_ffn_in['e7_b1'], 'L1_ffn_e7_w2': _L1_ffn_in['e7_w2'], 'L1_ffn_e7_b2': _L1_ffn_in['e7_b2'], 'L1_c': _L1_c, 'L1_wmod': _L1_wmod}
    _x0 = _d['L0_attn_x']
    _d['L0_attn_x'] = jax.random.normal(jax.random.fold_in(jax.random.key(seed), 1), (4, 1024, 256), dtype=_x0.dtype)
    del _x0
    return _d

def reference(L0_attn_x, L0_attn_w_in, L0_attn_conv_w, L0_attn_conv_b, L0_attn_dt_bias, L0_attn_A_log, L0_attn_D, L0_attn_norm_w, L0_attn_w_out, L0_ffn_down_w, L0_ffn_down_b, L0_ffn_up_w, L0_ffn_up_b, L0_ffn_router_w, L0_ffn_router_b, L0_ffn_shared_w1, L0_ffn_shared_b1, L0_ffn_shared_w2, L0_ffn_shared_b2, L0_ffn_core_w, L0_ffn_core_b, L0_ffn_e0_w1, L0_ffn_e0_b1, L0_ffn_e0_w2, L0_ffn_e0_b2, L0_ffn_e1_w1, L0_ffn_e1_b1, L0_ffn_e1_w2, L0_ffn_e1_b2, L0_ffn_e2_w1, L0_ffn_e2_b1, L0_ffn_e2_w2, L0_ffn_e2_b2, L0_ffn_e3_w1, L0_ffn_e3_b1, L0_ffn_e3_w2, L0_ffn_e3_b2, L0_ffn_e4_w1, L0_ffn_e4_b1, L0_ffn_e4_w2, L0_ffn_e4_b2, L0_ffn_e5_w1, L0_ffn_e5_b1, L0_ffn_e5_w2, L0_ffn_e5_b2, L0_ffn_e6_w1, L0_ffn_e6_b1, L0_ffn_e6_w2, L0_ffn_e6_b2, L0_ffn_e7_w1, L0_ffn_e7_b1, L0_ffn_e7_w2, L0_ffn_e7_b2, L0_c, L0_wmod, L1_attn_Wq, L1_attn_Wk, L1_attn_Wv, L1_attn_Wg, L1_attn_bg, L1_attn_Wo, L1_attn_bo, L1_ffn_down_w, L1_ffn_down_b, L1_ffn_up_w, L1_ffn_up_b, L1_ffn_router_w, L1_ffn_router_b, L1_ffn_shared_w1, L1_ffn_shared_b1, L1_ffn_shared_w2, L1_ffn_shared_b2, L1_ffn_core_w, L1_ffn_core_b, L1_ffn_e0_w1, L1_ffn_e0_b1, L1_ffn_e0_w2, L1_ffn_e0_b2, L1_ffn_e1_w1, L1_ffn_e1_b1, L1_ffn_e1_w2, L1_ffn_e1_b2, L1_ffn_e2_w1, L1_ffn_e2_b1, L1_ffn_e2_w2, L1_ffn_e2_b2, L1_ffn_e3_w1, L1_ffn_e3_b1, L1_ffn_e3_w2, L1_ffn_e3_b2, L1_ffn_e4_w1, L1_ffn_e4_b1, L1_ffn_e4_w2, L1_ffn_e4_b2, L1_ffn_e5_w1, L1_ffn_e5_b1, L1_ffn_e5_w2, L1_ffn_e5_b2, L1_ffn_e6_w1, L1_ffn_e6_b1, L1_ffn_e6_w2, L1_ffn_e6_b2, L1_ffn_e7_w1, L1_ffn_e7_b1, L1_ffn_e7_w2, L1_ffn_e7_b2, L1_c, L1_wmod):

    def _L0_attn_ref(x, w_in, conv_w, conv_b, dt_bias, A_log, D, norm_w, w_out):
        import jax, jax.numpy as jnp
        import numpy as np
        D_MODEL = 256
        D_STATE = 128
        HEADDIM = 64
        EXPAND = 2
        D_CONV = 4
        NGROUPS = 1
        CHUNK = 32
        EPS = 1e-05
        D_INNER = EXPAND * D_MODEL
        NHEADS = D_INNER // HEADDIM
        CONV_DIM = D_INNER + 2 * NGROUPS * D_STATE
        D_IN_PROJ = 2 * D_INNER + 2 * NGROUPS * D_STATE + NHEADS

        def _segsum(a):
            T = a.shape[-1]
            cs = jnp.cumsum(a, axis=-1)
            d = cs[..., :, None] - cs[..., None, :]
            mask = jnp.tril(jnp.ones((T, T), dtype=bool))
            return jnp.where(mask, d, -jnp.inf)

        def _ssd(X, A, Bm, Cm):
            b, l, h, p = X.shape
            n = Bm.shape[-1]
            c = l // CHUNK
            X = X.reshape(b, c, CHUNK, h, p)
            A = A.reshape(b, c, CHUNK, h).transpose(0, 3, 1, 2)
            Bm = Bm.reshape(b, c, CHUNK, n)
            Cm = Cm.reshape(b, c, CHUNK, n)
            A_cs = jnp.cumsum(A, axis=-1)
            Lmat = jnp.exp(_segsum(A))
            Y_diag = jnp.einsum('bcln,bcsn,bhcls,bcshp->bclhp', Cm, Bm, Lmat, X)
            decay_states = jnp.exp(A_cs[..., -1:] - A_cs)
            states = jnp.einsum('bcln,bhcl,bclhp->bchpn', Bm, decay_states, X)
            A_last = jnp.pad(A_cs[..., -1], ((0, 0), (0, 0), (1, 0)))
            decay_chunk = jnp.exp(_segsum(A_last))
            states = jnp.concatenate([jnp.zeros_like(states[:, :1]), states], axis=1)
            states = jnp.einsum('bhzc,bchpn->bzhpn', decay_chunk, states)[:, :-1]
            Y_off = jnp.einsum('bchpn,bcln,bhcl->bclhp', states, Cm, jnp.exp(A_cs))
            return (Y_diag + Y_off).reshape(b, l, h, p)

        def _mamba2(x, w_in, conv_w, conv_b, dt_bias, A_log, D, norm_w, w_out):
            B, L, _ = x.shape
            zxbcdt = jnp.einsum('bld,de->ble', x, w_in)
            z = zxbcdt[..., :D_INNER]
            xBC = zxbcdt[..., D_INNER:D_INNER + CONV_DIM]
            dt = zxbcdt[..., D_INNER + CONV_DIM:]
            dt = jax.nn.softplus(dt + dt_bias)
            xp = jnp.pad(xBC, ((0, 0), (D_CONV - 1, 0), (0, 0)))
            acc = conv_b
            xBC = sum((conv_w[:, k] * xp[:, k:k + L, :] for k in range(D_CONV))) + conv_b
            xBC = jax.nn.silu(xBC)
            xh = xBC[..., :D_INNER].reshape(B, L, NHEADS, HEADDIM)
            Bm = xBC[..., D_INNER:D_INNER + NGROUPS * D_STATE]
            Cm = xBC[..., D_INNER + NGROUPS * D_STATE:]
            A = -jnp.exp(A_log)
            y = _ssd(xh * dt[..., None], dt * A, Bm, Cm)
            y = y + xh * D[None, None, :, None]
            y = y.reshape(B, L, D_INNER)
            y = y * jax.nn.silu(z)
            y = y * jax.lax.rsqrt(jnp.mean(y * y, axis=-1, keepdims=True) + EPS) * norm_w
            return jnp.einsum('ble,ed->bld', y, w_out)
        return x + _mamba2(x, w_in, conv_w, conv_b, dt_bias, A_log, D, norm_w, w_out)

    def _L0_ffn_ref(x, down_w, down_b, up_w, up_b, router_w, router_b, shared_w1, shared_b1, shared_w2, shared_b2, core_w, core_b, e0_w1, e0_b1, e0_w2, e0_b2, e1_w1, e1_b1, e1_w2, e1_b2, e2_w1, e2_b1, e2_w2, e2_b2, e3_w1, e3_b1, e3_w2, e3_b2, e4_w1, e4_b1, e4_w2, e4_b2, e5_w1, e5_b1, e5_w2, e5_b2, e6_w1, e6_b1, e6_w2, e6_b2, e7_w1, e7_b1, e7_w2, e7_b2):
        import jax, jax.numpy as jnp
        import numpy as np
        COST_LAMBDA = 1e-07
        HID = [128, 256, 384, 512, 128, 256, 384, 512]
        TOP_K = 2

        def _gelu(v):
            return jax.nn.gelu(v, approximate=False)

        def _forward(x, down_w, down_b, up_w, up_b, router_w, router_b, shared_w1, shared_b1, shared_w2, shared_b2, core_w, core_b, expert_params):
            E = len(expert_params)
            h = x @ down_w + down_b
            cost = jnp.array([w1.shape[0] * w1.shape[1] + w2.shape[0] * w2.shape[1] for w1, _, w2, _ in expert_params], jnp.float32)
            logits = x @ router_w + router_b - COST_LAMBDA * cost
            probs = jax.nn.softmax(logits, axis=-1)
            topv, topi = jax.lax.top_k(probs, TOP_K)
            gate = jax.nn.softmax(topv, axis=-1)
            out = jnp.zeros_like(h)
            for k in range(TOP_K):
                mask = jax.nn.one_hot(topi[..., k], E, dtype=h.dtype)
                acc = jnp.zeros_like(h)
                for e, (w1, b1, w2, b2) in enumerate(expert_params):
                    hm = h * mask[..., e:e + 1]
                    acc = acc + (_gelu(_gelu(hm) @ w1 + b1) @ w2 + b2)
                out = out + acc * gate[..., k:k + 1]
            out = out + 0.1 * (_gelu(_gelu(h) @ shared_w1 + shared_b1) @ shared_w2 + shared_b2)
            out = out @ up_w + up_b
            out = out + (_gelu(x) @ core_w + core_b)
            return out
        ep = [(e0_w1, e0_b1, e0_w2, e0_b2), (e1_w1, e1_b1, e1_w2, e1_b2), (e2_w1, e2_b1, e2_w2, e2_b2), (e3_w1, e3_b1, e3_w2, e3_b2), (e4_w1, e4_b1, e4_w2, e4_b2), (e5_w1, e5_b1, e5_w2, e5_b2), (e6_w1, e6_b1, e6_w2, e6_b2), (e7_w1, e7_b1, e7_w2, e7_b2)]
        return _forward(x, down_w, down_b, up_w, up_b, router_w, router_b, shared_w1, shared_b1, shared_w2, shared_b2, core_w, core_b, ep)

    def _L1_attn_ref(x, Wq, Wk, Wv, Wg, bg, Wo, bo):
        import math
        import jax, jax.numpy as jnp
        import numpy as np
        B, L, HID = (2, 256, 256)
        H = 16
        D = HID // H
        EPS = 1e-06
        ROPE_BASE = 10000.0
        BETA_MIN, BETA_MAX = (0.8, 0.9995)

        def _rope_cache(seq_len, dim):
            half = dim // 2
            inv_freq = 1.0 / ROPE_BASE ** (jnp.arange(half, dtype=jnp.float32) / float(half))
            t = jnp.arange(seq_len, dtype=jnp.float32)
            freqs = t[:, None] * inv_freq[None, :]
            return (jnp.cos(freqs), jnp.sin(freqs))

        def _apply_rope(x, cos, sin):
            half = x.shape[-1] // 2
            xe, xo = (x[..., :half], x[..., half:])
            c = cos[None, None]
            s = sin[None, None]
            return jnp.concatenate([xe * c - xo * s, xe * s + xo * c], axis=-1)

        def _deltanet(x, Wq, Wk, Wv, Wg, bg, Wo, bo):
            Bb, Ll, _ = x.shape
            split = lambda t: t.reshape(Bb, Ll, H, D).transpose(0, 2, 1, 3)
            q = split(x @ Wq)
            k = split(x @ Wk)
            v = split(x @ Wv)
            cos, sin = _rope_cache(Ll, D)
            q = _apply_rope(q, cos, sin)
            k = _apply_rope(k, cos, sin)
            beta = jax.nn.sigmoid(x @ Wg + bg)
            beta = jnp.clip(beta, BETA_MIN, BETA_MAX).transpose(0, 2, 1)
            phi_q = jax.nn.elu(q) + 1.0
            phi_k = jax.nn.elu(k) + 1.0
            pq = phi_q.transpose(2, 0, 1, 3)
            pk = phi_k.transpose(2, 0, 1, 3)
            vt = v.transpose(2, 0, 1, 3)
            bt = beta.transpose(2, 0, 1)
            S0 = jnp.zeros((Bb, H, D, D), jnp.float32)
            z0 = jnp.zeros((Bb, H, D), jnp.float32)

            def step(carry, inp):
                S, z = carry
                pq_t, pk_t, v_t, b_t = inp
                S = S * b_t[..., None, None] + pk_t[..., :, None] * v_t[..., None, :]
                z = z * b_t[..., None] + pk_t
                numer = jnp.einsum('bhd,bhde->bhe', pq_t, S)
                denom = jnp.sum(pq_t * z, axis=-1, keepdims=True) + EPS
                return ((S, z), numer / denom)
            (_, _), y = jax.lax.scan(step, (S0, z0), (pq, pk, vt, bt))
            y = y.transpose(1, 0, 2, 3).reshape(Bb, Ll, HID)
            return y @ Wo + bo
        return _deltanet(x, Wq, Wk, Wv, Wg, bg, Wo, bo)

    def _L1_ffn_ref(x, down_w, down_b, up_w, up_b, router_w, router_b, shared_w1, shared_b1, shared_w2, shared_b2, core_w, core_b, e0_w1, e0_b1, e0_w2, e0_b2, e1_w1, e1_b1, e1_w2, e1_b2, e2_w1, e2_b1, e2_w2, e2_b2, e3_w1, e3_b1, e3_w2, e3_b2, e4_w1, e4_b1, e4_w2, e4_b2, e5_w1, e5_b1, e5_w2, e5_b2, e6_w1, e6_b1, e6_w2, e6_b2, e7_w1, e7_b1, e7_w2, e7_b2):
        import jax, jax.numpy as jnp
        import numpy as np
        COST_LAMBDA = 1e-07
        HID = [128, 256, 384, 512, 128, 256, 384, 512]
        TOP_K = 2

        def _gelu(v):
            return jax.nn.gelu(v, approximate=False)

        def _forward(x, down_w, down_b, up_w, up_b, router_w, router_b, shared_w1, shared_b1, shared_w2, shared_b2, core_w, core_b, expert_params):
            E = len(expert_params)
            h = x @ down_w + down_b
            cost = jnp.array([w1.shape[0] * w1.shape[1] + w2.shape[0] * w2.shape[1] for w1, _, w2, _ in expert_params], jnp.float32)
            logits = x @ router_w + router_b - COST_LAMBDA * cost
            probs = jax.nn.softmax(logits, axis=-1)
            topv, topi = jax.lax.top_k(probs, TOP_K)
            gate = jax.nn.softmax(topv, axis=-1)
            out = jnp.zeros_like(h)
            for k in range(TOP_K):
                mask = jax.nn.one_hot(topi[..., k], E, dtype=h.dtype)
                acc = jnp.zeros_like(h)
                for e, (w1, b1, w2, b2) in enumerate(expert_params):
                    hm = h * mask[..., e:e + 1]
                    acc = acc + (_gelu(_gelu(hm) @ w1 + b1) @ w2 + b2)
                out = out + acc * gate[..., k:k + 1]
            out = out + 0.1 * (_gelu(_gelu(h) @ shared_w1 + shared_b1) @ shared_w2 + shared_b2)
            out = out @ up_w + up_b
            out = out + (_gelu(x) @ core_w + core_b)
            return out
        ep = [(e0_w1, e0_b1, e0_w2, e0_b2), (e1_w1, e1_b1, e1_w2, e1_b2), (e2_w1, e2_b1, e2_w2, e2_b2), (e3_w1, e3_b1, e3_w2, e3_b2), (e4_w1, e4_b1, e4_w2, e4_b2), (e5_w1, e5_b1, e5_w2, e5_b2), (e6_w1, e6_b1, e6_w2, e6_b2), (e7_w1, e7_b1, e7_w2, e7_b2)]
        return _forward(x, down_w, down_b, up_w, up_b, router_w, router_b, shared_w1, shared_b1, shared_w2, shared_b2, core_w, core_b, ep)
    x = L0_attn_x
    mod = (_silu(L0_c) @ L0_wmod).reshape(L0_c.shape[0], 6, 1, -1)
    sa, ca, ga, sb, cb, gb = (mod[:, 0], mod[:, 1], mod[:, 2], mod[:, 3], mod[:, 4], mod[:, 5])
    ga = (2 * (ga >= 0) - 1) * jnp.maximum(jnp.abs(ga), 0.25)
    gb = (2 * (gb >= 0) - 1) * jnp.maximum(jnp.abs(gb), 0.25)
    h = _layernorm(x, axis=-1) * (1 + ca) + sa
    x = x + ga * _L0_attn_ref(h, L0_attn_w_in, L0_attn_conv_w, L0_attn_conv_b, L0_attn_dt_bias, L0_attn_A_log, L0_attn_D, L0_attn_norm_w, L0_attn_w_out)
    h = _layernorm(x, axis=-1) * (1 + cb) + sb
    x = x + gb * _L0_ffn_ref(h, L0_ffn_down_w, L0_ffn_down_b, L0_ffn_up_w, L0_ffn_up_b, L0_ffn_router_w, L0_ffn_router_b, L0_ffn_shared_w1, L0_ffn_shared_b1, L0_ffn_shared_w2, L0_ffn_shared_b2, L0_ffn_core_w, L0_ffn_core_b, L0_ffn_e0_w1, L0_ffn_e0_b1, L0_ffn_e0_w2, L0_ffn_e0_b2, L0_ffn_e1_w1, L0_ffn_e1_b1, L0_ffn_e1_w2, L0_ffn_e1_b2, L0_ffn_e2_w1, L0_ffn_e2_b1, L0_ffn_e2_w2, L0_ffn_e2_b2, L0_ffn_e3_w1, L0_ffn_e3_b1, L0_ffn_e3_w2, L0_ffn_e3_b2, L0_ffn_e4_w1, L0_ffn_e4_b1, L0_ffn_e4_w2, L0_ffn_e4_b2, L0_ffn_e5_w1, L0_ffn_e5_b1, L0_ffn_e5_w2, L0_ffn_e5_b2, L0_ffn_e6_w1, L0_ffn_e6_b1, L0_ffn_e6_w2, L0_ffn_e6_b2, L0_ffn_e7_w1, L0_ffn_e7_b1, L0_ffn_e7_w2, L0_ffn_e7_b2)
    mod = (_silu(L1_c) @ L1_wmod).reshape(L1_c.shape[0], 6, 1, -1)
    sa, ca, ga, sb, cb, gb = (mod[:, 0], mod[:, 1], mod[:, 2], mod[:, 3], mod[:, 4], mod[:, 5])
    ga = (2 * (ga >= 0) - 1) * jnp.maximum(jnp.abs(ga), 0.25)
    gb = (2 * (gb >= 0) - 1) * jnp.maximum(jnp.abs(gb), 0.25)
    h = _layernorm(x, axis=-1) * (1 + ca) + sa
    x = x + ga * _L1_attn_ref(h, L1_attn_Wq, L1_attn_Wk, L1_attn_Wv, L1_attn_Wg, L1_attn_bg, L1_attn_Wo, L1_attn_bo)
    h = _layernorm(x, axis=-1) * (1 + cb) + sb
    x = x + gb * _L1_ffn_ref(h, L1_ffn_down_w, L1_ffn_down_b, L1_ffn_up_w, L1_ffn_up_b, L1_ffn_router_w, L1_ffn_router_b, L1_ffn_shared_w1, L1_ffn_shared_b1, L1_ffn_shared_w2, L1_ffn_shared_b2, L1_ffn_core_w, L1_ffn_core_b, L1_ffn_e0_w1, L1_ffn_e0_b1, L1_ffn_e0_w2, L1_ffn_e0_b2, L1_ffn_e1_w1, L1_ffn_e1_b1, L1_ffn_e1_w2, L1_ffn_e1_b2, L1_ffn_e2_w1, L1_ffn_e2_b1, L1_ffn_e2_w2, L1_ffn_e2_b2, L1_ffn_e3_w1, L1_ffn_e3_b1, L1_ffn_e3_w2, L1_ffn_e3_b2, L1_ffn_e4_w1, L1_ffn_e4_b1, L1_ffn_e4_w2, L1_ffn_e4_b2, L1_ffn_e5_w1, L1_ffn_e5_b1, L1_ffn_e5_w2, L1_ffn_e5_b2, L1_ffn_e6_w1, L1_ffn_e6_b1, L1_ffn_e6_w2, L1_ffn_e6_b2, L1_ffn_e7_w1, L1_ffn_e7_b1, L1_ffn_e7_w2, L1_ffn_e7_b2)
    return x

_drawn_inputs = setup_inputs


def setup_inputs(seed=0):
    import zlib

    import numpy as np

    out = dict(_drawn_inputs(seed))
    spreads = {'L0_attn_conv_b': (0.0, 0.1),
     'L0_attn_D': (1.0, 0.6),
     'L0_attn_norm_w': (1.0, 0.2),
     'L0_ffn_down_b': (0.0, 0.8),
     'L0_ffn_up_b': (0.0, 0.348),
     'L0_ffn_router_b': (0.0, 0.8),
     'L0_ffn_shared_b1': (0.0, 0.8),
     'L0_ffn_shared_b2': (0.0, 0.8),
     'L0_ffn_core_b': (0.0, 0.32),
     'L0_ffn_e0_b1': (0.0, 0.8),
     'L0_ffn_e0_b2': (0.0, 0.8),
     'L0_ffn_e1_b1': (0.0, 0.8),
     'L0_ffn_e1_b2': (0.0, 0.8),
     'L0_ffn_e2_b1': (0.0, 0.8),
     'L0_ffn_e2_b2': (0.0, 0.8),
     'L0_ffn_e3_b1': (0.0, 0.8),
     'L0_ffn_e3_b2': (0.0, 0.8),
     'L0_ffn_e4_b1': (0.0, 0.8),
     'L0_ffn_e4_b2': (0.0, 0.8),
     'L0_ffn_e5_b1': (0.0, 0.8),
     'L0_ffn_e5_b2': (0.0, 0.8),
     'L0_ffn_e6_b1': (0.0, 0.8),
     'L0_ffn_e6_b2': (0.0, 0.8),
     'L0_ffn_e7_b1': (0.0, 0.8),
     'L0_ffn_e7_b2': (0.0, 0.8),
     'L1_attn_bg': (3.891820192337036, 0.6),
     'L1_attn_bo': (0.0, 0.352),
     'L1_ffn_down_b': (0.0, 0.8),
     'L1_ffn_up_b': (0.0, 0.325),
     'L1_ffn_router_b': (0.0, 0.8),
     'L1_ffn_shared_b1': (0.0, 2.0),
     'L1_ffn_shared_b2': (0.0, 2.0),
     'L1_ffn_core_b': (0.0, 0.347),
     'L1_ffn_e0_b1': (0.0, 0.8),
     'L1_ffn_e0_b2': (0.0, 0.8),
     'L1_ffn_e1_b1': (0.0, 0.8),
     'L1_ffn_e1_b2': (0.0, 0.8),
     'L1_ffn_e2_b1': (0.0, 0.8),
     'L1_ffn_e2_b2': (0.0, 0.8),
     'L1_ffn_e3_b1': (0.0, 0.8),
     'L1_ffn_e3_b2': (0.0, 0.8),
     'L1_ffn_e4_b1': (0.0, 0.8),
     'L1_ffn_e4_b2': (0.0, 0.8),
     'L1_ffn_e5_b1': (0.0, 0.8),
     'L1_ffn_e5_b2': (0.0, 0.8),
     'L1_ffn_e6_b1': (0.0, 0.8),
     'L1_ffn_e6_b2': (0.0, 0.8),
     'L1_ffn_e7_b1': (0.0, 0.8),
     'L1_ffn_e7_b2': (0.0, 0.8)}
    factors = {'L0_attn_dt_bias': 2.726,
     'L0_attn_A_log': 22.707,
     'L0_ffn_down_w': 8.0,
     'L0_ffn_up_w': 3.57,
     'L0_ffn_router_w': 8.0,
     'L0_ffn_shared_w1': 8.0,
     'L0_ffn_shared_w2': 8.0,
     'L0_ffn_e0_w1': 8.0,
     'L0_ffn_e0_w2': 8.0,
     'L0_ffn_e1_w1': 8.0,
     'L0_ffn_e1_w2': 8.0,
     'L0_ffn_e2_w1': 8.0,
     'L0_ffn_e2_w2': 8.0,
     'L0_ffn_e3_w1': 8.0,
     'L0_ffn_e3_w2': 8.0,
     'L0_ffn_e4_w1': 8.0,
     'L0_ffn_e4_w2': 8.0,
     'L0_ffn_e5_w1': 8.0,
     'L0_ffn_e5_w2': 8.0,
     'L0_ffn_e6_w1': 8.0,
     'L0_ffn_e6_w2': 8.0,
     'L0_ffn_e7_w1': 8.0,
     'L0_ffn_e7_w2': 8.0,
     'L1_attn_Wq': 8.0,
     'L1_attn_Wk': 8.0,
     'L1_attn_Wg': 8.0,
     'L1_ffn_down_w': 8.0,
     'L1_ffn_up_w': 4.187,
     'L1_ffn_router_w': 8.0,
     'L1_ffn_shared_w1': 8.0,
     'L1_ffn_shared_w2': 8.0,
     'L1_ffn_e0_w1': 8.0,
     'L1_ffn_e0_w2': 8.0,
     'L1_ffn_e1_w1': 8.0,
     'L1_ffn_e1_w2': 8.0,
     'L1_ffn_e2_w1': 8.0,
     'L1_ffn_e2_w2': 8.0,
     'L1_ffn_e3_w1': 8.0,
     'L1_ffn_e3_w2': 8.0,
     'L1_ffn_e4_w1': 8.0,
     'L1_ffn_e4_w2': 8.0,
     'L1_ffn_e5_w1': 8.0,
     'L1_ffn_e5_w2': 8.0,
     'L1_ffn_e6_w1': 8.0,
     'L1_ffn_e6_w2': 8.0,
     'L1_ffn_e7_w1': 8.0,
     'L1_ffn_e7_w2': 8.0,
     'L1_ffn_core_w': 2.773}
    for name, (base, spread) in spreads.items():
        noise = np.random.default_rng([zlib.crc32(name.encode()), seed]).standard_normal(out[name].shape)
        drawn = base * np.exp(spread * noise) if base else spread * noise
        out[name] = jnp.asarray(drawn.astype(out[name].dtype))
    for name, factor in factors.items():
        out[name] = (out[name] * factor).astype(out[name].dtype)
    return out
```

```python
from contextlib import ExitStack

import numpy as np

import concourse.bass as bass
from concourse import mybir

F32 = mybir.dt.float32
U32 = mybir.dt.uint32
ALU = mybir.AluOpType
ACT = mybir.ActivationFunctionType
AX_X = mybir.AxisListType.X

P = 128
B = 4
T = 1024
D = 256
KD = D // P
NBLK = T // P
DI = 512
NS = 128
NH = 8
HD = DI // NH
CONV = 4
XM = (DI + 2 * NS) // P
DIN = 2 * DI + 2 * NS + NH
LH = 16
LD = D // LH
LG = P // LD
EXT = LD + 1
HID = [128, 256, 384, 512, 128, 256, 384, 512]
NE = len(HID)
L = 128
TILES = [h // P for h in HID]
FIRST = [sum(TILES[:e]) for e in range(NE)]
NT = sum(TILES)
GC = NE + 1
COST_LAMBDA = 1e-07
RING = 8

W_DOWN = 0
W_UP = W_DOWN + KD * L
W_CORE = W_UP + D
W_ROUT = W_CORE + KD * D
W_S1 = W_ROUT + KD * NE
W_S2 = W_S1 + L
W_E1 = W_S2 + L
W_E2 = W_E1 + NT * P
W_FFN = W_E2 + NT * L
C_DOWN, C_S1, C_B1 = 0, 1, 2
C_FFN = 2 + NT
C_CW, C_CB, C_NW = 0, XM * CONV, XM * CONV + XM
C_MAM = C_NW + DI // P
R_DT, R_AL, R_D, R_BG, R_RB, R_COST = 0, 8, 16, 24, 40, 56
R_ALL = 64
W_QK = 0
W_V = W_QK + KD * 2 * D
W_G = W_V + KD * D
W_O = W_G + KD * LH
W_LIN = W_O + KD * D


class Signal:

    def __init__(self, ctx, nc, name, per_block):
        self.sem, self.n = ctx.enter_context(nc.semaphore(name)), per_block

    def __call__(self, blk, k=0):
        return self.sem, blk * self.n + (k + 1)

    def last(self, blk):
        return self.sem, blk * self.n + self.n


def wait_before(eng, sig, blk, k):
    if isinstance(blk, int) and blk == 0:
        return
    eng.wait_ge(sig.sem, blk * sig.n + (k + 1 - sig.n))


class Chain:

    def __init__(self, ctx, nc, name, per_block):
        self.sem, self.n, self.k = ctx.enter_context(nc.semaphore(name)), per_block, 0

    def step(self, eng, blk, ins):
        self.k += 1
        ins.then_inc(self.sem, 1)
        eng.wait_ge(self.sem, blk * self.n + self.k)

    def close(self):
        assert self.k == self.n, (self.sem, self.k)
        self.k = 0


def program(nc, dram, out):
    ctx = ExitStack()
    with ctx:
        def sb(name, *shape, dt=F32):
            return ctx.enter_context(nc.sbuf_tensor(name, [shape[0], int(np.prod(shape[1:]))], dt))

        def v3(t, a):
            return t[:, :].rearrange("p (a b) -> p a b", a=a)

        def v4(t, a, b):
            return t[:, :].rearrange("p (a b c) -> p a b c", a=a, b=b)

        def signal(name, n):
            return Signal(ctx, nc, name, n)

        w_in = v3(sb("w_in", P, KD, DIN), KD)
        w_out = v3(sb("w_out", P, DI // P, D), DI // P)
        ffn_w = [sb(f"ffn_w{y}", P, W_FFN) for y in range(2)]
        lin_w = sb("lin_w", P, W_LIN)
        mam_c = sb("mam_c", P, C_MAM)
        ffn_c = [sb(f"ffn_c{y}", P, C_FFN) for y in range(2)]
        rows = sb("rows", P, R_ALL)
        a_neg = sb("a_neg", P, NH)
        router_bias = [sb(f"router_bias{y}", P, NE) for y in range(2)]
        ident = sb("ident", P, P)
        upto = sb("upto", P, P)
        after = sb("after", P, P)
        ones = sb("ones", P, P)
        block8 = sb("block8", P, LG)
        parity = sb("parity", P, 2)
        iota8 = sb("iota8", P, NE)
        eps_ln = sb("eps_ln", P, 1)
        spare = sb("spare", P, 1)
        mod_c = [v4(sb(f"mod_c{g}", P, 2, KD, B), 2, KD) for g in range(4)]
        gate_bc = [sb(f"gate_bc{g}", P, B * D) for g in range(4)]
        out_bias = v3(sb("out_bias", P, 3 * D), 3)
        cw = [sb(f"cw{y}", GC, L) for y in range(2)]

        x_of = [sb(f"x{g}", P, B * D) for g in range(4)]
        x_in_of = [x_of[0], x_of[0], x_of[1], x_of[2]]

        stats = [sb(f"stats{s}", P, B, 6) for s in range(2)]
        mv = [sb(f"mv{s}", P, B, 2) for s in range(2)]
        var_e = [sb(f"var_e{s}", P, B) for s in range(2)]
        rstd = [sb(f"rstd{s}", P, B) for s in range(2)]
        rtmp = [sb(f"rtmp{s}", P, B) for s in range(2)]
        area_v = sb("area_v", P, 2 * B * (P + CONV - 1))
        area_s = sb("area_s", P, NH * P)
        u_ring = sb("u_ring", P, RING * B * P)
        xn = [area_v[:, 0:B * D], u_ring[:, 0:B * D]]
        hT = [v3(sb(f"hT{s}", P, KD, B * P), KD) for s in range(2)]

        raw = v4(area_v, 2, B)
        tails = v4(sb("tails", P, XM, B, CONV - 1), XM, B)
        acc = v3(area_s, 2)
        xs_all = sb("xs", P, XM, B * P)
        xs = v3(xs_all, XM)
        tz = sb("tz", P, DI)
        sz = sb("sz", P, DI)
        dt_v = sb("dt_v", P, B * NH)
        dt_n = sb("dt_n", P, B * NH)
        dt_s = sb("dt_s", P, B * NH)
        dA = sb("dA", P, B * NH)
        dec = sb("dec", P, 3, B * NH)
        dtd = sb("dtd", P, B * NH)
        va = area_v[:, 0:NH * P]
        seg = area_s
        cbm = sb("cbm", P, P)
        xt = sb("xt", P, DI)
        bt = sb("bt", P, NS)
        xd = sb("xd", P, DI)
        th = sb("th", P, 2, DI)
        xdt, xdec = th[:, 0:DI], th[:, DI:2 * DI]
        yg = sb("yg", P, DI)
        yst = sb("yst", P, 4)
        yst2 = sb("yst2", P, 2)
        gT = sb("gT", P, DI)
        state = [sb(f"state{r}", P, DI) for r in range(B)]
        res_a = sb("res_a", P, D)

        rope = v3(sb("rope", P, 2, LD // 2), 2)
        lg = sb("lg", P, B * LH)
        la = sb("la", P, B * LH)
        le = v4(sb("le", P, 3, B, LH), 3, B)
        qk, qr1, qr2, qm = xs_all[:, 0:512], xs_all[:, 512:1024], xs_all[:, 1024:1536], xs_all[:, 1536:2048]
        qkT = v3_(xs_all[:, 2048:2560], 4)
        qpar = xs_all[:, 2560:3072].rearrange("p (a b c) -> p a b c", a=2, b=2)
        v1 = sb("v1", P, LH * EXT)
        am = [area_v[:, 0:512], area_v[:, 512:1024], area_s[:, 0:512], area_s[:, 512:1024]]
        lst = [v3(sb(f"lst{r}", P, 2, LG * EXT), 2) for r in range(B)]
        ltm = sb("ltm", P, 2 * LG * EXT)
        lbt = sb("lbt", P, 2 * LG)
        lden = sb("lden", P, LH)
        ly, lyT = yg[:, 0:D], gT[:, 0:D]

        rt = [sb(f"rt{k}", P, B * NE) for k in range(3)]
        rm = [sb(f"rm{k}", P, B) for k in range(4)]
        p8 = v3(sb("p8", P, B, 8), B)
        i8 = v3(sb("i8", P, B, 8, dt=U32), B)
        i8f = v3(sb("i8f", P, B, 2), B)
        g2 = v3(sb("g2", P, B, 2), B)
        gates = v3(sb("gates", P, B, GC), B)
        gatesT = sb("gatesT", GC, B * P)
        gh = sb("gh", P, KD, B * P)
        ghT = v3(gh, KD)
        gl = sb("gl", P, B * P)
        u = [u_ring[:, k * B * P:(k + 1) * B * P] for k in range(RING)]
        fo = sb("fo", P, B * L)
        foT, res_f = gl, (u[2], u[3])

        A = [ctx.enter_context(nc.psum_tensor(f"A{k}", [P, 512], F32)) for k in range(4)]
        F = [ctx.enter_context(nc.psum_tensor(f"F{k}", [P, 512], F32)) for k in range(4)]

        wmod = [xs_all]
        c_t = sb("c_t", P, 2, KD * B)
        c_s = sb("c_s", P, 2, KD * B)
        c_rep = area_v[:, 0:KD * B * P]
        gb1 = sb("gb1", P, NT)
        gsel = v3(sb("gsel", P, NT, GC), NT)
        b2rows = [sb(f"b2rows{y}", GC, L) for y in range(2)]
        b2sel = sb("b2sel", GC, GC)
        ub2 = area_s[:, 0:3 * D]

        def one(name):
            return ctx.enter_context(nc.semaphore(name))

        loaded = {k: one(f"loaded_{k}") for k in
                  ("w_in", "w_out", "lin", "ffn0", "ffn1", "small", "mod0", "mod1")}
        masks_made = one("masks_made")
        pool_chain = one("pool_chain")
        set_dve = one("set_dve")
        set_act = one("set_act")
        set_pe = one("set_pe")
        set_done = one("set_done")

        x_in = signal("x_in", 16)
        x_out = signal("x_out", 16)
        rope_in = signal("rope_in", 16)
        x_done = [None] + [signal(f"x{g}_done", B) for g in (1, 2, 3, 4)]
        copied = [None] + [signal(f"x{g}_copied", 2) for g in (1, 2, 3)]
        v_norm = [signal(f"norm{g}_var", 1) for g in range(4)]
        r_norm = [signal(f"norm{g}_rstd0", 1) for g in range(4)]
        xn_made = [signal(f"xn{g}_made", B) for g in range(4)]
        xn_turned = [signal(f"xn{g}_turned", 1) for g in range(4)]
        act_n = [signal(f"norm{g}_ln", 1) for g in range(4)]
        hT_made = [signal(f"hT{g}_made", B) for g in range(4)]
        dve_a0 = Chain(ctx, nc, "dve_a0", 50)
        act_a0 = Chain(ctx, nc, "act_a0", 1 + B)
        dt_raw = signal("dt_raw", 1)
        dt_abs = signal("dt_abs", 1)
        dt_ln = signal("dt_ln", 1)
        dA_made = signal("dA_made", 1)
        dec_raw = signal("dec_raw", 1)
        dec_made = signal("dec_made", 1)
        dtd_made = signal("dtd_made", 1)
        tail_put = signal("tail_put", XM)
        tail_kept = signal("tail_kept", XM)
        xbc_raw = signal("xbc_raw", XM)
        xbc_in = signal("xbc_in", XM)
        conv_made = signal("conv_made", XM)
        conv_tanh = signal("conv_tanh", XM)
        xs_made = signal("xs_made", XM)
        z_raw = signal("z_raw", B)
        z_tanh = signal("z_tanh", B)
        sz_made = signal("sz_made", B)
        xb_turned = signal("xb_turned", B)
        xt_made = signal("xt_made", B)
        va_made = signal("va_made", B)
        seg_raw = signal("seg_raw", 2 * B)
        seg_exp = signal("seg_exp", B)
        mh_made = signal("mh_made", B)
        xdt_made = signal("xdt_made", B)
        xd_made = signal("xd_made", B)
        yoff_raw = signal("yoff_raw", B)
        dst_raw = signal("dst_raw", B)
        ydiag_raw = signal("ydiag_raw", B)
        state_made = signal("state_made", B)
        yg_made = signal("yg_made", B)
        ysum_made = signal("ysum_made", B)
        ygn_made = signal("ygn_made", B)
        yg_turned = signal("yg_turned", B)
        gT_made = signal("gT_made", B)
        out0_raw = signal("out0_raw", B)
        ysq_ln = signal("ysq_ln", B)
        dve_y = Chain(ctx, nc, "dve_y", 5 * B)
        dve_a1 = Chain(ctx, nc, "dve_a1", 40)
        lg_raw = signal("lg_raw", 1)
        lg_v = signal("lg_v", 1)
        lg_e = signal("lg_e", 1)
        lg_b = signal("lg_b", 1)
        la_made = signal("la_made", 1)
        cs_raw = signal("cs_raw", 1)
        le_made = signal("le_made", 1)
        qk_raw = signal("qk_raw", B)
        v_raw = signal("v_raw", B)
        v1_made = signal("v1_made", B)
        qneg_made = signal("qneg_made", B)
        qexp_made = signal("qexp_made", B)
        qs_made = signal("qs_made", B)
        qk_turned = signal("qk_turned", B)
        qkT_made = signal("qkT_made", B)
        qpar_made = signal("qpar_made", B)
        att_raw = signal("att_raw", B)
        am_made = signal("am_made", B)
        ly_raw = signal("ly_raw", B)
        lst_raw = signal("lst_raw", B)
        lst_made = signal("lst_made", B)
        ly_made = signal("ly_made", B)
        ly_turned = signal("ly_turned", B)
        lyT_made = signal("lyT_made", B)
        out2_raw = signal("out2_raw", B)
        dve_f = [Chain(ctx, nc, f"dve_f{y}", 4 + 17) for y in range(2)]
        logit_raw = [signal(f"logit_raw{y}", 1) for y in range(2)]
        rt_max = [signal(f"rt_max{y}", 1) for y in range(2)]
        rt_exp = [signal(f"rt_exp{y}", 1) for y in range(2)]
        top_diff = [signal(f"top_diff{y}", 1) for y in range(2)]
        top_exp = [signal(f"top_exp{y}", 1) for y in range(2)]
        gates_made = [signal(f"gates_made{y}", 1) for y in range(2)]
        gates_turned = [signal(f"gates_turned{y}", 1) for y in range(2)]
        gatesT_made = [signal(f"gatesT_made{y}", 1) for y in range(2)]
        lh_raw = [signal(f"lh_raw{y}", 1) for y in range(2)]
        gl_made = [signal(f"gl_made{y}", 1) for y in range(2)]
        gh_made = [signal(f"gh_made{y}", 1) for y in range(2)]
        hid_raw = [signal(f"hid_raw{y}", NT + 1) for y in range(2)]
        u_made = [signal(f"u_made{y}", NT + 1) for y in range(2)]
        exp_raw = [signal(f"exp_raw{y}", NE + 1) for y in range(2)]
        fo_made = [signal(f"fo_made{y}", NE + 1) for y in range(2)]
        fo_turned = [signal(f"fo_turned{y}", 1) for y in range(2)]
        foT_made = [signal(f"foT_made{y}", 1) for y in range(2)]
        outf_raw = [signal(f"outf_raw{y}", 2) for y in range(2)]
        res_made = [signal(f"res_made{g}", 1) for g in range(4)]

        def bc(ap, *shape):
            return ap.to_broadcast(list(shape))

        def walk(eng, attn0, ffn, attn1):
            def one_block(blk):
                attn0(blk)
                ffn(0, blk)
                attn1(blk)
                ffn(1, blk)

            one_block(0)
            with eng.Fori(1, NBLK) as blk:
                one_block(blk)

        block = ctx.enter_context(nc.Block())

        @block.sync
        def _(sp):
            sp.dma_start(c_t[:, :], dram["c_t"]).then_inc(loaded["small"], 16)
            sp.dma_start(mam_c[:, :], dram["mam_c"]).then_inc(loaded["small"], 16)
            sp.dma_start(rows[:, :], dram["rows"]).then_inc(loaded["small"], 16)
            for y in range(2):
                sp.dma_start(ffn_c[y][:, :], dram[f"ffn_c{y}"]).then_inc(loaded["small"], 16)
                sp.dma_start(b2rows[y][:, :], dram[f"b2rows{y}"]).then_inc(loaded["small"], 16)
            sp.dma_start(out_bias, dram["ub"]).then_inc(loaded["small"], 16)
            sp.dma_start(ub2, dram["ub2"]).then_inc(loaded["small"], 16)
            sp.dma_start(wmod[0][:, :], dram["wmod0"]).then_inc(loaded["mod0"], 16)
            sp.dma_start(w_in, dram["w_in"]).then_inc(loaded["w_in"], 16)
            sp.dma_start(w_out, dram["w_out"]).then_inc(loaded["w_out"], 16)
            sp.dma_start(ffn_w[0][:, :], dram["ffn_w0"]).then_inc(loaded["ffn0"], 16)
            sp.dma_start(lin_w[:, :], dram["lin_w"]).then_inc(loaded["lin"], 16)
            sp.dma_start(ffn_w[1][:, :], dram["ffn_w1"]).then_inc(loaded["ffn1"], 16)
            sp.wait_ge(set_pe, MOD_READ)
            sp.dma_start(wmod[0][:, :], dram["wmod1"]).then_inc(loaded["mod1"], 16)

            def load(blk):
                wait_before(sp, copied[1], blk, 1)
                wait_before(sp, xn_made[1], blk, B - 1)
                sp.dma_start(v3(x_of[0], B), dram["x"][:, bass.ts(blk, P), :].rearrange("b t d -> t b d")
                             ).then_inc(x_in.sem, 16)
                wait_before(sp, qs_made, blk, B - 1)
                sp.dma_start(rope, dram["rope"][bass.ts(blk, P), :].rearrange("t (a b) -> t a b", a=2)
                             ).then_inc(rope_in.sem, 16)

            def store(blk):
                sp.wait_ge(*x_done[4](blk, B - 1))
                sp.dma_start(out[:, bass.ts(blk, P), :].rearrange("b t d -> t b d"), v3(x_of[3], B)
                             ).then_inc(x_out.sem, 16)

            load(0)
            with sp.Fori(1, NBLK) as blk:
                before = sp.snap(blk - 1)
                for v in (blk * 2, blk * B):
                    sp.compute_val(v)
                load(blk)
                store(before)
            store(NBLK - 1)
            sp.wait_ge(x_out.sem, 16 * NBLK)

        @block.gpsimd
        def _(pool):
            made = [0]

            def mask(t, rows_, cols, base, mult, pattern, op, fill, view=None):
                pool.affine_select(out=t, in_=t, compare_op=op, fill=fill, base=base,
                                   pattern=pattern, channel_multiplier=mult).then_inc(pool_chain, 1)
                made[0] += 1
                pool.wait_ge(pool_chain, made[0])

            def clear(t, value=0.0):
                pool.memset(t, value).then_inc(pool_chain, 1)
                made[0] += 1

            clear(ident[:, :])
            clear(upto[:, :], 1.0)
            clear(after[:, :], 1.0)
            clear(ones[:, :], 1.0)
            clear(block8[:, :], 1.0)
            clear(parity[:, :], 0.0)
            clear(eps_ln[:, :], 1e-05)
            clear(tails[:, :, :, :])
            for r in range(B):
                clear(state[r][:, :])
                clear(lst[r])
            clear(gates)
            clear(v1[:, :], 1.0)
            clear(gsel)
            clear(b2sel[:, :])
            for e in range(NE):
                clear(iota8[:, e:e + 1], float(e))
            pool.wait_ge(pool_chain, made[0])
            mask(ident[:, :], P, P, 0, 1, [[-1, P]], ALU.not_equal, 1.0)
            mask(upto[:, :], P, P, 0, -1, [[1, P]], ALU.is_ge, 0.0)
            mask(after[:, :], P, P, 0, 1, [[-1, P]], ALU.is_gt, 0.0)
            mask(block8[:, :], P, LG, 0, 1, [[-LD, LG]], ALU.is_ge, 0.0)
            mask(block8[:, :], P, LG, LD - 1, -1, [[LD, LG]], ALU.is_ge, 0.0)
            clear(gates[:, :, NE:GC], 1.0)
            clear(b2sel[:, NE:GC], 1.0)
            pool.wait_ge(pool_chain, made[0])
            mask(b2sel[:, NE:GC], GC, 1, -NE, 1, [[0, 1]], ALU.not_equal, 0.1)
            pool.memset(th[:, 0:1], 0.0).then_inc(masks_made, 1)
            pool.wait_ge(masks_made, 1)
            pool.wait_ge(loaded["small"], 16 * NSMALL)
            pool.tensor_tensor(out_bias, out_bias, v3(ub2, 3), ALU.add).then_inc(set_done, 1)
            pool.wait_ge(set_done, 1)

            def attn0(blk):
                unit = v3_(ones[:, 0:B * (CONV - 1)], B)
                for m in range(XM):
                    if m >= 2:
                        pool.wait_ge(*conv_made(blk, m - 2))
                    else:
                        pool.wait_ge(*hT_made[0](blk, B - 1))
                    wait_before(pool, tail_kept, blk, m)
                    tail = tails[:, m, :, :]
                    pool.tensor_tensor(raw[:, m % 2, :, 0:CONV - 1], tail, unit, ALU.mult).then_inc(tail_put.sem, 1)
                    pool.wait_ge(*tail_put(blk, m))
                    pool.wait_ge(*xbc_in(blk, m))
                    tail = raw[:, m % 2, :, P:P + CONV - 1]
                    pool.tensor_tensor(tails[:, m, :, :], tail, unit, ALU.mult).then_inc(tail_kept.sem, 1)
                pool.wait_ge(*dtd_made(blk))
                pool.wait_ge(*xs_made(blk, XM - 1))
                for r in range(B):
                    h = slice(r * NH, (r + 1) * NH)
                    pool.wait_ge(*xt_made(blk, r))
                    if r:
                        pool.wait_ge(*dst_raw(blk, r - 1))
                        pool.wait_ge(*yg_made(blk, r - 1))
                    pool.tensor_tensor(v3(xdec, NH), v3(xt, NH), bc(dtd[:, h].unsqueeze(2), P, NH, HD),
                                       ALU.mult).then_inc(xdt_made.sem, 1)
                    pool.tensor_tensor(v3(xd, NH), v3(xt, NH),
                                       bc(rows[:, R_D:R_D + NH].unsqueeze(2), P, NH, HD),
                                       ALU.mult).then_inc(xd_made.sem, 1)

            def copy_with_bias(g, blk):
                pool.wait_ge(*x_done[g](blk, B - 1))
                if g < 3:
                    wait_before(pool, copied[g + 1], blk, 1)
                    wait_before(pool, xn_made[g + 1], blk, B - 1)
                elif not isinstance(blk, int) or blk:
                    pool.wait_ge(x_out.sem, blk * 16)
                pool.tensor_tensor(v3(x_of[g], B), v3(gate_bc[g], B), bc(out_bias[:, g - 1:g, :], P, B, D),
                                   ALU.mult).then_inc(copied[g].sem, 1)
                pool.wait_ge(*copied[g](blk, 0))
                pool.tensor_tensor(x_of[g][:, :], x_of[g][:, :], x_in_of[g][:, :], ALU.add
                                   ).then_inc(copied[g].sem, 1)

            def attn1(blk):
                copy_with_bias(2, blk)

            def ffn(y, blk):
                copy_with_bias(1 + 2 * y, blk)

            walk(pool, attn0, ffn, attn1)

        @block.scalar
        def _(act):
            act.wait_ge(loaded["small"], 16 * NSMALL)
            act.activation(c_s[:, :], c_t[:, :], ACT.Tanh, scale=0.5).then_inc(set_act, 1)
            act.activation(a_neg[:, :], rows[:, R_AL:R_AL + NH], ACT.Exp).then_inc(set_act, 1)
            act.activation(gb1[:, :], ffn_c[0][:, C_B1:C_B1 + NT], ACT.Gelu).then_inc(set_act, 1)
            act.wait_ge(set_dve, SET_SEL0)
            act.activation(gb1[:, :], ffn_c[1][:, C_B1:C_B1 + NT], ACT.Gelu).then_inc(set_act, 1)
            act.wait_ge(set_dve, SET_ALL)
            act.wait_ge(masks_made, 1)

            def norm(g, blk):
                s = g % 2
                act.wait_ge(*v_norm[g](blk))
                act.activation(rtmp[s][:, :], var_e[s][:, :], ACT.Ln).then_inc(act_n[g].sem, 1)
                act.wait_ge(*act_n[g](blk))
                act.activation(rstd[s][:, :], rtmp[s][:, :], ACT.Exp, scale=-0.5).then_inc(r_norm[g].sem, 1)
                bank = A if s == 0 else F
                act.wait_ge(*xn_turned[g](blk))
                for r in range(B):
                    for k in range(KD):
                        last = act.activation(hT[s][:, k, r * P:(r + 1) * P], bank[k][:, r * P:(r + 1) * P],
                                              ACT.Identity, scale=mod_c[g][:, 1, k, r:r + 1],
                                              bias=mod_c[g][:, 0, k, r:r + 1])
                    last.then_inc(hT_made[g].sem, 1)

            def attn0(blk):
                norm(0, blk)
                act.wait_ge(*dt_abs(blk))
                act_a0.step(act, blk, act.activation(dt_n[:, :], dt_n[:, :], ACT.Exp))
                act.activation(dt_n[:, :], dt_n[:, :], ACT.Ln, bias=1.0).then_inc(dt_ln.sem, 1)
                act.wait_ge(*dec_raw(blk))
                act.activation(dec[:, :], A[2][:, B * NH:4 * B * NH], ACT.Exp).then_inc(dec_made.sem, 1)
                def conv_tanh_of(m):
                    act.wait_ge(*conv_made(blk, m))
                    if m >= 2:
                        act.wait_ge(*xs_made(blk, m - 2))
                    act.activation(v3(th, 2)[:, m % 2, :], acc[:, m % 2, :], ACT.Tanh).then_inc(conv_tanh.sem, 1)

                for m in range(XM):
                    act.wait_ge(*xbc_raw(blk, m))
                    if m >= 2:
                        act.wait_ge(*conv_made(blk, m - 2))
                        act.wait_ge(*tail_kept(blk, m - 2))
                    act.activation(raw[:, m % 2, :, CONV - 1:], v3(A[(m + 3) % 4], B), ACT.Copy
                                   ).then_inc(xbc_in.sem, 1)
                    if m:
                        conv_tanh_of(m - 1)
                conv_tanh_of(XM - 1)
                for r in range(B):
                    act.wait_ge(*xb_turned(blk, r))
                    if r:
                        act.wait_ge(*xd_made(blk, r - 1))
                    act.activation(xt[:, :], A[2][:, :], ACT.Copy)
                    act.activation(bt[:, :], A[3][:, 0:NS], ACT.Copy).then_inc(xt_made.sem, 1)
                    act.wait_ge(*z_raw(blk, r))
                    act.activation(tz[:, :], A[1][:, :], ACT.Tanh).then_inc(z_tanh.sem, 1)
                    act.wait_ge(*seg_raw(blk, 2 * r))
                    act.activation(seg[:, 0:512], A[0][:, :], ACT.Exp)
                    act.wait_ge(*seg_raw(blk, 2 * r + 1))
                    act.activation(seg[:, 512:1024], A[1][:, :], ACT.Exp).then_inc(seg_exp.sem, 1)
                    act.wait_ge(*yg_made(blk, r))
                    act_a0.step(act, blk, act.activation(gT[:, :], yg[:, :], ACT.Square,
                                                         accum_out=yst[:, 0:1]))
                    act.activation(yst[:, 1:2], yst[:, 0:1], ACT.Ln, scale=1.0 / DI,
                                   bias=eps_ln[:, 0:1]).then_inc(ysq_ln.sem, 1)
                    act.wait_ge(*ysq_ln(blk, r))
                    act.activation(yst[:, 2:3], yst[:, 1:2], ACT.Exp, scale=-0.5).then_inc(ysum_made.sem, 1)
                    act.wait_ge(*yg_turned(blk, r))
                    act.activation(gT[:, :], A[0][:, :], ACT.Copy).then_inc(gT_made.sem, 1)
                act_a0.close()

            def attn1(blk):
                norm(2, blk)
                act.wait_ge(*lg_v(blk))
                act.activation(lg[:, :], lg[:, :], ACT.Exp, scale=-1.0).then_inc(lg_e.sem, 1)
                act.wait_ge(*lg_b(blk))
                act.activation(la[:, :], la[:, :], ACT.Ln).then_inc(la_made.sem, 1)
                act.wait_ge(*cs_raw(blk))
                act.activation(le[:, 0, :, :], v3_(A[2][:, 64:128], B), ACT.Exp)
                act.activation(le[:, 1, :, :], v3_(A[2][:, 64:128], B), ACT.Exp, scale=-1.0)
                act.activation(le[:, 2, :, :], v3_(A[2][:, 128:192], B), ACT.Exp).then_inc(le_made.sem, 1)
                for r in range(B):
                    act.wait_ge(*v_raw(blk, r))
                    if r:
                        act.wait_ge(*ly_raw(blk, r - 1))
                        act.wait_ge(*lst_raw(blk, r - 1))
                    act.activation(v3(v1, LH)[:, :, 0:LD], v3_(A[1][:, 0:D], LH), ACT.Copy
                                   ).then_inc(v1_made.sem, 1)
                    act.wait_ge(*qneg_made(blk, r))
                    act.activation(qm[:, :], qm[:, :], ACT.Exp).then_inc(qexp_made.sem, 1)
                    act.wait_ge(*qk_turned(blk, r))
                    act.activation(qkT, v3_(A[0][:, :], 4), ACT.Copy).then_inc(qkT_made.sem, 1)
                    act.wait_ge(*ly_turned(blk, r))
                    act.activation(lyT[:, :], A[2][:, 0:D], ACT.Copy).then_inc(lyT_made.sem, 1)

            def ffn(y, blk):
                g = 1 + 2 * y
                norm(g, blk)
                act.wait_ge(*rt_max[y](blk))
                act.activation(rt[1][:, :], rt[0][:, :], ACT.Exp).then_inc(rt_exp[y].sem, 1)
                act.wait_ge(*top_diff[y](blk))
                act.activation(rm[2][:, :], rm[1][:, :], ACT.Exp).then_inc(top_exp[y].sem, 1)
                act.wait_ge(*lh_raw[y](blk))
                act.activation(gl[:, :], F[3][:, :], ACT.Gelu, bias=ffn_c[y][:, C_DOWN:C_DOWN + 1]
                               ).then_inc(gl_made[y].sem, 1)
                act.activation(ghT, hT[1], ACT.Gelu).then_inc(gh_made[y].sem, 1)
                act.wait_ge(*gates_turned[y](blk))
                act.activation(gatesT[:, :], F[2][0:GC, :], ACT.Copy).then_inc(gatesT_made[y].sem, 1)
                for j in range(NT + 1):
                    act.wait_ge(*hid_raw[y](blk, j))
                    col = C_S1 if j == 0 else C_B1 + j - 1
                    if j >= RING:
                        act.wait_ge(*exp_raw[y](blk, reader(j - RING)))
                    act.activation(u[j % RING][:, :], F[j % 2][:, :], ACT.Gelu,
                                   bias=ffn_c[y][:, col:col + 1]).then_inc(u_made[y].sem, 1)
                act.wait_ge(*fo_turned[y](blk))
                act.activation(foT[:, :], F[0][:, :], ACT.Copy).then_inc(foT_made[y].sem, 1)

            walk(act, attn0, ffn, attn1)

        @block.vector
        def _(dve):
            made = [0]

            def setup(ins):
                made[0] += 1
                ins.then_inc(set_dve, 1)
                dve.wait_ge(set_dve, made[0])

            dve.wait_ge(masks_made, 1)
            dve.wait_ge(set_act, 1)
            setup(dve.tensor_scalar(c_t[:, :], c_t[:, :], 0.5, None, ALU.mult))
            setup(dve.scalar_tensor_tensor(c_s[:, :], c_s[:, :], 1.0, c_t[:, :], ALU.add, ALU.mult))
            assert made[0] == SET_C
            dve.wait_ge(set_act, 2)
            setup(dve.tensor_scalar(a_neg[:, :], a_neg[:, :], -1.0, None, ALU.mult))
            for y in range(2):
                setup(dve.tensor_tensor(router_bias[y][:, :], rows[:, R_RB + 8 * y:R_RB + 8 * y + 8],
                                        rows[:, R_COST:R_COST + 8], ALU.subtract))
            setup(dve.tensor_scalar(mam_c[:, 0:C_NW], mam_c[:, 0:C_NW], 0.5, None, ALU.mult))
            dve.wait_ge(loaded["w_in"], 16)
            setup(dve.tensor_scalar(w_in[:, :, 0:DI], w_in[:, :, 0:DI], 0.5, None, ALU.mult))
            dve.wait_ge(loaded["w_out"], 16)
            for k in range(DI // P):
                setup(dve.tensor_scalar(w_out[:, k, :], w_out[:, k, :], mam_c[:, C_NW + k:C_NW + k + 1],
                                        None, ALU.mult))
            dve.wait_ge(set_act, 2)
            for y in range(2):
                setup(dve.tensor_reduce(parity[:, y:y + 1], v3(block8, LG // 2)[:, :, y], AX_X, ALU.add))
            for y in range(2):
                dve.wait_ge(loaded[f"ffn{y}"], 16)
                dve.wait_ge(set_act, 3 + y)
                if y:
                    dve.wait_ge(set_pe, CONST_READ0)
                for e in range(NE):
                    j = slice(FIRST[e], FIRST[e] + TILES[e])
                    setup(dve.tensor_scalar(gsel[:, j, e:e + 1], gb1[:, j].unsqueeze(2), -1.0, None, ALU.mult))
                setup(dve.tensor_copy(gsel[:, :, NE:GC], gb1[:, :].unsqueeze(2)))
                setup(dve.tensor_scalar(ffn_w[y][:, W_S2:W_S2 + L], ffn_w[y][:, W_S2:W_S2 + L], 0.1,
                                        None, ALU.mult))
                assert made[0] == (SET_SEL0, SET_SEL1)[y]
                dve.wait_ge(set_pe, (CONST_DONE0, CONST_DONE1)[y])
                setup(dve.tensor_copy(cw[y][:, :], F[0][0:GC, 0:L]))
            assert made[0] == SET_CW
            for y in range(2):
                if y:
                    dve.wait_ge(set_pe, MOD_READ)
                setup(dve.tensor_copy(c_rep.rearrange("p (a b) -> p a b", a=KD * B),
                                      bc(v3(c_s, 2)[:, y, :].unsqueeze(2), P, KD * B, P)))
                assert made[0] == (SET_REP0, SET_REP1)[y]
                dve.wait_ge(set_pe, (MODC0, MODC1)[y])
                for s in range(2):
                    src = F[1][:, 16 * s:16 * s + 16].rearrange("p (w k b) -> p w k b", w=2, k=KD)
                    setup(dve.tensor_copy(mod_c[2 * y + s][:, 0, :, :], src[:, 0, :, :]))
                    setup(dve.tensor_scalar(mod_c[2 * y + s][:, 1, :, :], src[:, 1, :, :], 1.0, None, ALU.add))
                for s in range(2):
                    for h in range(2):
                        n = 2 * s + h
                        dve.wait_ge(set_pe, (MODC0, MODC1)[y] + 1 + n)
                        gb = gate_bc[2 * y + s][:, h * 2 * D:(h + 1) * 2 * D]
                        src = F[2 + h][:, :]
                        sign = u[2]
                        setup(dve.tensor_scalar(sign, src, 0.0, 2.0, ALU.is_ge, ALU.mult))
                        setup(dve.tensor_scalar(sign, sign, -1.0, None, ALU.add))
                        setup(dve.tensor_tensor(gb, sign, src, ALU.mult))
                        setup(dve.scalar_tensor_tensor(gb, gb, 0.25, sign, ALU.max, ALU.mult))
            assert made[0] == SET_GATES == SET_ALL
            dve.wait_ge(set_done, 1)

            def carry_wait():
                dve.memset(spare[:, 0:1], 0.0)

            def norm(g, blk, chain):
                s = g % 2
                xg = v3(x_in_of[g], B)
                if g == 0:
                    dve.wait_ge(x_in.sem, blk * 16 + 16)
                else:
                    dve.wait_ge(*x_done[g](blk, B - 1))
                for r in range(B):
                    last = dve.bn_stats(v3(stats[s], B)[:, r, :], xg[:, r, :])
                chain.step(dve, blk, last)
                carry_wait()
                for r in range(B):
                    last = dve.bn_aggr(v3(mv[s], B)[:, r, :], v3(stats[s], B)[:, r, :])
                chain.step(dve, blk, last)
                dve.tensor_scalar(var_e[s][:, :], v3(mv[s], B)[:, :, 1], 1e-05, None, ALU.add
                                  ).then_inc(v_norm[g].sem, 1)
                dve.wait_ge(*r_norm[g](blk))
                chain.step(dve, blk, dve.tensor_tensor(rtmp[s][:, :], rstd[s][:, :], rstd[s][:, :], ALU.mult))
                chain.step(dve, blk, dve.tensor_tensor(rtmp[s][:, :], rtmp[s][:, :], var_e[s][:, :], ALU.mult))
                chain.step(dve, blk, dve.tensor_scalar(rtmp[s][:, :], rtmp[s][:, :], -0.5, 1.5, ALU.mult, ALU.add))
                chain.step(dve, blk, dve.tensor_tensor(rstd[s][:, :], rstd[s][:, :], rtmp[s][:, :], ALU.mult))
                for r in range(B):
                    dve.tensor_scalar(v3(xn[s], B)[:, r, :], xg[:, r, :], v3(mv[s], B)[:, r, 0:1],
                                      rstd[s][:, r:r + 1], ALU.subtract, ALU.mult).then_inc(xn_made[g].sem, 1)

            def residual(g, blk, bank, cols, r, n, tmp, chain):
                w = slice(r * D, (r + n) * D)
                chain.step(dve, blk, dve.tensor_tensor(tmp, bank[:, cols], gate_bc[g][:, w], ALU.mult))
                dve.tensor_tensor(x_of[g][:, w], x_of[g][:, w], tmp, ALU.add).then_inc(x_done[g + 1].sem, n)

            def attn0(blk):
                c = dve_a0
                norm(0, blk, c)
                dve.wait_ge(*dt_raw(blk))
                c.step(dve, blk, dve.tensor_tensor(v3(dt_v, B), v3_(A[2][:, 0:B * NH], B),
                                                   bc(rows[:, R_DT:R_DT + NH].unsqueeze(1), P, B, NH), ALU.add))
                dve.scalar_tensor_tensor(dt_n[:, :], dt_v[:, :], -1.0, dt_v[:, :], ALU.mult, ALU.min
                                         ).then_inc(dt_abs.sem, 1)
                dve.wait_ge(*dt_ln(blk))
                c.step(dve, blk, dve.scalar_tensor_tensor(dt_s[:, :], dt_v[:, :], 0.0, dt_n[:, :],
                                                          ALU.max, ALU.add))
                dve.tensor_tensor(v3(dA, B), v3(dt_s, B), bc(a_neg[:, :].unsqueeze(1), P, B, NH), ALU.mult
                                  ).then_inc(dA_made.sem, 1)
                dve.wait_ge(*dec_made(blk))
                dve.tensor_tensor(dtd[:, :], dt_s[:, :], v3(dec, 3)[:, 0, :], ALU.mult).then_inc(dtd_made.sem, 1)
                for m in range(XM):
                    dve.wait_ge(*xbc_in(blk, m))
                    dve.wait_ge(*tail_put(blk, m))
                    if m >= 2:
                        dve.wait_ge(*xs_made(blk, m - 2))
                    o = v3(acc[:, m % 2, :], B)
                    src = raw[:, m % 2, :, :]
                    w = [mam_c[:, C_CW + m * CONV + k:C_CW + m * CONV + k + 1] for k in range(CONV)]
                    c.step(dve, blk, dve.tensor_scalar(o, src[:, :, 3:3 + P], w[3],
                                                       mam_c[:, C_CB + m:C_CB + m + 1], ALU.mult, ALU.add))
                    for k in (0, 1):
                        c.step(dve, blk, dve.scalar_tensor_tensor(o, src[:, :, k:k + P], w[k], o,
                                                                  ALU.mult, ALU.add))
                    dve.scalar_tensor_tensor(o, src[:, :, 2:2 + P], w[2], o, ALU.mult, ALU.add
                                             ).then_inc(conv_made.sem, 1)
                    if m:
                        silu(blk, m - 1)
                silu(blk, XM - 1)
                for r in range(B):
                    h = slice(r * NH, (r + 1) * NH)
                    dve.wait_ge(*dA_made(blk))
                    if r:
                        dve.wait_ge(*seg_raw(blk, 2 * r - 1))
                    else:
                        dve.wait_ge(*tail_kept(blk, XM - 1))
                    dve.tensor_tensor(v3(va, NH), bc(upto[:, :].unsqueeze(1), P, NH, P),
                                      bc(dA[:, h].unsqueeze(2), P, NH, P), ALU.mult).then_inc(va_made.sem, 1)
                    dve.wait_ge(*z_tanh(blk, r))
                    dve.scalar_tensor_tensor(sz[:, :], tz[:, :], 1.0, A[1][:, :], ALU.add, ALU.mult
                                             ).then_inc(sz_made.sem, 1)
                    dve.wait_ge(*xt_made(blk, r))
                    c.step(dve, blk, dve.tensor_tensor(cbm[:, :], A[3][:, NS:2 * NS], upto[:, :], ALU.mult))
                    dve.tensor_tensor(v3(xdt, NH), v3(xt, NH), bc(dt_s[:, h].unsqueeze(2), P, NH, HD), ALU.mult)
                    dve.wait_ge(*seg_exp(blk, r))
                    dve.tensor_tensor(v3(seg, NH), v3(seg, NH), bc(cbm[:, :].unsqueeze(1), P, NH, P), ALU.mult
                                      ).then_inc(mh_made.sem, 1)
                    dve.wait_ge(*yoff_raw(blk, r))
                    c.step(dve, blk, dve.tensor_tensor(v3(yg, NH), v3_(A[0][:, :], NH),
                                                       bc(v3(dec, 3)[:, 1, h].unsqueeze(2), P, NH, HD), ALU.mult))
                    dve.wait_ge(*xd_made(blk, r))
                    c.step(dve, blk, dve.tensor_tensor(yg[:, :], yg[:, :], xd[:, :], ALU.add))
                    c.step(dve, blk, dve.tensor_tensor(v3(state[r], NH), v3(state[r], NH),
                                                       bc(v3(dec, 3)[:, 2, h].unsqueeze(2), P, NH, HD), ALU.mult))
                    dve.wait_ge(*dst_raw(blk, r))
                    dve.tensor_tensor(state[r][:, :], state[r][:, :], A[1][:, :], ALU.add
                                      ).then_inc(state_made.sem, 1)
                    dve.wait_ge(*ydiag_raw(blk, r))
                    c.step(dve, blk, dve.tensor_tensor(yg[:, :], yg[:, :], A[2][:, :], ALU.add))
                    dve.tensor_tensor(yg[:, :], yg[:, :], sz[:, :], ALU.mult).then_inc(yg_made.sem, 1)
                    dve.wait_ge(*ysum_made(blk, r))
                    newton(blk)
                    dve.tensor_scalar(yg[:, :], yg[:, :], yst[:, 2:3], None, ALU.mult).then_inc(ygn_made.sem, 1)
                    dve.wait_ge(*out0_raw(blk, r))
                    residual(0, blk, A[3], slice(2 * NS, 2 * NS + D), r, 1, res_a[:, :], c)
                c.close()
                dve_y.close()

            def newton(blk):
                c = dve_y
                c.step(dve, blk, dve.tensor_scalar(yst2[:, 0:1], yst[:, 0:1], 1.0 / DI, 1e-05, ALU.mult, ALU.add))
                c.step(dve, blk, dve.tensor_tensor(yst2[:, 1:2], yst[:, 2:3], yst[:, 2:3], ALU.mult))
                c.step(dve, blk, dve.tensor_tensor(yst2[:, 1:2], yst2[:, 1:2], yst2[:, 0:1], ALU.mult))
                c.step(dve, blk, dve.tensor_scalar(yst2[:, 1:2], yst2[:, 1:2], -0.5, 1.5, ALU.mult, ALU.add))
                c.step(dve, blk, dve.tensor_tensor(yst[:, 2:3], yst[:, 2:3], yst2[:, 1:2], ALU.mult))

            def silu(blk, m):
                dve.wait_ge(*conv_tanh(blk, m))
                dve.scalar_tensor_tensor(xs[:, m, :], v3(th, 2)[:, m % 2, :], 1.0, acc[:, m % 2, :],
                                         ALU.add, ALU.mult).then_inc(xs_made.sem, 1)

            def attn1(blk):
                c = dve_a1
                norm(2, blk, c)
                dve.wait_ge(*lg_raw(blk))
                dve.tensor_tensor(v3(lg, B), v3_(A[2][:, 0:B * LH], B),
                                  bc(rows[:, R_BG:R_BG + LH].unsqueeze(1), P, B, LH), ALU.add
                                  ).then_inc(lg_v.sem, 1)
                dve.wait_ge(*lg_e(blk))
                c.step(dve, blk, dve.tensor_scalar(la[:, :], lg[:, :], 1.0, None, ALU.add))
                c.step(dve, blk, dve.reciprocal(la[:, :], la[:, :]))
                dve.tensor_scalar(la[:, :], la[:, :], 0.8, 0.9995, ALU.max, ALU.min).then_inc(lg_b.sem, 1)
                dve.wait_ge(*le_made(blk))
                dve.wait_ge(rope_in.sem, blk * 16 + 16)
                for r in range(B):
                    dve.wait_ge(*qk_raw(blk, r))
                    half = LD // 2
                    both = A[0][:, :].rearrange("p (h t e) -> p (h t) e", t=2, e=half)
                    cos = bc(rope[:, 0, :].unsqueeze(1), P, 4 * LH, half)
                    sin = bc(rope[:, 1, :].unsqueeze(1), P, 4 * LH, half)
                    dve.tensor_tensor(v3(qr1, 4 * LH), both, cos, ALU.mult)
                    c.step(dve, blk, dve.tensor_tensor(v3(qr2, 4 * LH), both, sin, ALU.mult))
                    t1, t2, o = (v4(t, 2 * LH, 2) for t in (qr1, qr2, qk))
                    dve.tensor_tensor(o[:, :, 0, :], t1[:, :, 0, :], t2[:, :, 1, :], ALU.subtract)
                    c.step(dve, blk, dve.tensor_tensor(o[:, :, 1, :], t2[:, :, 0, :], t1[:, :, 1, :], ALU.add))
                    dve.tensor_scalar(qm[:, :], qk[:, :], 0.0, None, ALU.min).then_inc(qneg_made.sem, 1)
                    dve.wait_ge(*qexp_made(blk, r))
                    c.step(dve, blk, dve.scalar_tensor_tensor(qk[:, :], qk[:, :], 0.0, qm[:, :], ALU.max, ALU.add))
                    for n in range(2):
                        q = slice(n * D, (n + 1) * D)
                        last = dve.tensor_tensor(v3_(qk[:, q], LH), v3_(qk[:, q], LH),
                                                 bc(le[:, n, r, :].unsqueeze(2), P, LH, LD), ALU.mult)
                    last.then_inc(qs_made.sem, 1)
                    dve.wait_ge(*qkT_made(blk, r))
                    for n in range(2):
                        last = dve.tensor_tensor(qpar[:, n, :, :], bc(qkT[:, n, :].unsqueeze(1), P, 2, P),
                                                 bc(parity[:, :].unsqueeze(2), P, 2, P), ALU.mult)
                    last.then_inc(qpar_made.sem, 1)
                    c.step(dve, blk, dve.tensor_tensor(v3(lbt, 2), v3_(le[:, 2, r, :], 2),
                                                       bc(block8[:, :].unsqueeze(1), P, 2, LG), ALU.mult))
                    dve.wait_ge(*att_raw(blk, r))
                    for k in range(4):
                        last = dve.tensor_tensor(v3(am[k], 4),
                                                 v3_(A[k][:, :], 4), bc(upto[:, :].unsqueeze(1), P, 4, P), ALU.mult)
                    last.then_inc(am_made.sem, 1)
                    dve.wait_ge(*ly_raw(blk, r))
                    num = A[0][:, 0:LH * EXT].rearrange("p (h e) -> p h e", h=LH)
                    c.step(dve, blk, dve.tensor_scalar(lden[:, :].unsqueeze(2), num[:, :, LD:EXT], 1e-06, None, ALU.add))
                    c.step(dve, blk, dve.reciprocal(lden[:, :], lden[:, :]))
                    dve.tensor_tensor(v3(ly, LH), num[:, :, 0:LD], bc(lden[:, :].unsqueeze(2), P, LH, LD),
                                      ALU.mult).then_inc(ly_made.sem, 1)
                    dve.wait_ge(*lst_raw(blk, r))
                    sums = A[1][:, 0:2 * LG * EXT]
                    c.step(dve, blk, dve.tensor_tensor(v3(ltm, 2), lst[r], v3_(sums, 2), ALU.add))
                    dve.tensor_tensor(lst[r].rearrange("p g (h e) -> p (g h) e", e=EXT), v3(ltm, 2 * LG),
                                      bc(lbt[:, :].unsqueeze(2), P, 2 * LG, EXT), ALU.mult).then_inc(lst_made.sem, 1)
                    dve.wait_ge(*out2_raw(blk, r))
                    if r == 0:
                        dve.wait_ge(*copied[2](blk, 1))
                    residual(2, blk, A[3], slice(0, D), r, 1, res_a[:, :], c)
                c.close()

            def ffn(y, blk):
                g, c = 1 + 2 * y, dve_f[y]
                norm(g, blk, c)
                e3 = v3(rt[0], B)
                dve.wait_ge(*logit_raw[y](blk))
                c.step(dve, blk, dve.tensor_tensor(e3, v3_(F[2][:, 0:B * NE], B),
                                                   bc(router_bias[y][:, :].unsqueeze(1), P, B, NE), ALU.add))
                c.step(dve, blk, dve.tensor_reduce(rm[0][:, :], e3, AX_X, ALU.max))
                dve.tensor_tensor(e3, e3, bc(rm[0][:, :].unsqueeze(2), P, B, NE), ALU.subtract
                                  ).then_inc(rt_max[y].sem, 1)
                dve.wait_ge(*rt_exp[y](blk))
                p3 = v3(rt[1], B)
                c.step(dve, blk, dve.tensor_reduce(rm[0][:, :], p3, AX_X, ALU.add))
                c.step(dve, blk, dve.reciprocal(rm[0][:, :], rm[0][:, :]))
                c.step(dve, blk, dve.tensor_tensor(p3, p3, bc(rm[0][:, :].unsqueeze(2), P, B, NE), ALU.mult))
                carry_wait()
                for r in range(B):
                    last = dve.max(p8[:, r, :], p3[:, r, :])
                c.step(dve, blk, last)
                dve.tensor_tensor(rm[1][:, :], p8[:, :, 1], p8[:, :, 0], ALU.subtract).then_inc(top_diff[y].sem, 1)
                for r in range(B):
                    last = dve.max_index(i8[:, r, :], p8[:, r, :], p3[:, r, :])
                c.step(dve, blk, last)
                c.step(dve, blk, dve.tensor_copy(i8f, i8[:, :, 0:2]))
                dve.wait_ge(*top_exp[y](blk))
                c.step(dve, blk, dve.tensor_scalar(rm[3][:, :], rm[2][:, :], 1.0, None, ALU.add))
                c.step(dve, blk, dve.reciprocal(g2[:, :, 0], rm[3][:, :]))
                c.step(dve, blk, dve.tensor_tensor(g2[:, :, 1], g2[:, :, 0], rm[2][:, :], ALU.mult))
                for n, t in ((0, rt[0]), (1, rt[2])):
                    last = dve.tensor_tensor(v3(t, B), bc(iota8[:, :].unsqueeze(1), P, B, NE),
                                             bc(i8f[:, :, n:n + 1], P, B, NE), ALU.is_equal)
                c.step(dve, blk, last)
                for n, t in ((0, rt[0]), (1, rt[2])):
                    last = dve.tensor_tensor(v3(t, B), v3(t, B), bc(g2[:, :, n:n + 1], P, B, NE), ALU.mult)
                c.step(dve, blk, last)
                dve.tensor_tensor(gates[:, :, 0:NE], e3, v3(rt[2], B), ALU.add).then_inc(gates_made[y].sem, 1)
                dve.wait_ge(*exp_raw[y](blk, 0))
                dve.tensor_copy(fo[:, :], F[2][:, :]).then_inc(fo_made[y].sem, 1)
                for e in range(NE):
                    dve.wait_ge(*fo_made[y](blk, e))
                    dve.wait_ge(*exp_raw[y](blk, e + 1))
                    for r in range(B):
                        w = slice(r * L, (r + 1) * L)
                        last = dve.scalar_tensor_tensor(fo[:, w], F[2 + (e + 1) % 2][:, w], gates[:, r, e:e + 1],
                                                        fo[:, w], ALU.mult, ALU.add)
                    last.then_inc(fo_made[y].sem, 1)
                dve.wait_ge(*copied[g](blk, 1))
                for n in range(2):
                    dve.wait_ge(*outf_raw[y](blk, n))
                    residual(g, blk, F[2 + n], slice(0, 2 * D), 2 * n, 2, res_f[n][:, :], c)
                c.close()

            walk(dve, attn0, ffn, attn1)

        @block.tensor
        def _(pe):
            made = [0]

            def setup(ins):
                made[0] += 1
                ins.then_inc(set_pe, 1)

            for y in range(2):
                pe.wait_ge(set_dve, (SET_SEL0, SET_SEL1)[y])
                for j in range(NT):
                    last = pe.matmul(F[0][0:GC, 0:L], gsel[:, j, :], ffn_w[y][:, W_E2 + j * L:W_E2 + (j + 1) * L],
                                     start=(j == 0), stop=False)
                setup(last)
                setup(pe.matmul(F[0][0:GC, 0:L], b2sel[:, :], b2rows[y][:, :], start=False, stop=True))
                assert made[0] == (CONST_DONE0, CONST_DONE1)[y]
                if y == 0:
                    pe.wait_ge(set_dve, SET_SEL0 + 1)
            for y in range(2):
                pe.wait_ge(loaded[f"mod{y}"], 16)
                pe.wait_ge(set_dve, (SET_REP0, SET_REP1)[y])
                wm = v3_(wmod[0][:, :], KD)
                cs = v3(c_s, 2)[:, y, :].rearrange("p (k b) -> p k b", k=KD)
                for s in range(2):
                    for w in range(2):
                        for kh in range(KD):
                            o = 16 * s + 8 * w + B * kh
                            c0 = (3 * s + w) * D + kh * P
                            for k in range(KD):
                                last = pe.matmul(F[1][:, o:o + B], wm[:, k, c0:c0 + P], cs[:, k, :],
                                                 start=(k == 0), stop=(k == KD - 1))
                setup(last)
                rep = c_rep.rearrange("p (k b t) -> p k b t", k=KD, b=B)
                for s in range(2):
                    for h in range(2):
                        if s:
                            pe.wait_ge(set_dve, (SET_REP0, SET_REP1)[y] + 4 + 4 * (h + 1))
                        for b in range(2):
                            for k in range(KD):
                                last = pe.matmul(F[2 + h][:, b * D:(b + 1) * D], rep[:, k, 2 * h + b, :],
                                                 wm[:, k, (3 * s + 2) * D:(3 * s + 3) * D],
                                                 start=(k == 0), stop=(k == KD - 1))
                        setup(last)
                assert made[0] == (MOD_READ, MOD_READ + 5)[y]
            pe.wait_ge(set_dve, SET_ALL)
            pe.wait_ge(loaded["lin"], 16)

            def norm(g, blk):
                s = g % 2
                bank = A if s == 0 else F
                for r in range(B):
                    pe.wait_ge(*xn_made[g](blk, r))
                    for k in range(KD):
                        last = pe.transpose(bank[k][:, r * P:(r + 1) * P], v3(xn[s], B)[:, r, k * P:(k + 1) * P],
                                            ident[:, :])
                last.then_inc(xn_turned[g].sem, 1)
                pe.wait_ge(*hT_made[g](blk, B - 1))

            def over_d(dst, lhs, rhs, **kw):
                for k in range(KD):
                    last = pe.matmul(dst, lhs(k), rhs(k), start=(k == 0), stop=(k == KD - 1))
                return last

            def attn0(blk):
                wait_before(pe, x_done[3], blk, B - 1)
                norm(0, blk)
                h = hT[0]
                for r in range(B):
                    last = over_d(A[2][:, r * NH:(r + 1) * NH], lambda k: h[:, k, r * P:(r + 1) * P],
                                  lambda k: w_in[:, k, DIN - NH:DIN])
                last.then_inc(dt_raw.sem, 1)
                pe.wait_ge(*dA_made(blk))
                for n, m in enumerate((after, upto, ones)):
                    last = pe.matmul(A[2][:, (1 + n) * B * NH:(2 + n) * B * NH], m[:, :], dA[:, :],
                                     start=True, stop=True)
                last.then_inc(dec_raw.sem, 1)
                for m in range(XM):
                    if m == 3:
                        pe.wait_ge(*dec_made(blk))
                    if m >= 4:
                        pe.wait_ge(*xbc_in(blk, m - 4))
                    over_d(A[(m + 3) % 4][:, :], lambda k: w_in[:, k, DI + m * P:DI + (m + 1) * P],
                           lambda k: h[:, k, :]).then_inc(xbc_raw.sem, 1)
                pe.wait_ge(*xs_made(blk, XM - 1))
                for r in range(B):
                    t = slice(r * P, (r + 1) * P)
                    if r:
                        pe.wait_ge(*yg_made(blk, r - 1))
                        pe.wait_ge(*x_done[1](blk, r - 1))
                    for m in range(4):
                        pe.transpose(A[2][:, m * P:(m + 1) * P], xs[:, m, t], ident[:, :])
                    pe.transpose(A[3][:, 0:NS], xs[:, 4, t], ident[:, :])
                    pe.matmul(A[3][:, NS:2 * NS], xs[:, 4, t], xs[:, 5, t], start=True, stop=True
                              ).then_inc(xb_turned.sem, 1)
                    over_d(A[1][:, :], lambda k: h[:, k, t], lambda k: w_in[:, k, 0:DI]).then_inc(z_raw.sem, 1)
                    pe.wait_ge(*va_made(blk, r))
                    for k in range(2):
                        if k:
                            pe.wait_ge(*sz_made(blk, r))
                        pe.matmul(A[k][:, :], after[:, :], va[:, k * 512:(k + 1) * 512], start=True, stop=True
                                  ).then_inc(seg_raw.sem, 1)
                    pe.wait_ge(*seg_exp(blk, r))
                    wait_before(pe, state_made, blk, r)
                    pe.matmul(A[0][:, :], xs[:, 5, t], state[r][:, :], start=True, stop=True
                              ).then_inc(yoff_raw.sem, 1)
                    pe.wait_ge(*xdt_made(blk, r))
                    pe.matmul(A[1][:, :], bt[:, :], xdec[:, :], start=True, stop=True).then_inc(dst_raw.sem, 1)
                    pe.wait_ge(*mh_made(blk, r))
                    for q in range(NH):
                        last = pe.matmul(A[2][:, q * HD:(q + 1) * HD], v3(seg, NH)[:, q, :],
                                         xdt[:, q * HD:(q + 1) * HD], start=True, stop=True)
                    last.then_inc(ydiag_raw.sem, 1)
                    pe.wait_ge(*ygn_made(blk, r))
                    for m in range(4):
                        last = pe.transpose(A[0][:, m * P:(m + 1) * P], yg[:, m * P:(m + 1) * P], ident[:, :])
                    last.then_inc(yg_turned.sem, 1)
                    pe.wait_ge(*gT_made(blk, r))
                    o = A[3][:, 2 * NS:2 * NS + D]
                    for m in range(4):
                        pe.matmul(o, gT[:, m * P:(m + 1) * P], w_out[:, m, :], start=(m == 0), stop=False)
                    for k in range(KD):
                        last = pe.matmul(o[:, k * P:(k + 1) * P], h[:, k, t], ident[:, :], start=False,
                                         stop=(k == KD - 1))
                    last.then_inc(out0_raw.sem, 1)

            def attn1(blk):
                pe.wait_ge(*x_done[1](blk, B - 1))
                norm(2, blk)
                h = hT[0]
                wq = v3_(lin_w[:, W_QK:W_V], KD)
                wv = v3_(lin_w[:, W_V:W_G], KD)
                wg = v3_(lin_w[:, W_G:W_O], KD)
                wo = v3_(lin_w[:, W_O:W_LIN], KD)
                for r in range(B):
                    last = over_d(A[2][:, r * LH:(r + 1) * LH], lambda k: h[:, k, r * P:(r + 1) * P],
                                  lambda k: wg[:, k, :])
                last.then_inc(lg_raw.sem, 1)
                pe.wait_ge(*la_made(blk))
                for n, m in enumerate((upto, ones)):
                    last = pe.matmul(A[2][:, (1 + n) * 64:(2 + n) * 64], m[:, :], la[:, :], start=True, stop=True)
                last.then_inc(cs_raw.sem, 1)
                pe.wait_ge(*le_made(blk))
                for r in range(B):
                    t = slice(r * P, (r + 1) * P)
                    if r:
                        pe.wait_ge(*ly_made(blk, r - 1))
                        pe.wait_ge(*lst_made(blk, r - 1))
                    over_d(A[0][:, :], lambda k: h[:, k, t], lambda k: wq[:, k, :]).then_inc(qk_raw.sem, 1)
                    over_d(A[1][:, 0:D], lambda k: h[:, k, t], lambda k: wv[:, k, :]).then_inc(v_raw.sem, 1)
                    pe.wait_ge(*qs_made(blk, r))
                    for m in range(4):
                        last = pe.transpose(A[0][:, m * P:(m + 1) * P], qk[:, m * P:(m + 1) * P], ident[:, :])
                    last.then_inc(qk_turned.sem, 1)
                    pe.wait_ge(*qkT_made(blk, r))
                    pe.wait_ge(*qpar_made(blk, r))
                    pe.wait_ge(*v1_made(blk, r))
                    if r:
                        pe.wait_ge(*x_done[3](blk, r - 1))
                    for n in range(2):
                        for q in range(4):
                            last = pe.matmul(A[q][:, n * D:(n + 1) * D], qkT[32 * q:32 * q + 32, 2 + n, :],
                                             qpar[32 * q:32 * q + 32, n, :, :], start=True, stop=True)
                    last.then_inc(att_raw.sem, 1)
                    pe.wait_ge(*am_made(blk, r))
                    wait_before(pe, lst_made, blk, r)
                    for n in range(2):
                        o = n * LG * EXT
                        pe.matmul(A[0][:, o:o + LG * EXT], qkT[:, n, :], lst[r][:, n, :], start=(n == 0), stop=False,
                                  skip_group_check=True)
                    for n in range(2):
                        for q in range(4):
                            for j in range(2):
                                hd = LG * n + 2 * q + j
                                last = pe.matmul(A[0][:, hd * EXT:(hd + 1) * EXT],
                                                 am[q][:, n * D + j * P:n * D + (j + 1) * P],
                                                 v3(v1, LH)[:, hd, :], start=False, stop=(hd == LH - 1),
                                                 skip_group_check=True)
                    last.then_inc(ly_raw.sem, 1)
                    for n in range(2):
                        o = n * LG * EXT
                        last = pe.matmul(A[1][:, o:o + LG * EXT], qk[:, D + n * P:D + (n + 1) * P],
                                         v1[:, o:o + LG * EXT], start=True, stop=True)
                    last.then_inc(lst_raw.sem, 1)
                    pe.wait_ge(*ly_made(blk, r))
                    for m in range(2):
                        last = pe.transpose(A[2][:, m * P:(m + 1) * P], ly[:, m * P:(m + 1) * P], ident[:, :])
                    last.then_inc(ly_turned.sem, 1)
                    pe.wait_ge(*lyT_made(blk, r))
                    over_d(A[3][:, 0:D], lambda k: lyT[:, k * P:(k + 1) * P], lambda k: wo[:, k, :]
                           ).then_inc(out2_raw.sem, 1)

            def ffn(y, blk):
                g = 1 + 2 * y
                w = ffn_w[y]
                if y:
                    pe.wait_ge(*x_done[2](blk, B - 1))
                else:
                    wait_before(pe, x_done[4], blk, B - 1)
                norm(g, blk)
                h = hT[1]
                for r in range(B):
                    last = over_d(F[2][:, r * NE:(r + 1) * NE], lambda k: h[:, k, r * P:(r + 1) * P],
                                  lambda k: w[:, W_ROUT + k * NE:W_ROUT + (k + 1) * NE])
                last.then_inc(logit_raw[y].sem, 1)
                over_d(F[3][:, :], lambda k: w[:, W_DOWN + k * L:W_DOWN + (k + 1) * L],
                       lambda k: h[:, k, :]).then_inc(lh_raw[y].sem, 1)
                pe.wait_ge(*gl_made[y](blk))

                def hidden(j):
                    if j >= 2:
                        pe.wait_ge(*u_made[y](blk, j - 2))
                    c0 = W_S1 if j == 0 else W_E1 + (j - 1) * P
                    pe.matmul(F[j % 2][:, :], w[:, c0:c0 + P], gl[:, :], start=True, stop=True
                              ).then_inc(hid_raw[y].sem, 1)

                def expert_out(e):
                    js = [0] if e == 0 else [1 + FIRST[e - 1] + t for t in range(TILES[e - 1])]
                    if e >= 2:
                        pe.wait_ge(*fo_made[y](blk, e - 2))
                    if e == 0:
                        pe.wait_ge(*gatesT_made[y](blk))
                    pe.wait_ge(*u_made[y](blk, js[-1]))
                    for r in range(B):
                        t = slice(r * P, (r + 1) * P)
                        for n, j in enumerate(js):
                            c0 = W_S2 if j == 0 else W_E2 + (j - 1) * L
                            last = pe.matmul(F[2 + e % 2][:, t], u[j % RING][:, t], w[:, c0:c0 + L],
                                             start=(n == 0), stop=(n == len(js) - 1 and e > 0))
                        if e == 0:
                            last = pe.matmul(F[2][:, t], gatesT[:, t], cw[y][:, :], start=False, stop=True)
                    last.then_inc(exp_raw[y].sem, 1)

                hidden(0)
                hidden(1)
                pe.wait_ge(*gates_made[y](blk))
                for r in range(B):
                    last = pe.transpose(F[2][0:GC, r * P:(r + 1) * P], gates[:, r, :], ident[:, :])
                last.then_inc(gates_turned[y].sem, 1)
                for e in range(NE + 1):
                    if e < NE:
                        for t in range(TILES[e]):
                            if 1 + FIRST[e] + t >= 2:
                                hidden(1 + FIRST[e] + t)
                    expert_out(e)
                pe.wait_ge(*fo_made[y](blk, NE))
                pe.wait_ge(*u_made[y](blk, NT))
                for r in range(B):
                    last = pe.transpose(F[0][:, r * P:(r + 1) * P], fo[:, r * P:(r + 1) * P], ident[:, :])
                last.then_inc(fo_turned[y].sem, 1)
                pe.wait_ge(*foT_made[y](blk))
                pe.wait_ge(*gh_made[y](blk))
                for n in range(2):
                    for b in range(2):
                        r = 2 * n + b
                        t = slice(r * P, (r + 1) * P)
                        o = F[2 + n][:, b * D:(b + 1) * D]
                        pe.matmul(o, foT[:, t], w[:, W_UP:W_UP + D], start=True, stop=False)
                        for k in range(KD):
                            last = pe.matmul(o, ghT[:, k, t], w[:, W_CORE + k * D:W_CORE + (k + 1) * D],
                                             start=False, stop=(k == KD - 1))
                    last.then_inc(outf_raw[y].sem, 1)

            walk(pe, attn0, ffn, attn1)


def v3_(ap, a):
    return ap.rearrange("p (a b) -> p a b", a=a)


def reader(j):
    return 0 if j == 0 else 1 + max(e for e in range(NE) if FIRST[e] <= j - 1)


NSMALL = 9
SET_C = 2
SET_SEL0 = SET_C + 1 + 2 + 1 + 1 + DI // P + 2 + NE + 2
SET_SEL1 = SET_SEL0 + 1 + NE + 2
SET_CW = SET_SEL1 + 1
SET_REP0 = SET_CW + 1
SET_REP1 = SET_REP0 + 4 + 16 + 1
SET_GATES = SET_REP1 + 4 + 16
SET_ALL = SET_GATES
CONST_READ0, CONST_DONE0 = 1, 2
CONST_DONE1 = 4
MODC0 = CONST_DONE1 + 1
MOD_READ = MODC0 + 4
MODC1 = MOD_READ + 1


def kernel(**inputs):
    import concourse.bacc as bacc
    from concourse.bass_utils import run_bass_kernel_spmd as run

    f = {k: np.ascontiguousarray(v) for k, v in inputs.items()}

    def halves(w):
        return w.reshape(w.shape[0] // P, P, w.shape[1]).transpose(1, 0, 2).reshape(P, -1)

    def over_p(*vecs):
        row = np.concatenate([v.reshape(1, -1) for v in vecs], 1)
        return np.ascontiguousarray(np.broadcast_to(row, (P, row.shape[1])))

    arrays = {"x": f["L0_attn_x"]}
    arrays["w_in"] = halves(f["L0_attn_w_in"]).reshape(P, KD, DIN)
    arrays["w_out"] = halves(f["L0_attn_w_out"]).reshape(P, DI // P, D)
    conv_w = f["L0_attn_conv_w"].reshape(XM, P, CONV).transpose(1, 0, 2).reshape(P, XM * CONV)
    arrays["mam_c"] = np.concatenate([conv_w, f["L0_attn_conv_b"].reshape(XM, P).T,
                                      f["L0_attn_norm_w"].reshape(DI // P, P).T], 1)
    cost = np.array([2 * L * h for h in HID], np.float32) * np.float32(COST_LAMBDA)
    arrays["rows"] = over_p(f["L0_attn_dt_bias"], f["L0_attn_A_log"], f["L0_attn_D"], f["L1_attn_bg"],
                            f["L0_ffn_router_b"], f["L1_ffn_router_b"], cost)
    arrays["c_t"] = np.concatenate([f[f"L{y}_c"].reshape(B, KD, P).transpose(2, 1, 0).reshape(P, -1)
                                    for y in range(2)], 1)
    for y in range(2):
        g = {k[len(f"L{y}_ffn_"):]: v for k, v in f.items() if k.startswith(f"L{y}_ffn_")}
        arrays[f"ffn_w{y}"] = np.concatenate(
            [halves(g["down_w"]), g["up_w"], halves(g["core_w"]), halves(g["router_w"]), g["shared_w1"],
             g["shared_w2"]] + [g[f"e{e}_w1"] for e in range(NE)] + [halves(g[f"e{e}_w2"]) for e in range(NE)], 1)
        arrays[f"ffn_c{y}"] = np.concatenate(
            [g["down_b"].reshape(P, 1), g["shared_b1"].reshape(P, 1)]
            + [g[f"e{e}_b1"].reshape(-1, P).T for e in range(NE)], 1)
        arrays[f"b2rows{y}"] = np.stack([g[f"e{e}_b2"] for e in range(NE)] + [g["shared_b2"]], 0)
        arrays[f"wmod{y}"] = halves(f[f"L{y}_wmod"])
    arrays["ub"] = over_p(f["L0_ffn_up_b"], f["L1_attn_bo"], f["L1_ffn_up_b"])
    arrays["ub2"] = over_p(f["L0_ffn_core_b"], np.zeros(D, np.float32), f["L1_ffn_core_b"])
    arrays["lin_w"] = np.concatenate([halves(np.concatenate([f["L1_attn_Wq"], f["L1_attn_Wk"]], 1)),
                                      halves(f["L1_attn_Wv"]), halves(f["L1_attn_Wg"]),
                                      halves(f["L1_attn_Wo"])], 1)
    half = LD // 2
    inv = (1.0 / np.float32(10000.0) ** (np.arange(half, dtype=np.float32) / np.float32(half))).astype(np.float32)
    ang = np.arange(T, dtype=np.float32)[:, None] * inv[None, :]
    arrays["rope"] = np.concatenate([np.cos(ang), np.sin(ang)], 1).astype(np.float32)

    nc = bacc.Bacc("TRN2", target_bir_lowering=False, num_devices=1)
    dram = {}
    arrays = {k: np.ascontiguousarray(v) for k, v in arrays.items()}
    for k, v in arrays.items():
        dram[k] = nc.dram_tensor(f"in_{k}", list(v.shape), F32, kind="ExternalInput").ap()
    out = nc.dram_tensor("out", [B, T, D], F32, kind="ExternalOutput").ap()
    program(nc, dram, out)
    r = run(nc, [{f"in_{k}": v for k, v in arrays.items()}], core_ids=[0])
    return r.results[0]["out"]
```

```python
from contextlib import ExitStack

import numpy as np

import concourse.bass as bass
from concourse import mybir

F32 = mybir.dt.float32
U32 = mybir.dt.uint32
I32 = mybir.dt.int32
ALU = mybir.AluOpType
ACT = mybir.ActivationFunctionType
AX_X = mybir.AxisListType.X

P = 128
B = 4
T = 1024
D = 256
KD = D // P
NBLK = T // P
DI = 512
NS = 128
NH = 8
HD = DI // NH
CONV = 4
XM = (DI + 2 * NS) // P
DIN = 2 * DI + 2 * NS + NH
LH = 16
LD = D // LH
LG = P // LD
EXT = LD + 1
HID = [128, 256, 384, 512, 128, 256, 384, 512]
NE = len(HID)
L = 128
TILES = [h // P for h in HID]
FIRST = [sum(TILES[:e]) for e in range(NE)]
NT = sum(TILES)
GC = NE + 1
COST_LAMBDA = 1e-07
RING = 8
SHARED = -1
GROUPS = [[SHARED, 0, 1], [3], [2, 4], [7], [5, 6]]
UNITS = [e for grp in GROUPS for e in grp]
UNIT_TILES = [1 if e == SHARED else TILES[e] for e in UNITS]
UNIT_FIRST = [sum(UNIT_TILES[:n]) for n in range(len(UNITS))]

W_DOWN = 0
W_UP = W_DOWN + KD * L
W_CORE = W_UP + D
W_ROUT = W_CORE + KD * D
W_S1 = W_ROUT + KD * NE
W_S2 = W_S1 + L
W_E1 = W_S2 + L
W_E2 = W_E1 + NT * P
W_FFN = W_E2 + NT * L
C_DOWN, C_S1, C_B1 = 0, 1, 2
C_FFN = 2 + NT
C_CW, C_CB, C_NW = 0, XM * CONV, XM * CONV + XM
C_MAM = C_NW + DI // P
R_DT, R_AL, R_D, R_BG, R_RB, R_COST = 0, 8, 16, 24, 40, 56
R_ALL = 64
W_QK = 0
W_V = W_QK + KD * 2 * D
W_G = W_V + KD * D
W_O = W_G + KD * LH
W_LIN = W_O + KD * D


class Signal:

    def __init__(self, ctx, nc, name, per_block):
        self.sem, self.n = ctx.enter_context(nc.semaphore(name)), per_block

    def __call__(self, blk, k=0):
        return self.sem, blk * self.n + (k + 1)

    def last(self, blk):
        return self.sem, blk * self.n + self.n


def wait_before(eng, sig, blk, k):
    if isinstance(blk, int) and blk == 0:
        return
    eng.wait_ge(sig.sem, blk * sig.n + (k + 1 - sig.n))


class Chain:

    def __init__(self, ctx, nc, name, per_block):
        self.sem, self.n, self.k = ctx.enter_context(nc.semaphore(name)), per_block, 0

    def step(self, eng, blk, ins):
        self.k += 1
        ins.then_inc(self.sem, 1)
        eng.wait_ge(self.sem, blk * self.n + self.k)

    def close(self):
        assert self.k == self.n, (self.sem, self.k)
        self.k = 0


def program(nc, dram, out):
    ctx = ExitStack()
    with ctx:
        def sb(name, *shape, dt=F32):
            return ctx.enter_context(nc.sbuf_tensor(name, [shape[0], int(np.prod(shape[1:]))], dt))

        def v3(t, a):
            return t[:, :].rearrange("p (a b) -> p a b", a=a)

        def v4(t, a, b):
            return t[:, :].rearrange("p (a b c) -> p a b c", a=a, b=b)

        def signal(name, n):
            return Signal(ctx, nc, name, n)

        w_in = v3(sb("w_in", P, KD, DIN), KD)
        w_out = v3(sb("w_out", P, DI // P, D), DI // P)
        ffn_w = [sb(f"ffn_w{y}", P, W_FFN) for y in range(2)]
        lin_w = sb("lin_w", P, W_LIN)
        mam_c = sb("mam_c", P, C_MAM)
        ffn_c = [sb(f"ffn_c{y}", P, C_FFN) for y in range(2)]
        rows = sb("rows", P, R_ALL)
        a_neg = sb("a_neg", P, NH)
        router_bias = [sb(f"router_bias{y}", P, NE) for y in range(2)]
        ident = sb("ident", P, P)
        upto = sb("upto", P, P)
        after = sb("after", P, P)
        ones = sb("ones", P, P)
        block8 = sb("block8", P, LG)
        parity = sb("parity", P, 2)
        iota8 = sb("iota8", P, NE)
        eps_ln = sb("eps_ln", P, 1)
        spare = sb("spare", P, 1)
        mod_c = [v4(sb(f"mod_c{g}", P, 2, KD, B), 2, KD) for g in range(4)]
        gate_bc = [sb(f"gate_bc{g}", P, B * D) for g in range(4)]
        out_bias = v3(sb("out_bias", P, 3 * D), 3)
        cw = [sb(f"cw{y}", GC, L) for y in range(2)]

        x_of = [sb(f"x{g}", P, B * D) for g in range(4)]
        x_in_of = [x_of[0], x_of[0], x_of[1], x_of[2]]

        stats = [sb(f"stats{s}", P, B, 6) for s in range(2)]
        mv = [sb(f"mv{s}", P, B, 2) for s in range(2)]
        var_e = [sb(f"var_e{s}", P, B) for s in range(2)]
        rstd = [sb(f"rstd{s}", P, B) for s in range(2)]
        rtmp = [sb(f"rtmp{s}", P, B) for s in range(2)]
        area_v = sb("area_v", P, 2 * B * (P + CONV - 1))
        area_s = sb("area_s", P, NH * P)
        u_ring = sb("u_ring", P, RING * B * P)
        xn = [area_v[:, 0:B * D], u_ring[:, 0:B * D]]
        hT = [v3(sb(f"hT{s}", P, KD, B * P), KD) for s in range(2)]

        raw = v4(area_v, 2, B)
        tails = v4(sb("tails", P, XM, B, CONV - 1), XM, B)
        acc = v3(area_s, 2)
        xs_all = sb("xs", P, XM, B * P)
        xs = v3(xs_all, XM)
        tz = sb("tz", P, DI)
        sz = sb("sz", P, DI)
        dt_v = sb("dt_v", P, B * NH)
        dt_n = sb("dt_n", P, B * NH)
        dt_s = sb("dt_s", P, B * NH)
        dA = sb("dA", P, B * NH)
        dec = sb("dec", P, 3, B * NH)
        dtd = sb("dtd", P, B * NH)
        va = area_v[:, 0:NH * P]
        seg = area_s
        cbm = sb("cbm", P, P)
        xt = sb("xt", P, DI)
        bt = sb("bt", P, NS)
        xd = sb("xd", P, DI)
        th = sb("th", P, 2, DI)
        xdt, xdec = th[:, 0:DI], th[:, DI:2 * DI]
        yg = sb("yg", P, DI)
        yst = sb("yst", P, 4)
        gT = sb("gT", P, DI)
        state = [sb(f"state{r}", P, DI) for r in range(B)]
        res_a = sb("res_a", P, D)

        rope = v3(sb("rope", P, 2, LD // 2), 2)
        lg = sb("lg", P, B * LH)
        la = sb("la", P, B * LH)
        le = v4(sb("le", P, 3, B, LH), 3, B)
        qk, qr1, qr2, qm = xs_all[:, 0:512], xs_all[:, 512:1024], xs_all[:, 1024:1536], xs_all[:, 1536:2048]
        qkT = v3_(xs_all[:, 2048:2560], 4)
        qpar = xs_all[:, 2560:3072].rearrange("p (a b c) -> p a b c", a=2, b=2)
        v1 = sb("v1", P, LH * EXT)
        am = [area_v[:, 0:512], area_v[:, 512:1024], area_s[:, 0:512], area_s[:, 512:1024]]
        lst = [v3(sb(f"lst{r}", P, 2, LG * EXT), 2) for r in range(B)]
        ltm = sb("ltm", P, 2 * LG * EXT)
        lbt = sb("lbt", P, 2 * LG)
        lden = sb("lden", P, LH)
        ly, lyT = yg[:, 0:D], gT[:, 0:D]

        rt = [sb(f"rt{k}", P, B * NE) for k in range(3)]
        rm = [sb(f"rm{k}", P, B) for k in range(4)]
        p8 = v3(sb("p8", P, B, 8), B)
        i8 = v3(sb("i8", P, B, 8, dt=U32), B)
        i8f = v3(sb("i8f", P, B, 2), B)
        g2 = v3(sb("g2", P, B, 2), B)
        gates = v3(sb("gates", P, B, GC), B)
        gatesT = sb("gatesT", GC, B * P)
        gh = sb("gh", P, KD, B * P)
        ghT = v3(gh, KD)
        gl = sb("gl", P, B * P)
        u = [u_ring[:, k * B * P:(k + 1) * B * P] for k in range(RING)]
        fo = sb("fo", P, B * L)
        foT, res_f = gl, (u[2], u[3])

        A = [ctx.enter_context(nc.psum_tensor(f"A{k}", [P, 512], F32)) for k in range(4)]
        F = [ctx.enter_context(nc.psum_tensor(f"F{k}", [P, 512], F32)) for k in range(4)]

        wmod = [xs_all]
        c_t = sb("c_t", P, 2, KD * B)
        c_s = sb("c_s", P, 2, KD * B)
        c_rep = area_v[:, 0:KD * B * P]
        gb1 = sb("gb1", P, NT)
        gsel = v3(sb("gsel", P, NT, GC), NT)
        b2rows = [sb(f"b2rows{y}", GC, L) for y in range(2)]
        b2sel = sb("b2sel", GC, GC)
        ub2 = area_s[:, 0:3 * D]

        def one(name):
            return ctx.enter_context(nc.semaphore(name))

        loaded = {k: one(f"loaded_{k}") for k in
                  ("w_in", "w_out", "lin", "ffn0", "ffn1", "small", "mod0", "mod1")}
        masks_made = one("masks_made")
        pool_chain = one("pool_chain")
        set_dve = one("set_dve")
        set_act = one("set_act")
        set_pe = one("set_pe")
        set_done = one("set_done")

        x_in = signal("x_in", 16)
        x_out = signal("x_out", 16)
        rope_in = signal("rope_in", 16)
        x_done = [None] + [signal(f"x{g}_done", B) for g in (1, 2, 3, 4)]
        copied = [None] + [signal(f"x{g}_copied", B) for g in (1, 2, 3)]
        xn_made = [signal(f"xn{g}_made", B) for g in range(4)]
        xn_turned = [signal(f"xn{g}_turned", 1) for g in range(4)]
        hT_made = [signal(f"hT{g}_made", B) for g in range(4)]
        dve_a0 = Chain(ctx, nc, "dve_a0", 121)
        dt_exp = signal("dt_exp", 1)
        dt_raw = signal("dt_raw", 1)
        dt_abs = signal("dt_abs", 1)
        dt_ln = signal("dt_ln", 1)
        dA_made = signal("dA_made", 1)
        dec_raw = signal("dec_raw", 1)
        dec_made = signal("dec_made", 1)
        dtd_made = signal("dtd_made", 1)
        tail_put = signal("tail_put", XM)
        tail_kept = signal("tail_kept", XM)
        xbc_raw = signal("xbc_raw", XM)
        xbc_in = signal("xbc_in", XM)
        conv_made = signal("conv_made", XM)
        conv_tanh = signal("conv_tanh", XM)
        xs_made = signal("xs_made", XM)
        z_raw = signal("z_raw", B)
        z_tanh = signal("z_tanh", B)
        sz_made = signal("sz_made", B)
        xb_turned = signal("xb_turned", B)
        xt_made = signal("xt_made", B)
        va_made = signal("va_made", B)
        seg_raw = signal("seg_raw", 2 * B)
        seg_exp = signal("seg_exp", B)
        mh_made = signal("mh_made", B)
        xdt_made = signal("xdt_made", B)
        xd_made = signal("xd_made", B)
        yoff_raw = signal("yoff_raw", B)
        dst_raw = signal("dst_raw", B)
        ydiag_raw = signal("ydiag_raw", B)
        state_made = signal("state_made", B)
        yg_made = signal("yg_made", B)
        ysum_made = signal("ysum_made", B)
        ygn_made = signal("ygn_made", B)
        yg_turned = signal("yg_turned", B)
        gT_made = signal("gT_made", B)
        out0_raw = signal("out0_raw", B)
        dve_a1 = Chain(ctx, nc, "dve_a1", 51)
        lg_raw = signal("lg_raw", 1)
        lg_v = signal("lg_v", 1)
        lg_e = signal("lg_e", 1)
        lg_b = signal("lg_b", 1)
        la_made = signal("la_made", 1)
        cs_raw = signal("cs_raw", 1)
        le_made = signal("le_made", 1)
        qk_raw = signal("qk_raw", B)
        v_raw = signal("v_raw", B)
        v1_made = signal("v1_made", B)
        qneg_made = signal("qneg_made", B)
        qexp_made = signal("qexp_made", B)
        qs_made = signal("qs_made", B)
        qk_turned = signal("qk_turned", B)
        qkT_made = signal("qkT_made", B)
        qpar_made = signal("qpar_made", B)
        att_raw = signal("att_raw", B)
        am_made = signal("am_made", B)
        ly_raw = signal("ly_raw", B)
        lst_raw = signal("lst_raw", B)
        lst_made = signal("lst_made", B)
        ly_made = signal("ly_made", B)
        ly_turned = signal("ly_turned", B)
        lyT_made = signal("lyT_made", B)
        out2_raw = signal("out2_raw", B)
        dve_f = [Chain(ctx, nc, f"dve_f{y}", 30) for y in range(2)]
        logit_raw = [signal(f"logit_raw{y}", 1) for y in range(2)]
        rt_max = [signal(f"rt_max{y}", 1) for y in range(2)]
        rt_exp = [signal(f"rt_exp{y}", 1) for y in range(2)]
        top_diff = [signal(f"top_diff{y}", 1) for y in range(2)]
        top_tanh = [signal(f"top_tanh{y}", 1) for y in range(2)]
        gates_made = [signal(f"gates_made{y}", 1) for y in range(2)]
        gates_turned = [signal(f"gates_turned{y}", 1) for y in range(2)]
        gatesT_made = [signal(f"gatesT_made{y}", 1) for y in range(2)]
        lh_raw = [signal(f"lh_raw{y}", 1) for y in range(2)]
        gl_made = [signal(f"gl_made{y}", 1) for y in range(2)]
        gh_made = [signal(f"gh_made{y}", 1) for y in range(2)]
        hid_raw = [signal(f"hid_raw{y}", NT + 1) for y in range(2)]
        u_made = [signal(f"u_made{y}", NT + 1) for y in range(2)]
        exp_raw = [signal(f"exp_raw{y}", NE + 1) for y in range(2)]
        fo_made = [signal(f"fo_made{y}", NE + 1) for y in range(2)]
        fo_turned = [signal(f"fo_turned{y}", 1) for y in range(2)]
        foT_made = [signal(f"foT_made{y}", 1) for y in range(2)]
        outf_raw = [signal(f"outf_raw{y}", 2) for y in range(2)]
        res_made = [signal(f"res_made{g}", 1) for g in range(4)]

        def bc(ap, *shape):
            return ap.to_broadcast(list(shape))

        def alone(stage):
            for _ in stage:
                pass

        def beside(attn, ffn, ahead):
            for count in ahead:
                for _ in range(count):
                    next(ffn)
                next(attn)
            assert next(attn, None) is None
            alone(ffn)

        def walk(eng, attn0, ffn, attn1):
            alone(attn0(0))
            beside(attn0(1), ffn(0, 0), AHEAD0)
            alone(attn1(0))
            with eng.Fori(1, NBLK - 1) as i:
                beside(attn0(i + 1), ffn(0, i), AHEAD0)
                beside(attn1(i), ffn(1, i - 1), AHEAD1)
            alone(ffn(0, NBLK - 1))
            beside(attn1(NBLK - 1), ffn(1, NBLK - 2), AHEAD1)
            alone(ffn(1, NBLK - 1))

        block = ctx.enter_context(nc.Block())

        @block.sync
        def _(sp):
            sp.dma_start(c_t[:, :], dram["c_t"]).then_inc(loaded["small"], 16)
            sp.dma_start(mam_c[:, :], dram["mam_c"]).then_inc(loaded["small"], 16)
            sp.dma_start(rows[:, :], dram["rows"]).then_inc(loaded["small"], 16)
            for y in range(2):
                sp.dma_start(ffn_c[y][:, :], dram[f"ffn_c{y}"]).then_inc(loaded["small"], 16)
                sp.dma_start(b2rows[y][:, :], dram[f"b2rows{y}"]).then_inc(loaded["small"], 16)
            sp.dma_start(out_bias, dram["ub"]).then_inc(loaded["small"], 16)
            sp.dma_start(ub2, dram["ub2"]).then_inc(loaded["small"], 16)
            sp.dma_start(wmod[0][:, :], dram["wmod0"]).then_inc(loaded["mod0"], 16)
            sp.dma_start(w_in, dram["w_in"]).then_inc(loaded["w_in"], 16)
            sp.dma_start(w_out, dram["w_out"]).then_inc(loaded["w_out"], 16)
            sp.dma_start(ffn_w[0][:, :], dram["ffn_w0"]).then_inc(loaded["ffn0"], 16)
            sp.dma_start(lin_w[:, :], dram["lin_w"]).then_inc(loaded["lin"], 16)
            sp.dma_start(ffn_w[1][:, :], dram["ffn_w1"]).then_inc(loaded["ffn1"], 16)
            sp.wait_ge(set_pe, MOD_READ)
            sp.dma_start(wmod[0][:, :], dram["wmod1"]).then_inc(loaded["mod1"], 16)

            def load_x(blk):
                wait_before(sp, copied[1], blk, B - 1)
                wait_before(sp, xn_made[1], blk, B - 1)
                sp.dma_start(v3(x_of[0], B), dram["x"][:, bass.ts(blk, P), :].rearrange("b t d -> t b d")
                             ).then_inc(x_in.sem, 16)

            def load_rope(blk):
                wait_before(sp, qs_made, blk, B - 1)
                sp.dma_start(rope, dram["rope"][bass.ts(blk, P), :].rearrange("t (a b) -> t a b", a=2)
                             ).then_inc(rope_in.sem, 16)

            def store(blk):
                sp.wait_ge(*x_done[4](blk, B - 1))
                sp.dma_start(out[:, bass.ts(blk, P), :].rearrange("b t d -> t b d"), v3(x_of[3], B)
                             ).then_inc(x_out.sem, 16)

            sp.sem_inc(x_out.sem, 16)
            for blk in (0, 1):
                load_x(blk)
                load_rope(blk)
            with sp.Fori(1, NBLK - 1) as i:
                load_x(i + 1)
                load_rope(i + 1)
                store(i - 1)
            store(NBLK - 2)
            store(NBLK - 1)
            sp.wait_ge(x_out.sem, 16 * NBLK + 16)

        @block.gpsimd
        def _(pool):
            made = [0]

            def mask(t, rows_, cols, base, mult, pattern, op, fill, view=None):
                pool.affine_select(out=t, in_=t, compare_op=op, fill=fill, base=base,
                                   pattern=pattern, channel_multiplier=mult).then_inc(pool_chain, 1)
                made[0] += 1
                pool.wait_ge(pool_chain, made[0])

            def clear(t, value=0.0):
                pool.memset(t, value).then_inc(pool_chain, 1)
                made[0] += 1

            clear(ident[:, :])
            clear(upto[:, :], 1.0)
            clear(after[:, :], 1.0)
            clear(ones[:, :], 1.0)
            clear(block8[:, :], 1.0)
            clear(parity[:, :], 0.0)
            clear(eps_ln[:, :], 1e-05)
            clear(tails[:, :, :, :])
            for r in range(B):
                clear(state[r][:, :])
                clear(lst[r])
            clear(gates)
            clear(v1[:, :], 1.0)
            clear(gsel)
            clear(b2sel[:, :])
            for e in range(NE):
                clear(iota8[:, e:e + 1], float(e))
            pool.wait_ge(pool_chain, made[0])
            mask(ident[:, :], P, P, 0, 1, [[-1, P]], ALU.not_equal, 1.0)
            mask(upto[:, :], P, P, 0, -1, [[1, P]], ALU.is_ge, 0.0)
            mask(after[:, :], P, P, 0, 1, [[-1, P]], ALU.is_gt, 0.0)
            mask(block8[:, :], P, LG, 0, 1, [[-LD, LG]], ALU.is_ge, 0.0)
            mask(block8[:, :], P, LG, LD - 1, -1, [[LD, LG]], ALU.is_ge, 0.0)
            clear(gates[:, :, NE:GC], 1.0)
            clear(b2sel[:, NE:GC], 1.0)
            pool.wait_ge(pool_chain, made[0])
            mask(b2sel[:, NE:GC], GC, 1, -NE, 1, [[0, 1]], ALU.not_equal, 0.1)
            pool.memset(th[:, 0:1], 0.0).then_inc(masks_made, 1)
            pool.wait_ge(masks_made, 1)
            pool.wait_ge(loaded["small"], 16 * NSMALL)
            pool.tensor_tensor(out_bias, out_bias, v3(ub2, 3), ALU.add).then_inc(set_done, 1)
            pool.wait_ge(set_done, 1)

            def put_tail(blk, m):
                if m >= 2:
                    pool.wait_ge(*conv_made(blk, m - 2))
                else:
                    pool.wait_ge(*hT_made[0](blk, B - 1))
                wait_before(pool, tail_kept, blk, m)
                pool.tensor_tensor(raw[:, m % 2, :, 0:CONV - 1], tails[:, m, :, :], unit, ALU.mult
                                   ).then_inc(tail_put.sem, 1)

            def keep_tail(blk, m):
                pool.wait_ge(*tail_put(blk, m))
                pool.wait_ge(*xbc_in(blk, m))
                pool.tensor_tensor(tails[:, m, :, :], raw[:, m % 2, :, P:P + CONV - 1], unit, ALU.mult
                                   ).then_inc(tail_kept.sem, 1)

            unit = v3_(ones[:, 0:B * (CONV - 1)], B)

            def attn0(blk):
                yield
                yield
                for m in range(XM):
                    put_tail(blk, m)
                    keep_tail(blk, m)
                    yield
                yield
                pool.wait_ge(*dtd_made(blk))
                pool.wait_ge(*xs_made(blk, XM - 1))
                for r in range(B):
                    h = slice(r * NH, (r + 1) * NH)
                    pool.wait_ge(*xt_made(blk, r))
                    if r:
                        pool.wait_ge(*dst_raw(blk, r - 1))
                        pool.wait_ge(*yg_made(blk, r - 1))
                    pool.tensor_tensor(v3(xdec, NH), v3(xt, NH), bc(dtd[:, h].unsqueeze(2), P, NH, HD),
                                       ALU.mult).then_inc(xdt_made.sem, 1)
                    pool.tensor_tensor(v3(xd, NH), v3(xt, NH),
                                       bc(rows[:, R_D:R_D + NH].unsqueeze(2), P, NH, HD),
                                       ALU.mult).then_inc(xd_made.sem, 1)
                    for _ in range(ROW_SLOTS):
                        yield

            def copy_with_bias(g, blk):
                pool.wait_ge(*x_done[g](blk, B - 1))
                if g < 3:
                    wait_before(pool, copied[g + 1], blk, B - 1)
                    wait_before(pool, xn_made[g + 1], blk, B - 1)
                else:
                    pool.wait_ge(x_out.sem, blk * 16 + 16)
                pool.tensor_tensor(v3(x_of[g], B), v3(gate_bc[g], B), bc(out_bias[:, g - 1:g, :], P, B, D),
                                   ALU.mult).then_inc(copied[g].sem, B // 2)
                pool.wait_ge(*copied[g](blk, B // 2 - 1))
                pool.tensor_tensor(x_of[g][:, :], x_of[g][:, :], x_in_of[g][:, :], ALU.add
                                   ).then_inc(copied[g].sem, B // 2)

            def attn1(blk):
                copy_with_bias(2, blk)
                for _ in range(len(AHEAD1)):
                    yield

            def ffn(y, blk):
                copy_with_bias(1 + 2 * y, blk)
                for _ in range(FFN_SLOTS):
                    yield

            walk(pool, attn0, ffn, attn1)

        @block.scalar
        def _(act):
            act.wait_ge(loaded["small"], 16 * NSMALL)
            act.activation(c_s[:, :], c_t[:, :], ACT.Tanh, scale=0.5).then_inc(set_act, 1)
            act.activation(a_neg[:, :], rows[:, R_AL:R_AL + NH], ACT.Exp).then_inc(set_act, 1)
            act.activation(gb1[:, :], ffn_c[0][:, C_B1:C_B1 + NT], ACT.Gelu).then_inc(set_act, 1)
            act.wait_ge(set_dve, SET_SEL0)
            act.activation(gb1[:, :], ffn_c[1][:, C_B1:C_B1 + NT], ACT.Gelu).then_inc(set_act, 1)
            act.wait_ge(set_dve, SET_ALL)
            act.wait_ge(masks_made, 1)

            def norm(g, blk):
                s = g % 2
                bank = A if s == 0 else F
                act.wait_ge(*xn_turned[g](blk))
                for r in range(B):
                    for k in range(KD):
                        last = act.activation(hT[s][:, k, r * P:(r + 1) * P], bank[k][:, r * P:(r + 1) * P],
                                              ACT.Identity, scale=mod_c[g][:, 1, k, r:r + 1],
                                              bias=mod_c[g][:, 0, k, r:r + 1])
                    last.then_inc(hT_made[g].sem, 1)

            def attn0(blk):
                norm(0, blk)
                yield
                act.wait_ge(*dt_abs(blk))
                act.activation(dt_n[:, :], dt_n[:, :], ACT.Exp).then_inc(dt_exp.sem, 1)
                act.wait_ge(*dt_exp(blk))
                act.activation(dt_n[:, :], dt_n[:, :], ACT.Ln, bias=1.0).then_inc(dt_ln.sem, 1)
                yield
                act.wait_ge(*dec_raw(blk))
                act.activation(dec[:, :], A[2][:, B * NH:4 * B * NH], ACT.Exp).then_inc(dec_made.sem, 1)

                def conv_tanh_of(m):
                    act.wait_ge(*conv_made(blk, m))
                    if m >= 2:
                        act.wait_ge(*xs_made(blk, m - 2))
                    act.activation(v3(th, 2)[:, m % 2, :], acc[:, m % 2, :], ACT.Tanh).then_inc(conv_tanh.sem, 1)

                for m in range(XM):
                    act.wait_ge(*xbc_raw(blk, m))
                    if m >= 2:
                        act.wait_ge(*conv_made(blk, m - 2))
                        act.wait_ge(*tail_kept(blk, m - 2))
                    act.activation(raw[:, m % 2, :, CONV - 1:], v3(A[(m + 3) % 4], B), ACT.Copy
                                   ).then_inc(xbc_in.sem, 1)
                    if m:
                        conv_tanh_of(m - 1)
                    yield
                conv_tanh_of(XM - 1)
                yield
                for r in range(B):
                    act.wait_ge(*xb_turned(blk, r))
                    if r:
                        act.wait_ge(*xd_made(blk, r - 1))
                    act.activation(xt[:, :], A[2][:, :], ACT.Copy)
                    act.activation(bt[:, :], A[3][:, 0:NS], ACT.Copy).then_inc(xt_made.sem, 1)
                    act.wait_ge(*z_raw(blk, r))
                    act.activation(tz[:, :], A[1][:, :], ACT.Tanh).then_inc(z_tanh.sem, 1)
                    yield
                    act.wait_ge(*seg_raw(blk, 2 * r))
                    act.activation(seg[:, 0:512], A[0][:, :], ACT.Exp)
                    act.wait_ge(*seg_raw(blk, 2 * r + 1))
                    act.activation(seg[:, 512:1024], A[1][:, :], ACT.Exp).then_inc(seg_exp.sem, 1)
                    yield
                    yield
                    act.wait_ge(*yg_made(blk, r))
                    act.activation(gT[:, :], yg[:, :], ACT.Square, accum_out=yst[:, 0:1]
                                   ).then_inc(ysum_made.sem, 1)
                    yield
                    act.wait_ge(*yg_turned(blk, r))
                    act.activation(gT[:, :], A[0][:, :], ACT.Copy).then_inc(gT_made.sem, 1)
                    yield
                    yield

            def attn1(blk):
                norm(2, blk)
                yield
                act.wait_ge(*lg_v(blk))
                act.activation(lg[:, :], lg[:, :], ACT.Exp, scale=-1.0).then_inc(lg_e.sem, 1)
                act.wait_ge(*lg_b(blk))
                act.activation(la[:, :], la[:, :], ACT.Ln).then_inc(la_made.sem, 1)
                yield
                act.wait_ge(*cs_raw(blk))
                act.activation(le[:, 0, :, :], v3_(A[2][:, 64:128], B), ACT.Exp)
                act.activation(le[:, 1, :, :], v3_(A[2][:, 64:128], B), ACT.Exp, scale=-1.0)
                act.activation(le[:, 2, :, :], v3_(A[2][:, 128:192], B), ACT.Exp).then_inc(le_made.sem, 1)
                yield
                for r in range(B):
                    act.wait_ge(*v_raw(blk, r))
                    if r:
                        act.wait_ge(*ly_raw(blk, r - 1))
                        act.wait_ge(*lst_raw(blk, r - 1))
                    act.activation(v3(v1, LH)[:, :, 0:LD], v3_(A[1][:, 0:D], LH), ACT.Copy
                                   ).then_inc(v1_made.sem, 1)
                    act.wait_ge(*qneg_made(blk, r))
                    act.activation(qm[:, :], qm[:, :], ACT.Exp).then_inc(qexp_made.sem, 1)
                    yield
                    act.wait_ge(*qk_turned(blk, r))
                    act.activation(qkT, v3_(A[0][:, :], 4), ACT.Copy).then_inc(qkT_made.sem, 1)
                    yield
                    yield
                    yield
                    act.wait_ge(*ly_turned(blk, r))
                    act.activation(lyT[:, :], A[2][:, 0:D], ACT.Copy).then_inc(lyT_made.sem, 1)
                    yield
                    yield

            def ffn(y, blk):
                g = 1 + 2 * y
                norm(g, blk)
                yield
                act.wait_ge(*rt_max[y](blk))
                act.activation(rt[1][:, :], rt[0][:, :], ACT.Exp).then_inc(rt_exp[y].sem, 1)
                act.wait_ge(*lh_raw[y](blk))
                act.activation(gl[:, :], F[3][:, :], ACT.Gelu, bias=ffn_c[y][:, C_DOWN:C_DOWN + 1]
                               ).then_inc(gl_made[y].sem, 1)
                act.activation(ghT, hT[1], ACT.Gelu).then_inc(gh_made[y].sem, 1)
                yield
                for n, group in enumerate(GROUPS):
                    for j in group_tiles(n):
                        act.wait_ge(*hid_raw[y](blk, j))
                        if j >= RING:
                            act.wait_ge(*exp_raw[y](blk, unit_of(j - RING)))
                        col = hidden_col(j)
                        act.activation(u[j % RING][:, :], F[j % 2][:, :], ACT.Gelu,
                                       bias=ffn_c[y][:, col:col + 1]).then_inc(u_made[y].sem, 1)
                    yield
                    if n == 0:
                        act.wait_ge(*top_diff[y](blk))
                        act.activation(rm[2][:, :], rm[1][:, :], ACT.Tanh, scale=0.5).then_inc(top_tanh[y].sem, 1)
                        act.wait_ge(*gates_turned[y](blk))
                        act.activation(gatesT[:, :], F[2][0:GC, :], ACT.Copy).then_inc(gatesT_made[y].sem, 1)
                        yield
                    for _ in range(B * len(group)):
                        yield
                act.wait_ge(*fo_turned[y](blk))
                act.activation(foT[:, :], F[0][:, :], ACT.Copy).then_inc(foT_made[y].sem, 1)
                yield
                yield

            walk(act, attn0, ffn, attn1)

        @block.vector
        def _(dve):
            made = [0]

            def setup(ins):
                made[0] += 1
                ins.then_inc(set_dve, 1)
                dve.wait_ge(set_dve, made[0])

            dve.wait_ge(masks_made, 1)
            dve.wait_ge(set_act, 1)
            setup(dve.tensor_scalar(c_t[:, :], c_t[:, :], 0.5, None, ALU.mult))
            setup(dve.scalar_tensor_tensor(c_s[:, :], c_s[:, :], 1.0, c_t[:, :], ALU.add, ALU.mult))
            assert made[0] == SET_C
            dve.wait_ge(set_act, 2)
            setup(dve.tensor_scalar(a_neg[:, :], a_neg[:, :], -1.0, None, ALU.mult))
            for y in range(2):
                setup(dve.tensor_tensor(router_bias[y][:, :], rows[:, R_RB + 8 * y:R_RB + 8 * y + 8],
                                        rows[:, R_COST:R_COST + 8], ALU.subtract))
            setup(dve.tensor_scalar(mam_c[:, 0:C_NW], mam_c[:, 0:C_NW], 0.5, None, ALU.mult))
            dve.wait_ge(loaded["w_in"], 16)
            setup(dve.tensor_scalar(w_in[:, :, 0:DI], w_in[:, :, 0:DI], 0.5, None, ALU.mult))
            dve.wait_ge(loaded["w_out"], 16)
            for k in range(DI // P):
                setup(dve.tensor_scalar(w_out[:, k, :], w_out[:, k, :], mam_c[:, C_NW + k:C_NW + k + 1],
                                        None, ALU.mult))
            dve.wait_ge(set_act, 2)
            for y in range(2):
                setup(dve.tensor_reduce(parity[:, y:y + 1], v3(block8, LG // 2)[:, :, y], AX_X, ALU.add))
            for y in range(2):
                dve.wait_ge(loaded[f"ffn{y}"], 16)
                dve.wait_ge(set_act, 3 + y)
                if y:
                    dve.wait_ge(set_pe, CONST_READ0)
                for e in range(NE):
                    j = slice(FIRST[e], FIRST[e] + TILES[e])
                    setup(dve.tensor_scalar(gsel[:, j, e:e + 1], gb1[:, j].unsqueeze(2), -1.0, None, ALU.mult))
                setup(dve.tensor_copy(gsel[:, :, NE:GC], gb1[:, :].unsqueeze(2)))
                setup(dve.tensor_scalar(ffn_w[y][:, W_S2:W_S2 + L], ffn_w[y][:, W_S2:W_S2 + L], 0.1,
                                        None, ALU.mult))
                assert made[0] == (SET_SEL0, SET_SEL1)[y]
                dve.wait_ge(set_pe, (CONST_DONE0, CONST_DONE1)[y])
                setup(dve.tensor_copy(cw[y][:, :], F[0][0:GC, 0:L]))
            assert made[0] == SET_CW
            for y in range(2):
                if y:
                    dve.wait_ge(set_pe, MOD_READ)
                setup(dve.tensor_copy(c_rep.rearrange("p (a b) -> p a b", a=KD * B),
                                      bc(v3(c_s, 2)[:, y, :].unsqueeze(2), P, KD * B, P)))
                assert made[0] == (SET_REP0, SET_REP1)[y]
                dve.wait_ge(set_pe, (MODC0, MODC1)[y])
                for s in range(2):
                    src = F[1][:, 16 * s:16 * s + 16].rearrange("p (w k b) -> p w k b", w=2, k=KD)
                    setup(dve.tensor_copy(mod_c[2 * y + s][:, 0, :, :], src[:, 0, :, :]))
                    setup(dve.tensor_scalar(mod_c[2 * y + s][:, 1, :, :], src[:, 1, :, :], 1.0, None, ALU.add))
                for s in range(2):
                    for h in range(2):
                        n = 2 * s + h
                        dve.wait_ge(set_pe, (MODC0, MODC1)[y] + 1 + n)
                        gb = gate_bc[2 * y + s][:, h * 2 * D:(h + 1) * 2 * D]
                        src = F[2 + h][:, :]
                        sign = u[2]
                        setup(dve.tensor_scalar(sign, src, 0.0, 2.0, ALU.is_ge, ALU.mult))
                        setup(dve.tensor_scalar(sign, sign, -1.0, None, ALU.add))
                        setup(dve.tensor_tensor(gb, sign, src, ALU.mult))
                        setup(dve.scalar_tensor_tensor(gb, gb, 0.25, sign, ALU.max, ALU.mult))
            assert made[0] == SET_GATES == SET_ALL
            dve.wait_ge(set_done, 1)

            def carry_wait():
                dve.memset(spare[:, 0:1], 0.0)

            def rsqrt(blk, chain, y, v, tmp):
                yi, vi = y.bitcast(I32), v.bitcast(I32)
                chain.step(dve, blk, dve.tensor_scalar(yi, vi, 1, None, ALU.logical_shift_right))
                chain.step(dve, blk, dve.tensor_scalar(yi, yi, -1.0, float(0x5F3759DF), ALU.mult, ALU.add))
                for _ in range(3):
                    chain.step(dve, blk, dve.tensor_tensor(tmp, y, y, ALU.mult))
                    chain.step(dve, blk, dve.tensor_tensor(tmp, tmp, v, ALU.mult))
                    chain.step(dve, blk, dve.tensor_scalar(tmp, tmp, -0.5, 1.5, ALU.mult, ALU.add))
                    chain.step(dve, blk, dve.tensor_tensor(y, y, tmp, ALU.mult))

            def norm(g, blk, chain):
                s = g % 2
                xg = v3(x_in_of[g], B)
                if g == 0:
                    dve.wait_ge(x_in.sem, blk * 16 + 16)
                else:
                    dve.wait_ge(*x_done[g](blk, B - 1))
                for r in range(B):
                    last = dve.bn_stats(v3(stats[s], B)[:, r, :], xg[:, r, :])
                chain.step(dve, blk, last)
                carry_wait()
                for r in range(B):
                    last = dve.bn_aggr(v3(mv[s], B)[:, r, :], v3(stats[s], B)[:, r, :])
                chain.step(dve, blk, last)
                chain.step(dve, blk, dve.tensor_scalar(var_e[s][:, :], v3(mv[s], B)[:, :, 1], 1e-05, None, ALU.add))
                rsqrt(blk, chain, rstd[s][:, :], var_e[s][:, :], rtmp[s][:, :])
                for r in range(B):
                    dve.tensor_scalar(v3(xn[s], B)[:, r, :], xg[:, r, :], v3(mv[s], B)[:, r, 0:1],
                                      rstd[s][:, r:r + 1], ALU.subtract, ALU.mult).then_inc(xn_made[g].sem, 1)

            def residual(g, blk, bank, cols, r, n, tmp, chain):
                w = slice(r * D, (r + n) * D)
                chain.step(dve, blk, dve.tensor_tensor(tmp, bank[:, cols], gate_bc[g][:, w], ALU.mult))
                dve.tensor_tensor(x_of[g][:, w], x_of[g][:, w], tmp, ALU.add).then_inc(x_done[g + 1].sem, n)

            def attn0(blk):
                c = dve_a0
                norm(0, blk, c)
                yield
                dve.wait_ge(*dt_raw(blk))
                c.step(dve, blk, dve.tensor_tensor(v3(dt_v, B), v3_(A[2][:, 0:B * NH], B),
                                                   bc(rows[:, R_DT:R_DT + NH].unsqueeze(1), P, B, NH), ALU.add))
                dve.scalar_tensor_tensor(dt_n[:, :], dt_v[:, :], -1.0, dt_v[:, :], ALU.mult, ALU.min
                                         ).then_inc(dt_abs.sem, 1)
                dve.wait_ge(*dt_ln(blk))
                c.step(dve, blk, dve.scalar_tensor_tensor(dt_s[:, :], dt_v[:, :], 0.0, dt_n[:, :],
                                                          ALU.max, ALU.add))
                dve.tensor_tensor(v3(dA, B), v3(dt_s, B), bc(a_neg[:, :].unsqueeze(1), P, B, NH), ALU.mult
                                  ).then_inc(dA_made.sem, 1)
                yield
                dve.wait_ge(*dec_made(blk))
                dve.tensor_tensor(dtd[:, :], dt_s[:, :], v3(dec, 3)[:, 0, :], ALU.mult).then_inc(dtd_made.sem, 1)
                for m in range(XM):
                    dve.wait_ge(*xbc_in(blk, m))
                    dve.wait_ge(*tail_put(blk, m))
                    if m >= 2:
                        dve.wait_ge(*xs_made(blk, m - 2))
                    o = v3(acc[:, m % 2, :], B)
                    src = raw[:, m % 2, :, :]
                    w = [mam_c[:, C_CW + m * CONV + k:C_CW + m * CONV + k + 1] for k in range(CONV)]
                    c.step(dve, blk, dve.tensor_scalar(o, src[:, :, 3:3 + P], w[3],
                                                       mam_c[:, C_CB + m:C_CB + m + 1], ALU.mult, ALU.add))
                    for k in (0, 1):
                        c.step(dve, blk, dve.scalar_tensor_tensor(o, src[:, :, k:k + P], w[k], o,
                                                                  ALU.mult, ALU.add))
                    dve.scalar_tensor_tensor(o, src[:, :, 2:2 + P], w[2], o, ALU.mult, ALU.add
                                             ).then_inc(conv_made.sem, 1)
                    if m:
                        silu(blk, m - 1)
                    yield
                silu(blk, XM - 1)
                yield
                for r in range(B):
                    h = slice(r * NH, (r + 1) * NH)
                    dve.wait_ge(*dA_made(blk))
                    if r:
                        dve.wait_ge(*seg_raw(blk, 2 * r - 1))
                    else:
                        dve.wait_ge(*tail_kept(blk, XM - 1))
                    dve.tensor_tensor(v3(va, NH), bc(upto[:, :].unsqueeze(1), P, NH, P),
                                      bc(dA[:, h].unsqueeze(2), P, NH, P), ALU.mult).then_inc(va_made.sem, 1)
                    dve.wait_ge(*z_tanh(blk, r))
                    dve.scalar_tensor_tensor(sz[:, :], tz[:, :], 1.0, A[1][:, :], ALU.add, ALU.mult
                                             ).then_inc(sz_made.sem, 1)
                    dve.wait_ge(*xt_made(blk, r))
                    c.step(dve, blk, dve.tensor_tensor(cbm[:, :], A[3][:, NS:2 * NS], upto[:, :], ALU.mult))
                    dve.tensor_tensor(v3(xdt, NH), v3(xt, NH), bc(dt_s[:, h].unsqueeze(2), P, NH, HD), ALU.mult)
                    yield
                    dve.wait_ge(*seg_exp(blk, r))
                    dve.tensor_tensor(v3(seg, NH), v3(seg, NH), bc(cbm[:, :].unsqueeze(1), P, NH, P), ALU.mult
                                      ).then_inc(mh_made.sem, 1)
                    yield
                    dve.wait_ge(*yoff_raw(blk, r))
                    c.step(dve, blk, dve.tensor_tensor(v3(yg, NH), v3_(A[0][:, :], NH),
                                                       bc(v3(dec, 3)[:, 1, h].unsqueeze(2), P, NH, HD), ALU.mult))
                    dve.wait_ge(*xd_made(blk, r))
                    c.step(dve, blk, dve.tensor_tensor(yg[:, :], yg[:, :], xd[:, :], ALU.add))
                    c.step(dve, blk, dve.tensor_tensor(v3(state[r], NH), v3(state[r], NH),
                                                       bc(v3(dec, 3)[:, 2, h].unsqueeze(2), P, NH, HD), ALU.mult))
                    dve.wait_ge(*dst_raw(blk, r))
                    dve.tensor_tensor(state[r][:, :], state[r][:, :], A[1][:, :], ALU.add
                                      ).then_inc(state_made.sem, 1)
                    yield
                    dve.wait_ge(*ydiag_raw(blk, r))
                    c.step(dve, blk, dve.tensor_tensor(yg[:, :], yg[:, :], A[2][:, :], ALU.add))
                    dve.tensor_tensor(yg[:, :], yg[:, :], sz[:, :], ALU.mult).then_inc(yg_made.sem, 1)
                    dve.wait_ge(*ysum_made(blk, r))
                    c.step(dve, blk, dve.tensor_scalar(yst[:, 0:1], yst[:, 0:1], 1.0 / DI, 1e-05, ALU.mult, ALU.add))
                    rsqrt(blk, c, yst[:, 2:3], yst[:, 0:1], yst[:, 1:2])
                    dve.tensor_scalar(yg[:, :], yg[:, :], yst[:, 2:3], None, ALU.mult).then_inc(ygn_made.sem, 1)
                    yield
                    yield
                    dve.wait_ge(*out0_raw(blk, r))
                    residual(0, blk, A[3], slice(2 * NS, 2 * NS + D), r, 1, res_a[:, :], c)
                    yield
                c.close()

            def silu(blk, m):
                dve.wait_ge(*conv_tanh(blk, m))
                dve.scalar_tensor_tensor(xs[:, m, :], v3(th, 2)[:, m % 2, :], 1.0, acc[:, m % 2, :],
                                         ALU.add, ALU.mult).then_inc(xs_made.sem, 1)

            def attn1(blk):
                c = dve_a1
                norm(2, blk, c)
                yield
                dve.wait_ge(*lg_raw(blk))
                dve.tensor_tensor(v3(lg, B), v3_(A[2][:, 0:B * LH], B),
                                  bc(rows[:, R_BG:R_BG + LH].unsqueeze(1), P, B, LH), ALU.add
                                  ).then_inc(lg_v.sem, 1)
                dve.wait_ge(*lg_e(blk))
                c.step(dve, blk, dve.tensor_scalar(la[:, :], lg[:, :], 1.0, None, ALU.add))
                c.step(dve, blk, dve.reciprocal(la[:, :], la[:, :]))
                dve.tensor_scalar(la[:, :], la[:, :], 0.8, 0.9995, ALU.max, ALU.min).then_inc(lg_b.sem, 1)
                yield
                dve.wait_ge(*le_made(blk))
                dve.wait_ge(rope_in.sem, blk * 16 + 16)
                yield
                for r in range(B):
                    dve.wait_ge(*qk_raw(blk, r))
                    half = LD // 2
                    both = A[0][:, :].rearrange("p (h t e) -> p (h t) e", t=2, e=half)
                    cos = bc(rope[:, 0, :].unsqueeze(1), P, 4 * LH, half)
                    sin = bc(rope[:, 1, :].unsqueeze(1), P, 4 * LH, half)
                    dve.tensor_tensor(v3(qr1, 4 * LH), both, cos, ALU.mult)
                    c.step(dve, blk, dve.tensor_tensor(v3(qr2, 4 * LH), both, sin, ALU.mult))
                    t1, t2, o = (v4(t, 2 * LH, 2) for t in (qr1, qr2, qk))
                    dve.tensor_tensor(o[:, :, 0, :], t1[:, :, 0, :], t2[:, :, 1, :], ALU.subtract)
                    c.step(dve, blk, dve.tensor_tensor(o[:, :, 1, :], t2[:, :, 0, :], t1[:, :, 1, :], ALU.add))
                    dve.tensor_scalar(qm[:, :], qk[:, :], 0.0, None, ALU.min).then_inc(qneg_made.sem, 1)
                    dve.wait_ge(*qexp_made(blk, r))
                    c.step(dve, blk, dve.scalar_tensor_tensor(qk[:, :], qk[:, :], 0.0, qm[:, :], ALU.max, ALU.add))
                    for n in range(2):
                        q = slice(n * D, (n + 1) * D)
                        last = dve.tensor_tensor(v3_(qk[:, q], LH), v3_(qk[:, q], LH),
                                                 bc(le[:, n, r, :].unsqueeze(2), P, LH, LD), ALU.mult)
                    last.then_inc(qs_made.sem, 1)
                    yield
                    dve.wait_ge(*qkT_made(blk, r))
                    for n in range(2):
                        last = dve.tensor_tensor(qpar[:, n, :, :], bc(qkT[:, n, :].unsqueeze(1), P, 2, P),
                                                 bc(parity[:, :].unsqueeze(2), P, 2, P), ALU.mult)
                    last.then_inc(qpar_made.sem, 1)
                    c.step(dve, blk, dve.tensor_tensor(v3(lbt, 2), v3_(le[:, 2, r, :], 2),
                                                       bc(block8[:, :].unsqueeze(1), P, 2, LG), ALU.mult))
                    yield
                    dve.wait_ge(*att_raw(blk, r))
                    for k in range(4):
                        last = dve.tensor_tensor(v3(am[k], 4),
                                                 v3_(A[k][:, :], 4), bc(upto[:, :].unsqueeze(1), P, 4, P), ALU.mult)
                    last.then_inc(am_made.sem, 1)
                    yield
                    dve.wait_ge(*ly_raw(blk, r))
                    num = A[0][:, 0:LH * EXT].rearrange("p (h e) -> p h e", h=LH)
                    c.step(dve, blk, dve.tensor_scalar(lden[:, :].unsqueeze(2), num[:, :, LD:EXT], 1e-06, None, ALU.add))
                    c.step(dve, blk, dve.reciprocal(lden[:, :], lden[:, :]))
                    dve.tensor_tensor(v3(ly, LH), num[:, :, 0:LD], bc(lden[:, :].unsqueeze(2), P, LH, LD),
                                      ALU.mult).then_inc(ly_made.sem, 1)
                    dve.wait_ge(*lst_raw(blk, r))
                    sums = A[1][:, 0:2 * LG * EXT]
                    c.step(dve, blk, dve.tensor_tensor(v3(ltm, 2), lst[r], v3_(sums, 2), ALU.add))
                    dve.tensor_tensor(lst[r].rearrange("p g (h e) -> p (g h) e", e=EXT), v3(ltm, 2 * LG),
                                      bc(lbt[:, :].unsqueeze(2), P, 2 * LG, EXT), ALU.mult).then_inc(lst_made.sem, 1)
                    yield
                    yield
                    dve.wait_ge(*out2_raw(blk, r))
                    if r == 0:
                        dve.wait_ge(*copied[2](blk, B - 1))
                    residual(2, blk, A[3], slice(0, D), r, 1, res_a[:, :], c)
                    yield
                c.close()

            def ffn(y, blk):
                g, c = 1 + 2 * y, dve_f[y]
                norm(g, blk, c)
                yield
                e3 = v3(rt[0], B)
                dve.wait_ge(*logit_raw[y](blk))
                c.step(dve, blk, dve.tensor_tensor(e3, v3_(F[2][:, 0:B * NE], B),
                                                   bc(router_bias[y][:, :].unsqueeze(1), P, B, NE), ALU.add))
                c.step(dve, blk, dve.tensor_reduce(rm[0][:, :], e3, AX_X, ALU.max))
                dve.tensor_tensor(e3, e3, bc(rm[0][:, :].unsqueeze(2), P, B, NE), ALU.subtract
                                  ).then_inc(rt_max[y].sem, 1)
                dve.wait_ge(*rt_exp[y](blk))
                p3 = v3(rt[1], B)
                c.step(dve, blk, dve.tensor_reduce(rm[0][:, :], p3, AX_X, ALU.add))
                c.step(dve, blk, dve.reciprocal(rm[0][:, :], rm[0][:, :]))
                c.step(dve, blk, dve.tensor_tensor(p3, p3, bc(rm[0][:, :].unsqueeze(2), P, B, NE), ALU.mult))
                carry_wait()
                for r in range(B):
                    last = dve.max(p8[:, r, :], p3[:, r, :])
                c.step(dve, blk, last)
                dve.tensor_tensor(rm[1][:, :], p8[:, :, 1], p8[:, :, 0], ALU.subtract).then_inc(top_diff[y].sem, 1)
                for r in range(B):
                    last = dve.max_index(i8[:, r, :], p8[:, r, :], p3[:, r, :])
                c.step(dve, blk, last)
                c.step(dve, blk, dve.tensor_copy(i8f, i8[:, :, 0:2]))
                yield
                yield
                dve.wait_ge(*top_tanh[y](blk))
                dve.tensor_scalar(g2[:, :, 0], rm[2][:, :], -0.5, 0.5, ALU.mult, ALU.add)
                c.step(dve, blk, dve.tensor_scalar(g2[:, :, 1], rm[2][:, :], 0.5, 0.5, ALU.mult, ALU.add))
                for n, t in ((0, rt[0]), (1, rt[2])):
                    last = dve.tensor_tensor(v3(t, B), bc(iota8[:, :].unsqueeze(1), P, B, NE),
                                             bc(i8f[:, :, n:n + 1], P, B, NE), ALU.is_equal)
                c.step(dve, blk, last)
                for n, t in ((0, rt[0]), (1, rt[2])):
                    last = dve.tensor_tensor(v3(t, B), v3(t, B), bc(g2[:, :, n:n + 1], P, B, NE), ALU.mult)
                c.step(dve, blk, last)
                dve.tensor_tensor(gates[:, :, 0:NE], e3, v3(rt[2], B), ALU.add).then_inc(gates_made[y].sem, 1)
                yield

                def weigh(n):
                    dve.wait_ge(*exp_raw[y](blk, n))
                    if n == 0:
                        dve.tensor_copy(fo[:, :], F[2][:, :]).then_inc(fo_made[y].sem, 1)
                        return
                    dve.wait_ge(*fo_made[y](blk, n - 1))
                    for r in range(B):
                        w, e = slice(r * L, (r + 1) * L), UNITS[n]
                        last = dve.scalar_tensor_tensor(fo[:, w], F[2 + n % 2][:, w], gates[:, r, e:e + 1],
                                                        fo[:, w], ALU.mult, ALU.add)
                    last.then_inc(fo_made[y].sem, 1)

                n = 0
                for k, group in enumerate(GROUPS):
                    if k:
                        if n:
                            weigh(n - 1)
                        yield
                    for q in range(len(group)):
                        if n and q:
                            weigh(n - 1)
                        n += 1
                        for _ in range(B):
                            yield
                weigh(n - 1)
                yield
                dve.wait_ge(*copied[g](blk, B - 1))
                for n in range(2):
                    dve.wait_ge(*outf_raw[y](blk, n))
                    residual(g, blk, F[2 + n], slice(0, 2 * D), 2 * n, 2, res_f[n][:, :], c)
                c.close()
                yield

            walk(dve, attn0, ffn, attn1)

        @block.tensor
        def _(pe):
            made = [0]

            def setup(ins):
                made[0] += 1
                ins.then_inc(set_pe, 1)

            for y in range(2):
                pe.wait_ge(set_dve, (SET_SEL0, SET_SEL1)[y])
                for j in range(NT):
                    last = pe.matmul(F[0][0:GC, 0:L], gsel[:, j, :], ffn_w[y][:, W_E2 + j * L:W_E2 + (j + 1) * L],
                                     start=(j == 0), stop=False)
                setup(last)
                setup(pe.matmul(F[0][0:GC, 0:L], b2sel[:, :], b2rows[y][:, :], start=False, stop=True))
                assert made[0] == (CONST_DONE0, CONST_DONE1)[y]
                if y == 0:
                    pe.wait_ge(set_dve, SET_SEL0 + 1)
            for y in range(2):
                pe.wait_ge(loaded[f"mod{y}"], 16)
                pe.wait_ge(set_dve, (SET_REP0, SET_REP1)[y])
                wm = v3_(wmod[0][:, :], KD)
                cs = v3(c_s, 2)[:, y, :].rearrange("p (k b) -> p k b", k=KD)
                for s in range(2):
                    for w in range(2):
                        for kh in range(KD):
                            o = 16 * s + 8 * w + B * kh
                            c0 = (3 * s + w) * D + kh * P
                            for k in range(KD):
                                last = pe.matmul(F[1][:, o:o + B], wm[:, k, c0:c0 + P], cs[:, k, :],
                                                 start=(k == 0), stop=(k == KD - 1))
                setup(last)
                rep = c_rep.rearrange("p (k b t) -> p k b t", k=KD, b=B)
                for s in range(2):
                    for h in range(2):
                        if s:
                            pe.wait_ge(set_dve, (SET_REP0, SET_REP1)[y] + 4 + 4 * (h + 1))
                        for b in range(2):
                            for k in range(KD):
                                last = pe.matmul(F[2 + h][:, b * D:(b + 1) * D], rep[:, k, 2 * h + b, :],
                                                 wm[:, k, (3 * s + 2) * D:(3 * s + 3) * D],
                                                 start=(k == 0), stop=(k == KD - 1))
                        setup(last)
                assert made[0] == (MOD_READ, MOD_READ + 5)[y]
            pe.wait_ge(set_dve, SET_ALL)
            pe.wait_ge(loaded["lin"], 16)

            def norm(g, blk):
                s = g % 2
                bank = A if s == 0 else F
                for r in range(B):
                    pe.wait_ge(*xn_made[g](blk, r))
                    for k in range(KD):
                        last = pe.transpose(bank[k][:, r * P:(r + 1) * P], v3(xn[s], B)[:, r, k * P:(k + 1) * P],
                                            ident[:, :])
                last.then_inc(xn_turned[g].sem, 1)

            def over_d(dst, lhs, rhs, **kw):
                for k in range(KD):
                    last = pe.matmul(dst, lhs(k), rhs(k), start=(k == 0), stop=(k == KD - 1))
                return last

            def attn0(blk):
                norm(0, blk)
                yield
                pe.wait_ge(*hT_made[0](blk, B - 1))
                h = hT[0]
                for r in range(B):
                    last = over_d(A[2][:, r * NH:(r + 1) * NH], lambda k: h[:, k, r * P:(r + 1) * P],
                                  lambda k: w_in[:, k, DIN - NH:DIN])
                last.then_inc(dt_raw.sem, 1)
                yield
                pe.wait_ge(*dA_made(blk))
                for n, m in enumerate((after, upto, ones)):
                    last = pe.matmul(A[2][:, (1 + n) * B * NH:(2 + n) * B * NH], m[:, :], dA[:, :],
                                     start=True, stop=True)
                last.then_inc(dec_raw.sem, 1)
                for m in range(XM):
                    if m == 3:
                        pe.wait_ge(*dec_made(blk))
                    if m >= 4:
                        pe.wait_ge(*xbc_in(blk, m - 4))
                    over_d(A[(m + 3) % 4][:, :], lambda k: w_in[:, k, DI + m * P:DI + (m + 1) * P],
                           lambda k: h[:, k, :]).then_inc(xbc_raw.sem, 1)
                    yield
                yield
                pe.wait_ge(*xs_made(blk, XM - 1))
                for r in range(B):
                    t = slice(r * P, (r + 1) * P)
                    if r:
                        pe.wait_ge(*yg_made(blk, r - 1))
                        pe.wait_ge(*x_done[1](blk, r - 1))
                    for m in range(4):
                        pe.transpose(A[2][:, m * P:(m + 1) * P], xs[:, m, t], ident[:, :])
                    pe.transpose(A[3][:, 0:NS], xs[:, 4, t], ident[:, :])
                    pe.matmul(A[3][:, NS:2 * NS], xs[:, 4, t], xs[:, 5, t], start=True, stop=True
                              ).then_inc(xb_turned.sem, 1)
                    over_d(A[1][:, :], lambda k: h[:, k, t], lambda k: w_in[:, k, 0:DI]).then_inc(z_raw.sem, 1)
                    yield
                    pe.wait_ge(*va_made(blk, r))
                    for k in range(2):
                        if k:
                            pe.wait_ge(*sz_made(blk, r))
                        pe.matmul(A[k][:, :], after[:, :], va[:, k * 512:(k + 1) * 512], start=True, stop=True
                                  ).then_inc(seg_raw.sem, 1)
                    yield
                    pe.wait_ge(*seg_exp(blk, r))
                    wait_before(pe, state_made, blk, r)
                    pe.matmul(A[0][:, :], xs[:, 5, t], state[r][:, :], start=True, stop=True
                              ).then_inc(yoff_raw.sem, 1)
                    pe.wait_ge(*xdt_made(blk, r))
                    pe.matmul(A[1][:, :], bt[:, :], xdec[:, :], start=True, stop=True).then_inc(dst_raw.sem, 1)
                    yield
                    pe.wait_ge(*mh_made(blk, r))
                    for q in range(NH):
                        last = pe.matmul(A[2][:, q * HD:(q + 1) * HD], v3(seg, NH)[:, q, :],
                                         xdt[:, q * HD:(q + 1) * HD], start=True, stop=True)
                    last.then_inc(ydiag_raw.sem, 1)
                    yield
                    pe.wait_ge(*ygn_made(blk, r))
                    for m in range(4):
                        last = pe.transpose(A[0][:, m * P:(m + 1) * P], yg[:, m * P:(m + 1) * P], ident[:, :])
                    last.then_inc(yg_turned.sem, 1)
                    yield
                    pe.wait_ge(*gT_made(blk, r))
                    o = A[3][:, 2 * NS:2 * NS + D]
                    for m in range(4):
                        pe.matmul(o, gT[:, m * P:(m + 1) * P], w_out[:, m, :], start=(m == 0), stop=False)
                    for k in range(KD):
                        last = pe.matmul(o[:, k * P:(k + 1) * P], h[:, k, t], ident[:, :], start=False,
                                         stop=(k == KD - 1))
                    last.then_inc(out0_raw.sem, 1)
                    yield

            def attn1(blk):
                norm(2, blk)
                yield
                pe.wait_ge(*hT_made[2](blk, B - 1))
                h = hT[0]
                wq = v3_(lin_w[:, W_QK:W_V], KD)
                wv = v3_(lin_w[:, W_V:W_G], KD)
                wg = v3_(lin_w[:, W_G:W_O], KD)
                wo = v3_(lin_w[:, W_O:W_LIN], KD)
                for r in range(B):
                    last = over_d(A[2][:, r * LH:(r + 1) * LH], lambda k: h[:, k, r * P:(r + 1) * P],
                                  lambda k: wg[:, k, :])
                last.then_inc(lg_raw.sem, 1)
                yield
                pe.wait_ge(*la_made(blk))
                for n, m in enumerate((upto, ones)):
                    last = pe.matmul(A[2][:, (1 + n) * 64:(2 + n) * 64], m[:, :], la[:, :], start=True, stop=True)
                last.then_inc(cs_raw.sem, 1)
                yield
                pe.wait_ge(*le_made(blk))
                for r in range(B):
                    t = slice(r * P, (r + 1) * P)
                    if r:
                        pe.wait_ge(*ly_made(blk, r - 1))
                        pe.wait_ge(*lst_made(blk, r - 1))
                    over_d(A[0][:, :], lambda k: h[:, k, t], lambda k: wq[:, k, :]).then_inc(qk_raw.sem, 1)
                    over_d(A[1][:, 0:D], lambda k: h[:, k, t], lambda k: wv[:, k, :]).then_inc(v_raw.sem, 1)
                    yield
                    pe.wait_ge(*qs_made(blk, r))
                    for m in range(4):
                        last = pe.transpose(A[0][:, m * P:(m + 1) * P], qk[:, m * P:(m + 1) * P], ident[:, :])
                    last.then_inc(qk_turned.sem, 1)
                    yield
                    pe.wait_ge(*qkT_made(blk, r))
                    pe.wait_ge(*qpar_made(blk, r))
                    pe.wait_ge(*v1_made(blk, r))
                    if r:
                        pe.wait_ge(*x_done[3](blk, r - 1))
                    for n in range(2):
                        for q in range(4):
                            last = pe.matmul(A[q][:, n * D:(n + 1) * D], qkT[32 * q:32 * q + 32, 2 + n, :],
                                             qpar[32 * q:32 * q + 32, n, :, :], start=True, stop=True)
                    last.then_inc(att_raw.sem, 1)
                    yield
                    pe.wait_ge(*am_made(blk, r))
                    wait_before(pe, lst_made, blk, r)
                    for n in range(2):
                        o = n * LG * EXT
                        pe.matmul(A[0][:, o:o + LG * EXT], qkT[:, n, :], lst[r][:, n, :], start=(n == 0), stop=False,
                                  skip_group_check=True)
                    for n in range(2):
                        for q in range(4):
                            for j in range(2):
                                hd = LG * n + 2 * q + j
                                last = pe.matmul(A[0][:, hd * EXT:(hd + 1) * EXT],
                                                 am[q][:, n * D + j * P:n * D + (j + 1) * P],
                                                 v3(v1, LH)[:, hd, :], start=False, stop=(hd == LH - 1),
                                                 skip_group_check=True)
                    last.then_inc(ly_raw.sem, 1)
                    for n in range(2):
                        o = n * LG * EXT
                        last = pe.matmul(A[1][:, o:o + LG * EXT], qk[:, D + n * P:D + (n + 1) * P],
                                         v1[:, o:o + LG * EXT], start=True, stop=True)
                    last.then_inc(lst_raw.sem, 1)
                    yield
                    pe.wait_ge(*ly_made(blk, r))
                    for m in range(2):
                        last = pe.transpose(A[2][:, m * P:(m + 1) * P], ly[:, m * P:(m + 1) * P], ident[:, :])
                    last.then_inc(ly_turned.sem, 1)
                    yield
                    pe.wait_ge(*lyT_made(blk, r))
                    over_d(A[3][:, 0:D], lambda k: lyT[:, k * P:(k + 1) * P], lambda k: wo[:, k, :]
                           ).then_inc(out2_raw.sem, 1)
                    yield

            def ffn(y, blk):
                g = 1 + 2 * y
                w = ffn_w[y]
                norm(g, blk)
                yield
                h = hT[1]
                pe.wait_ge(*hT_made[g](blk, B - 1))
                for r in range(B):
                    last = over_d(F[2][:, r * NE:(r + 1) * NE], lambda k: h[:, k, r * P:(r + 1) * P],
                                  lambda k: w[:, W_ROUT + k * NE:W_ROUT + (k + 1) * NE])
                last.then_inc(logit_raw[y].sem, 1)
                over_d(F[3][:, :], lambda k: w[:, W_DOWN + k * L:W_DOWN + (k + 1) * L],
                       lambda k: h[:, k, :]).then_inc(lh_raw[y].sem, 1)
                yield
                pe.wait_ge(*gl_made[y](blk))
                n = 0
                for k, group in enumerate(GROUPS):
                    for j in group_tiles(k):
                        if j >= 2:
                            pe.wait_ge(*u_made[y](blk, j - 2))
                        c0 = hidden_w(j)
                        pe.matmul(F[j % 2][:, :], w[:, c0:c0 + P], gl[:, :], start=True, stop=True
                                  ).then_inc(hid_raw[y].sem, 1)
                    yield
                    if k == 0:
                        pe.wait_ge(*gates_made[y](blk))
                        for r in range(B):
                            last = pe.transpose(F[2][0:GC, r * P:(r + 1) * P], gates[:, r, :], ident[:, :])
                        last.then_inc(gates_turned[y].sem, 1)
                        yield
                    for e in group:
                        js = range(UNIT_FIRST[n], UNIT_FIRST[n] + UNIT_TILES[n])
                        if n >= 2:
                            pe.wait_ge(*fo_made[y](blk, n - 2))
                        if n == 0:
                            pe.wait_ge(*gatesT_made[y](blk))
                        pe.wait_ge(*u_made[y](blk, js[-1]))
                        for r in range(B):
                            t = slice(r * P, (r + 1) * P)
                            for j in js:
                                c0 = out_w(j)
                                last = pe.matmul(F[2 + n % 2][:, t], u[j % RING][:, t], w[:, c0:c0 + L],
                                                 start=(j == js[0]), stop=(j == js[-1] and n > 0))
                            if n == 0:
                                last = pe.matmul(F[2][:, t], gatesT[:, t], cw[y][:, :], start=False, stop=True)
                            if r == B - 1:
                                last.then_inc(exp_raw[y].sem, 1)
                            yield
                        n += 1
                pe.wait_ge(*fo_made[y](blk, n - 1))
                pe.wait_ge(*u_made[y](blk, NT))
                for r in range(B):
                    last = pe.transpose(F[0][:, r * P:(r + 1) * P], fo[:, r * P:(r + 1) * P], ident[:, :])
                last.then_inc(fo_turned[y].sem, 1)
                yield
                pe.wait_ge(*foT_made[y](blk))
                pe.wait_ge(*gh_made[y](blk))
                for n in range(2):
                    for b in range(2):
                        r = 2 * n + b
                        t = slice(r * P, (r + 1) * P)
                        o = F[2 + n][:, b * D:(b + 1) * D]
                        pe.matmul(o, foT[:, t], w[:, W_UP:W_UP + D], start=True, stop=False)
                        for k in range(KD):
                            last = pe.matmul(o, ghT[:, k, t], w[:, W_CORE + k * D:W_CORE + (k + 1) * D],
                                             start=False, stop=(k == KD - 1))
                    last.then_inc(outf_raw[y].sem, 1)
                yield

            walk(pe, attn0, ffn, attn1)


def v3_(ap, a):
    return ap.rearrange("p (a b) -> p a b", a=a)


def group_tiles(k):
    first = sum(len(g) for g in GROUPS[:k])
    last = first + len(GROUPS[k]) - 1
    return range(UNIT_FIRST[first], UNIT_FIRST[last] + UNIT_TILES[last])


def unit_of(j):
    return max(n for n in range(len(UNITS)) if UNIT_FIRST[n] <= j)


def expert_tile(j):
    n = unit_of(j)
    return None if UNITS[n] == SHARED else FIRST[UNITS[n]] + j - UNIT_FIRST[n]


def hidden_col(j):
    t = expert_tile(j)
    return C_S1 if t is None else C_B1 + t


def hidden_w(j):
    t = expert_tile(j)
    return W_S1 if t is None else W_E1 + t * P


def out_w(j):
    t = expert_tile(j)
    return W_S2 if t is None else W_E2 + t * L


ROW_SLOTS = 6
FFN_SLOTS = 4 + B * len(UNITS) + len(GROUPS) - 1 + 2
AHEAD0 = [3, 1, 4, 2, 2, 2, 2, 1, 2,
          3, 2, 2, 2, 1, 1,
          1, 1, 1, 1, 1, 0,
          1, 2, 2, 2, 1, 1,
          0, 1, 1, 0, 0, 0]
AHEAD1 = [3, 1, 4,
          5, 4, 1, 1, 1, 1,
          1, 2, 2, 2, 1, 1,
          1, 1, 1, 1, 1, 0,
          1, 2, 2, 2, 1, 1]

NSMALL = 9
SET_C = 2
SET_SEL0 = SET_C + 1 + 2 + 1 + 1 + DI // P + 2 + NE + 2
SET_SEL1 = SET_SEL0 + 1 + NE + 2
SET_CW = SET_SEL1 + 1
SET_REP0 = SET_CW + 1
SET_REP1 = SET_REP0 + 4 + 16 + 1
SET_GATES = SET_REP1 + 4 + 16
SET_ALL = SET_GATES
CONST_READ0, CONST_DONE0 = 1, 2
CONST_DONE1 = 4
MODC0 = CONST_DONE1 + 1
MOD_READ = MODC0 + 4
MODC1 = MOD_READ + 1


def kernel(**inputs):
    import concourse.bacc as bacc
    from concourse.bass_utils import run_bass_kernel_spmd as run

    f = {k: np.ascontiguousarray(v) for k, v in inputs.items()}

    def halves(w):
        return w.reshape(w.shape[0] // P, P, w.shape[1]).transpose(1, 0, 2).reshape(P, -1)

    def over_p(*vecs):
        row = np.concatenate([v.reshape(1, -1) for v in vecs], 1)
        return np.ascontiguousarray(np.broadcast_to(row, (P, row.shape[1])))

    arrays = {"x": f["L0_attn_x"]}
    arrays["w_in"] = halves(f["L0_attn_w_in"]).reshape(P, KD, DIN)
    arrays["w_out"] = halves(f["L0_attn_w_out"]).reshape(P, DI // P, D)
    conv_w = f["L0_attn_conv_w"].reshape(XM, P, CONV).transpose(1, 0, 2).reshape(P, XM * CONV)
    arrays["mam_c"] = np.concatenate([conv_w, f["L0_attn_conv_b"].reshape(XM, P).T,
                                      f["L0_attn_norm_w"].reshape(DI // P, P).T], 1)
    cost = np.array([2 * L * h for h in HID], np.float32) * np.float32(COST_LAMBDA)
    arrays["rows"] = over_p(f["L0_attn_dt_bias"], f["L0_attn_A_log"], f["L0_attn_D"], f["L1_attn_bg"],
                            f["L0_ffn_router_b"], f["L1_ffn_router_b"], cost)
    arrays["c_t"] = np.concatenate([f[f"L{y}_c"].reshape(B, KD, P).transpose(2, 1, 0).reshape(P, -1)
                                    for y in range(2)], 1)
    for y in range(2):
        g = {k[len(f"L{y}_ffn_"):]: v for k, v in f.items() if k.startswith(f"L{y}_ffn_")}
        arrays[f"ffn_w{y}"] = np.concatenate(
            [halves(g["down_w"]), g["up_w"], halves(g["core_w"]), halves(g["router_w"]), g["shared_w1"],
             g["shared_w2"]] + [g[f"e{e}_w1"] for e in range(NE)] + [halves(g[f"e{e}_w2"]) for e in range(NE)], 1)
        arrays[f"ffn_c{y}"] = np.concatenate(
            [g["down_b"].reshape(P, 1), g["shared_b1"].reshape(P, 1)]
            + [g[f"e{e}_b1"].reshape(-1, P).T for e in range(NE)], 1)
        arrays[f"b2rows{y}"] = np.stack([g[f"e{e}_b2"] for e in range(NE)] + [g["shared_b2"]], 0)
        arrays[f"wmod{y}"] = halves(f[f"L{y}_wmod"])
    arrays["ub"] = over_p(f["L0_ffn_up_b"], f["L1_attn_bo"], f["L1_ffn_up_b"])
    arrays["ub2"] = over_p(f["L0_ffn_core_b"], np.zeros(D, np.float32), f["L1_ffn_core_b"])
    arrays["lin_w"] = np.concatenate([halves(np.concatenate([f["L1_attn_Wq"], f["L1_attn_Wk"]], 1)),
                                      halves(f["L1_attn_Wv"]), halves(f["L1_attn_Wg"]),
                                      halves(f["L1_attn_Wo"])], 1)
    half = LD // 2
    inv = (1.0 / np.float32(10000.0) ** (np.arange(half, dtype=np.float32) / np.float32(half))).astype(np.float32)
    ang = np.arange(T, dtype=np.float32)[:, None] * inv[None, :]
    arrays["rope"] = np.concatenate([np.cos(ang), np.sin(ang)], 1).astype(np.float32)

    nc = bacc.Bacc("TRN2", target_bir_lowering=False, num_devices=1)
    dram = {}
    arrays = {k: np.ascontiguousarray(v) for k, v in arrays.items()}
    for k, v in arrays.items():
        dram[k] = nc.dram_tensor(f"in_{k}", list(v.shape), F32, kind="ExternalInput").ap()
    out = nc.dram_tensor("out", [B, T, D], F32, kind="ExternalOutput").ap()
    program(nc, dram, out)
    r = run(nc, [{f"in_{k}": v for k, v in arrays.items()}], core_ids=[0])
    return r.results[0]["out"]
```

```python
from contextlib import ExitStack

import numpy as np

import concourse.bass as bass
from concourse import mybir

F32 = mybir.dt.float32
U32 = mybir.dt.uint32
I32 = mybir.dt.int32
ALU = mybir.AluOpType
ACT = mybir.ActivationFunctionType
AX_X = mybir.AxisListType.X

P = 128
B = 4
T = 1024
D = 256
KD = D // P
NBLK = T // P
DI = 512
NS = 128
NH = 8
HD = DI // NH
CONV = 4
XM = (DI + 2 * NS) // P
DIN = 2 * DI + 2 * NS + NH
LH = 16
LD = D // LH
LG = P // LD
EXT = LD + 1
HID = [128, 256, 384, 512, 128, 256, 384, 512]
NE = len(HID)
L = 128
TILES = [h // P for h in HID]
FIRST = [sum(TILES[:e]) for e in range(NE)]
NT = sum(TILES)
GC = NE + 1
COST_LAMBDA = 1e-07
RSQRT_SCALE = -8192.0
RING = 8
SHARED = -1
UNITS = [0, 1, SHARED, 3, 2, 4, 7, 5, 6]
FFN_ORDER = ["down", (0, 1), (2, 3), 0, (4, 5), 1, "gates", SHARED, (6, 7), (8, 9), 3, (10, 11),
             2, "norm_sums", (12, 13), 4, (14, 15), "norm_root", (16, 17), 7, "norm_rows",
             (18, 19), (20,), 5, "turn_next", 6, "core", "turn", "up"]
UNIT_TILES = [1 if e == SHARED else TILES[e] for e in UNITS]
UNIT_FIRST = [sum(UNIT_TILES[:n]) for n in range(len(UNITS))]

W_DOWN = 0
W_UP = W_DOWN + KD * L
W_CORE = W_UP + D
W_ROUT = W_CORE + KD * D
W_S1 = W_ROUT + KD * NE
W_S2 = W_S1 + L
W_E1 = W_S2 + L
W_E2 = W_E1 + NT * P
W_FFN = W_E2 + NT * L
C_DOWN, C_S1, C_B1 = 0, 1, 2
C_FFN = 2 + NT
C_CW, C_CB, C_NW = 0, XM * CONV, XM * CONV + XM
C_MAM = C_NW + DI // P
R_DT, R_AL, R_D, R_BG, R_RB, R_COST = 0, 8, 16, 24, 40, 56
R_ALL = 64
W_QK = 0
W_V = W_QK + KD * 2 * D
W_G = W_V + KD * D
W_O = W_G + KD * LH
W_LIN = W_O + KD * D


class Signal:

    def __init__(self, ctx, nc, name, per_block, start=0):
        self.sem, self.n, self.start = ctx.enter_context(nc.semaphore(name)), per_block, start

    def __call__(self, blk, k=0):
        return self.sem, blk * self.n + (self.start + k + 1)


def wait_before(eng, sig, blk, k):
    if isinstance(blk, int) and blk == 0:
        return
    eng.wait_ge(sig.sem, blk * sig.n + (k + 1 - sig.n))


class Chain:

    def __init__(self, ctx, nc, name, per_block):
        self.sem, self.n, self.k = ctx.enter_context(nc.semaphore(name)), per_block, 0

    def step(self, eng, blk, ins):
        self.k += 1
        ins.then_inc(self.sem, 1)
        eng.wait_ge(self.sem, blk * self.n + self.k)

    def close(self):
        assert self.k == self.n, (self.sem, self.k)
        self.k = 0


def program(nc, dram, out):
    ctx = ExitStack()
    with ctx:
        def sb(name, *shape, dt=F32):
            return ctx.enter_context(nc.sbuf_tensor(name, [shape[0], int(np.prod(shape[1:]))], dt))

        def v3(t, a):
            return t[:, :].rearrange("p (a b) -> p a b", a=a)

        def v4(t, a, b):
            return t[:, :].rearrange("p (a b c) -> p a b c", a=a, b=b)

        def signal(name, n):
            return Signal(ctx, nc, name, n)

        w_in = v3(sb("w_in", P, KD, DIN), KD)
        w_out = v3(sb("w_out", P, DI // P, D), DI // P)
        ffn_w = [sb(f"ffn_w{y}", P, W_FFN) for y in range(2)]
        lin_w = sb("lin_w", P, W_LIN)
        mam_c = sb("mam_c", P, C_MAM)
        ffn_c = [sb(f"ffn_c{y}", P, C_FFN) for y in range(2)]
        rows = sb("rows", P, R_ALL)
        a_neg = sb("a_neg", P, NH)
        router_bias = [sb(f"router_bias{y}", P, NE) for y in range(2)]
        ident = sb("ident", P, P)
        upto = sb("upto", P, P)
        after = sb("after", P, P)
        ones = sb("ones", P, P)
        block8 = sb("block8", P, LG)
        parity = sb("parity", P, 2)
        iota8 = sb("iota8", P, NE)
        eps_ln = sb("eps_ln", P, 1)
        spare = sb("spare", P, 1)
        mod_c = [v4(sb(f"mod_c{g}", P, 2, KD, B), 2, KD) for g in range(4)]
        gate_bc = [sb(f"gate_bc{g}", P, B * D) for g in range(4)]
        out_bias = v3(sb("out_bias", P, 3 * D), 3)
        cw = [sb(f"cw{y}", GC, L) for y in range(2)]

        x_of = [sb(f"x{g}", P, B * D) for g in range(4)]
        x_in_of = [x_of[0], x_of[0], x_of[1], x_of[2]]

        stats = [sb(f"stats{s}", P, B, 6) for s in range(2)]
        mv = [sb(f"mv{s}", P, B, 2) for s in range(2)]
        var_e = [sb(f"var_e{s}", P, B) for s in range(2)]
        rstd = [sb(f"rstd{s}", P, B) for s in range(2)]
        rtmp = [sb(f"rtmp{s}", P, B) for s in range(2)]
        area_v = sb("area_v", P, 2 * B * (P + CONV - 1))
        area_s = sb("area_s", P, NH * P)
        u_ring = sb("u_ring", P, RING * B * P)
        xn = [area_v[:, 0:B * D], u_ring[:, (RING - 2) * B * P:RING * B * P]]
        hT = [v3(sb(f"hT{s}", P, KD, B * P), KD) for s in range(2)]

        raw = v4(area_v, 2, B)
        tails = v4(sb("tails", P, XM, B, CONV - 1), XM, B)
        acc = [area_s[:, 0:B * P], area_s[:, B * P:2 * B * P], sb("acc", P, B * P)[:, :]]
        xs_all = sb("xs", P, XM, B * P)
        xs = v3(xs_all, XM)
        tz = sb("tz", P, DI)
        sz = sb("sz", P, DI)
        dt_v = sb("dt_v", P, B * NH)
        dt_n = sb("dt_n", P, B * NH)
        dt_s = sb("dt_s", P, B * NH)
        dA = sb("dA", P, B * NH)
        dec = sb("dec", P, 3, B * NH)
        dtd = sb("dtd", P, B * NH)
        va = area_v[:, 0:NH * P]
        seg = area_s
        cbm = sb("cbm", P, P)
        xt = sb("xt", P, DI)
        bt = sb("bt", P, NS)
        xd = sb("xd", P, DI)
        th = sb("th", P, 2, DI)
        xdt, xdec = th[:, 0:DI], th[:, DI:2 * DI]
        yg = sb("yg", P, DI)
        yst = sb("yst", P, 4)
        gT = sb("gT", P, DI)
        state = [sb(f"state{r}", P, DI) for r in range(B)]
        res_a = sb("res_a", P, D)

        rope = v3(sb("rope", P, 2, LD // 2), 2)
        lg = sb("lg", P, B * LH)
        la = sb("la", P, B * LH)
        le = v4(sb("le", P, 3, B, LH), 3, B)
        qk, qr1, qr2, qm = xs_all[:, 0:512], xs_all[:, 512:1024], xs_all[:, 1024:1536], xs_all[:, 1536:2048]
        qkT = v3_(xs_all[:, 2048:2560], 4)
        qpar = xs_all[:, 2560:3072].rearrange("p (a b c) -> p a b c", a=2, b=2)
        v1 = sb("v1", P, LH * EXT)
        am = [area_v[:, 0:512], area_v[:, 512:1024], area_s[:, 0:512], area_s[:, 512:1024]]
        lst = [v3(sb(f"lst{r}", P, 2, LG * EXT), 2) for r in range(B)]
        ltm = sb("ltm", P, 2 * LG * EXT)
        lbt = sb("lbt", P, 2 * LG)
        lden = sb("lden", P, LH)
        ly, lyT = yg[:, 0:D], gT[:, 0:D]

        rt = [sb(f"rt{k}", P, B * NE) for k in range(3)]
        rm = [sb(f"rm{k}", P, B) for k in range(4)]
        p8 = v3(sb("p8", P, B, 8), B)
        i8 = v3(sb("i8", P, B, 8, dt=U32), B)
        i8f = v3(sb("i8f", P, B, 2), B)
        g2 = v3(sb("g2", P, B, 2), B)
        gates = v3(sb("gates", P, B, GC), B)
        gatesT = sb("gatesT", GC, B * P)
        gh = sb("gh", P, KD, B * P)
        ghT = v3(gh, KD)
        gl = sb("gl", P, B * P)
        u = [u_ring[:, k * B * P:(k + 1) * B * P] for k in range(RING)]
        fo = sb("fo", P, B * L)
        foT, res_f = gl, (u[2], u[3])

        A = [ctx.enter_context(nc.psum_tensor(f"A{k}", [P, 512], F32)) for k in range(4)]
        F = [ctx.enter_context(nc.psum_tensor(f"F{k}", [P, 512], F32)) for k in range(4)]

        wmod = [xs_all, ffn_w[1][:, 0:KD * 6 * D]]
        c_t = sb("c_t", P, 2, KD * B)
        c_s = sb("c_s", P, 2, KD * B)
        c_rep = u_ring[:, 2 * B * P:4 * B * P]
        gb1 = sb("gb1", P, NT)
        gsel = v3(sb("gsel", P, NT, GC), NT)
        b2rows = [sb(f"b2rows{y}", GC, L) for y in range(2)]
        b2sel = sb("b2sel", GC, GC)
        ub2 = area_s[:, 0:3 * D]

        def one(name):
            return ctx.enter_context(nc.semaphore(name))

        loaded = {k: one(f"loaded_{k}") for k in
                  ("w_in", "w_out", "lin", "ffn0", "ffn1", "small", "mod0", "mod1")}
        masks_made = one("masks_made")
        pool_chain = one("pool_chain")
        set_dve = one("set_dve")
        set_act = one("set_act")
        set_pe = one("set_pe")
        set_done = one("set_done")

        x_in = signal("x_in", 16)
        x_out = signal("x_out", 16)
        rope_in = signal("rope_in", 16)
        x_done = [None] + [signal(f"x{g}_done", B) for g in (1, 2, 3)]
        x_done.append(Signal(ctx, nc, "x4_done", B, start=B))
        copied = [None] + [signal(f"x{g}_copied", B) for g in (1, 2, 3)]
        xn_made = [signal(f"xn{g}_made", B) for g in range(4)]
        xn_turned = [signal(f"xn{g}_turned", 1) for g in range(4)]
        hT_made = [signal(f"hT{g}_made", B) for g in range(4)]
        dve_n = [Chain(ctx, nc, f"dve_n{g}", 15) for g in range(4)]
        dve_a0 = Chain(ctx, nc, "dve_a0", 1 + 1 + 2 * XM + B * 15)
        dt_exp = signal("dt_exp", 1)
        dt_raw = signal("dt_raw", 1)
        dt_abs = signal("dt_abs", 1)
        dt_ln = signal("dt_ln", 1)
        dA_made = signal("dA_made", 1)
        dec_raw = signal("dec_raw", 1)
        dec_made = signal("dec_made", 1)
        dtd_made = signal("dtd_made", 1)
        tail_put = signal("tail_put", XM)
        tail_kept = signal("tail_kept", XM)
        xbc_raw = signal("xbc_raw", XM)
        xbc_in = signal("xbc_in", XM)
        conv_made = signal("conv_made", XM)
        conv_tanh = signal("conv_tanh", XM)
        xs_made = signal("xs_made", XM)
        z_raw = signal("z_raw", B)
        z_tanh = signal("z_tanh", B)
        sz_made = signal("sz_made", B)
        xb_turned = signal("xb_turned", B)
        xt_made = signal("xt_made", B)
        va_made = signal("va_made", B)
        seg_raw = signal("seg_raw", 2 * B)
        seg_exp = signal("seg_exp", B)
        mh_made = signal("mh_made", B)
        cbm_made = signal("cbm_made", B)
        xdt_made = signal("xdt_made", B)
        xd_made = signal("xd_made", B)
        yoff_raw = signal("yoff_raw", B)
        dst_raw = signal("dst_raw", B)
        ydiag_raw = signal("ydiag_raw", B)
        state_faded = signal("state_faded", B)
        state_made = signal("state_made", B)
        yg_made = signal("yg_made", B)
        ysum_made = signal("ysum_made", B)
        yg_turned = signal("yg_turned", B)
        gT_made = signal("gT_made", B)
        out0_raw = signal("out0_raw", B)
        dve_a1 = Chain(ctx, nc, "dve_a1", 2 + B * 8)
        lg_raw = signal("lg_raw", 1)
        lg_v = signal("lg_v", 1)
        lg_e = signal("lg_e", 1)
        lg_b = signal("lg_b", 1)
        la_made = signal("la_made", 1)
        cs_raw = signal("cs_raw", 1)
        le_made = signal("le_made", 1)
        qk_raw = signal("qk_raw", B)
        v_raw = signal("v_raw", B)
        v1_made = signal("v1_made", B)
        qneg_made = signal("qneg_made", B)
        qexp_made = signal("qexp_made", B)
        qs_made = signal("qs_made", B)
        qk_turned = signal("qk_turned", B)
        qkT_made = signal("qkT_made", B)
        qpar_made = signal("qpar_made", B)
        att_raw = signal("att_raw", B)
        am_made = signal("am_made", 4 * B)
        ly_raw = signal("ly_raw", B)
        lst_raw = signal("lst_raw", B)
        lst_made = signal("lst_made", B)
        ly_made = signal("ly_made", B)
        ly_turned = signal("ly_turned", B)
        lyT_made = signal("lyT_made", B)
        out2_raw = signal("out2_raw", B)
        dve_f = [Chain(ctx, nc, f"dve_f{y}", 13) for y in range(2)]
        logit_raw = [signal(f"logit_raw{y}", 1) for y in range(2)]
        rt_max = [signal(f"rt_max{y}", 1) for y in range(2)]
        rt_exp = [signal(f"rt_exp{y}", 1) for y in range(2)]
        top_diff = [signal(f"top_diff{y}", 1) for y in range(2)]
        top_tanh = [signal(f"top_tanh{y}", 1) for y in range(2)]
        gates_made = [signal(f"gates_made{y}", 1) for y in range(2)]
        gates_turned = [signal(f"gates_turned{y}", 1) for y in range(2)]
        gatesT_made = [signal(f"gatesT_made{y}", 1) for y in range(2)]
        lh_raw = [signal(f"lh_raw{y}", 1) for y in range(2)]
        gl_made = [signal(f"gl_made{y}", 1) for y in range(2)]
        gh_made = [signal(f"gh_made{y}", 1) for y in range(2)]
        hid_raw = [signal(f"hid_raw{y}", NT + 1) for y in range(2)]
        u_made = [signal(f"u_made{y}", NT + 1) for y in range(2)]
        exp_raw = [signal(f"exp_raw{y}", NE + 1) for y in range(2)]
        fo_made = [signal(f"fo_made{y}", NE + 1) for y in range(2)]
        fo_turned = [signal(f"fo_turned{y}", 1) for y in range(2)]
        foT_made = [signal(f"foT_made{y}", 1) for y in range(2)]
        outf_raw = [signal(f"outf_raw{y}", 2) for y in range(2)]
        res_made = [signal(f"res_made{g}", 1) for g in range(4)]

        def bc(ap, *shape):
            return ap.to_broadcast(list(shape))

        def alone(stage):
            for _ in stage:
                pass

        def beside(attn, ffn, ahead):
            for count in ahead:
                for _ in range(count):
                    next(ffn)
                next(attn)
            assert next(attn, None) is None
            alone(ffn)

        def walk(eng, attn0, ffn, attn1, start_ffn, setup_of=lambda y: iter(range(SETUP_SLOTS[y]))):
            beside(attn0(0), setup_of(0), SETUP_AHEAD0)
            start_ffn(1, 0)
            beside(attn0(1), ffn(0, 0, None), AHEAD0)
            beside(attn1(0), setup_of(1), SETUP_AHEAD1)
            start_ffn(1, 1)
            with eng.Fori(1, NBLK - 1) as i:
                beside(attn0(i + 1), ffn(0, i, (3, i - 1)), AHEAD0)
                beside(attn1(i), ffn(1, i - 1, (1, i + 1)), AHEAD1)
            alone(ffn(0, NBLK - 1, (3, NBLK - 2)))
            beside(attn1(NBLK - 1), ffn(1, NBLK - 2, None), AHEAD1)
            start_ffn(3, NBLK - 1)
            alone(ffn(1, NBLK - 1, None))

        block = ctx.enter_context(nc.Block())

        @block.sync
        def _(sp):
            sp.dma_start(c_t[:, :], dram["c_t"]).then_inc(loaded["small"], 16)
            sp.dma_start(mam_c[:, :], dram["mam_c"]).then_inc(loaded["small"], 16)
            sp.dma_start(rows[:, :], dram["rows"]).then_inc(loaded["small"], 16)
            for y in range(2):
                sp.dma_start(ffn_c[y][:, :], dram[f"ffn_c{y}"]).then_inc(loaded["small"], 16)
                sp.dma_start(b2rows[y][:, :], dram[f"b2rows{y}"]).then_inc(loaded["small"], 16)
            sp.dma_start(out_bias, dram["ub"]).then_inc(loaded["small"], 16)
            sp.dma_start(ub2, dram["ub2"]).then_inc(loaded["small"], 16)
            sp.dma_start(wmod[0][:, :], dram["wmod0"]).then_inc(loaded["mod0"], 16)
            sp.dma_start(v3(x_of[0], B), dram["x"][:, 0:P, :].rearrange("b t d -> t b d")).then_inc(x_in.sem, 16)
            sp.dma_start(w_in, dram["w_in"]).then_inc(loaded["w_in"], 16)
            sp.dma_start(w_out, dram["w_out"]).then_inc(loaded["w_out"], 16)
            sp.dma_start(wmod[1][:, :], dram["wmod1"]).then_inc(loaded["mod1"], 16)
            sp.dma_start(ffn_w[0][:, :], dram["ffn_w0"]).then_inc(loaded["ffn0"], 16)
            sp.dma_start(lin_w[:, :], dram["lin_w"]).then_inc(loaded["lin"], 16)

            def load_x(blk):
                wait_before(sp, copied[1], blk, B - 1)
                wait_before(sp, xn_made[1], blk, B - 1)
                sp.dma_start(v3(x_of[0], B), dram["x"][:, bass.ts(blk, P), :].rearrange("b t d -> t b d")
                             ).then_inc(x_in.sem, 16)

            def load_rope(blk):
                wait_before(sp, qs_made, blk, B - 1)
                sp.dma_start(rope, dram["rope"][bass.ts(blk, P), :].rearrange("t (a b) -> t a b", a=2)
                             ).then_inc(rope_in.sem, 16)

            def store(blk):
                sp.wait_ge(*x_done[4](blk, B - 1))
                sp.dma_start(out[:, bass.ts(blk, P), :].rearrange("b t d -> t b d"), v3(x_of[3], B)
                             ).then_inc(x_out.sem, 16)

            sp.sem_inc(x_out.sem, 16)
            sp.sem_inc(x_done[4].sem, B)
            load_rope(0)
            sp.wait_ge(set_pe, MOD_READ1)
            sp.dma_start(ffn_w[1][:, :], dram["ffn_w1"]).then_inc(loaded["ffn1"], 16)
            load_x(1)
            load_x(2)
            load_rope(1)
            with sp.Fori(2, NBLK - 1) as i:
                load_x(i + 1)
                load_rope(i)
                store(i - 2)
            load_rope(NBLK - 1)
            for blk in range(NBLK - 3, NBLK):
                store(blk)
            sp.wait_ge(x_out.sem, 16 * NBLK + 16)

        @block.gpsimd
        def _(pool):
            made = [0]

            def mask(t, rows_, cols, base, mult, pattern, op, fill, view=None):
                pool.affine_select(out=t, in_=t, compare_op=op, fill=fill, base=base,
                                   pattern=pattern, channel_multiplier=mult).then_inc(pool_chain, 1)
                made[0] += 1
                pool.wait_ge(pool_chain, made[0])

            def clear(t, value=0.0):
                pool.memset(t, value).then_inc(pool_chain, 1)
                made[0] += 1

            clear(ident[:, :])
            clear(upto[:, :], 1.0)
            clear(after[:, :], 1.0)
            clear(ones[:, :], 1.0)
            clear(block8[:, :], 1.0)
            clear(parity[:, :], 0.0)
            clear(eps_ln[:, :], 1e-05)
            clear(tails[:, :, :, :])
            for r in range(B):
                clear(state[r][:, :])
                clear(lst[r])
            clear(gates)
            clear(v1[:, :], 1.0)
            clear(gsel)
            clear(b2sel[:, :])
            for e in range(NE):
                clear(iota8[:, e:e + 1], float(e))
            pool.wait_ge(pool_chain, made[0])
            mask(ident[:, :], P, P, 0, 1, [[-1, P]], ALU.not_equal, 1.0)
            mask(upto[:, :], P, P, 0, -1, [[1, P]], ALU.is_ge, 0.0)
            mask(after[:, :], P, P, 0, 1, [[-1, P]], ALU.is_gt, 0.0)
            mask(block8[:, :], P, LG, 0, 1, [[-LD, LG]], ALU.is_ge, 0.0)
            mask(block8[:, :], P, LG, LD - 1, -1, [[LD, LG]], ALU.is_ge, 0.0)
            clear(gates[:, :, NE:GC], 1.0)
            clear(b2sel[:, NE:GC], 1.0)
            pool.wait_ge(pool_chain, made[0])
            mask(b2sel[:, NE:GC], GC, 1, -NE, 1, [[0, 1]], ALU.not_equal, 0.1)
            pool.memset(th[:, 0:1], 0.0).then_inc(masks_made, 1)
            pool.wait_ge(masks_made, 1)
            pool.wait_ge(loaded["small"], 16 * NSMALL)
            pool.tensor_tensor(out_bias, out_bias, v3(ub2, 3), ALU.add).then_inc(set_done, 1)
            pool.wait_ge(set_done, 1)

            def put_tail(blk, m):
                if m >= 2:
                    pool.wait_ge(*conv_made(blk, m - 2))
                else:
                    pool.wait_ge(*hT_made[0](blk, B - 1))
                wait_before(pool, tail_kept, blk, m)
                pool.tensor_tensor(raw[:, m % 2, :, 0:CONV - 1], tails[:, m, :, :], unit, ALU.mult
                                   ).then_inc(tail_put.sem, 1)

            def keep_tail(blk, m):
                pool.wait_ge(*tail_put(blk, m))
                pool.wait_ge(*xbc_in(blk, m))
                pool.tensor_tensor(tails[:, m, :, :], raw[:, m % 2, :, P:P + CONV - 1], unit, ALU.mult
                                   ).then_inc(tail_kept.sem, 1)

            unit = v3_(ones[:, 0:B * (CONV - 1)], B)

            def attn0(blk):
                for _ in range(3):
                    yield
                for m in range(XM):
                    put_tail(blk, m)
                    keep_tail(blk, m)
                    yield
                yield
                pool.wait_ge(*dtd_made(blk))
                pool.wait_ge(*xs_made(blk, XM - 1))
                for r in range(B):
                    h = slice(r * NH, (r + 1) * NH)
                    pool.wait_ge(*xt_made(blk, r))
                    if r:
                        pool.wait_ge(*dst_raw(blk, r - 1))
                        pool.wait_ge(*yg_made(blk, r - 1))
                    pool.tensor_tensor(v3(xdec, NH), v3(xt, NH), bc(dtd[:, h].unsqueeze(2), P, NH, HD),
                                       ALU.mult).then_inc(xdt_made.sem, 1)
                    pool.tensor_tensor(v3(xd, NH), v3(xt, NH),
                                       bc(rows[:, R_D:R_D + NH].unsqueeze(2), P, NH, HD),
                                       ALU.mult).then_inc(xd_made.sem, 1)
                    yield
                    if r:
                        yield
                        yield
                    yield
                    pool.wait_ge(*yoff_raw(blk, r))
                    pool.tensor_tensor(v3(state[r], NH), v3(state[r], NH),
                                       bc(v3(dec, 3)[:, 2, h].unsqueeze(2), P, NH, HD), ALU.mult
                                       ).then_inc(state_faded.sem, 1)
                    yield
                    yield
                yield
                yield

            def copy_with_bias(g, blk):
                pool.wait_ge(*x_done[g](blk, B - 1))
                if g < 3:
                    wait_before(pool, copied[g + 1], blk, B - 1)
                    wait_before(pool, xn_made[g + 1], blk, B - 1)
                else:
                    pool.wait_ge(x_out.sem, blk * 16 + 16)
                pool.tensor_tensor(v3(x_of[g], B), v3(gate_bc[g], B), bc(out_bias[:, g - 1:g, :], P, B, D),
                                   ALU.mult).then_inc(copied[g].sem, B // 2)
                pool.wait_ge(*copied[g](blk, B // 2 - 1))
                pool.tensor_tensor(x_of[g][:, :], x_of[g][:, :], x_in_of[g][:, :], ALU.add
                                   ).then_inc(copied[g].sem, B // 2)

            def attn1(blk):
                copy_with_bias(2, blk)
                for _ in range(len(AHEAD1)):
                    yield

            def ffn(y, blk, following):
                for k in range(len(FFN_SLOTS)):
                    if following and k == FFN_SLOTS.index("norm_rows"):
                        copy_with_bias(*following)
                    yield

            walk(pool, attn0, ffn, attn1, copy_with_bias)

        @block.scalar
        def _(act):
            act.wait_ge(loaded["small"], 16 * NSMALL)
            act.activation(c_s[:, :], c_t[:, :], ACT.Tanh, scale=0.5).then_inc(set_act, 1)
            act.activation(a_neg[:, :], rows[:, R_AL:R_AL + NH], ACT.Exp).then_inc(set_act, 1)
            act.wait_ge(set_dve, SET_ALL)
            act.wait_ge(masks_made, 1)

            def setup_of(y):
                for _ in range(SETUP_SLOTS[y] - 2):
                    yield
                if y:
                    act.wait_ge(set_dve, SET_SEL0)
                act.activation(gb1[:, :], ffn_c[y][:, C_B1:C_B1 + NT], ACT.Gelu).then_inc(set_act, 1)
                yield
                yield

            def norm(g, blk):
                s = g % 2
                bank = A if s == 0 else F
                act.wait_ge(*xn_turned[g](blk))
                for r in range(B):
                    for k in range(KD):
                        last = act.activation(hT[s][:, k, r * P:(r + 1) * P], bank[k][:, r * P:(r + 1) * P],
                                              ACT.Identity, scale=mod_c[g][:, 1, k, r:r + 1],
                                              bias=mod_c[g][:, 0, k, r:r + 1])
                    last.then_inc(hT_made[g].sem, 1)

            def attn0(blk):
                yield
                norm(0, blk)
                yield
                act.wait_ge(*dt_abs(blk))
                act.activation(dt_n[:, :], dt_n[:, :], ACT.Exp).then_inc(dt_exp.sem, 1)
                act.wait_ge(*dt_exp(blk))
                act.activation(dt_n[:, :], dt_n[:, :], ACT.Ln, bias=1.0).then_inc(dt_ln.sem, 1)
                yield

                def conv_tanh_of(m):
                    act.wait_ge(*conv_made(blk, m))
                    if m >= 2:
                        act.wait_ge(*xs_made(blk, m - 2))
                    act.activation(v3(th, 2)[:, m % 2, :], acc[m % 3], ACT.Tanh).then_inc(conv_tanh.sem, 1)

                for m in range(XM):
                    if m == 2:
                        act.wait_ge(*dec_raw(blk))
                        act.activation(dec[:, :], A[2][:, B * NH:4 * B * NH], ACT.Exp).then_inc(dec_made.sem, 1)
                    act.wait_ge(*xbc_raw(blk, m))
                    if m >= 2:
                        act.wait_ge(*conv_made(blk, m - 2))
                        act.wait_ge(*tail_kept(blk, m - 2))
                    act.activation(raw[:, m % 2, :, CONV - 1:], v3(A[(m + 3) % 4], B), ACT.Copy)
                    if m >= 3:
                        act.wait_ge(*xs_made(blk, m - 3))
                    act.activation(v3_(acc[m % 3], B), v3(A[(m + 3) % 4], B), ACT.Identity,
                                   scale=mam_c[:, C_CW + m * CONV + 3:C_CW + m * CONV + 4],
                                   bias=mam_c[:, C_CB + m:C_CB + m + 1]).then_inc(xbc_in.sem, 1)
                    if m:
                        conv_tanh_of(m - 1)
                    yield
                conv_tanh_of(XM - 1)
                yield

                def turned(r):
                    act.wait_ge(*xb_turned(blk, r))
                    if r:
                        act.wait_ge(*xd_made(blk, r - 1))
                    act.activation(xt[:, :], A[2][:, :], ACT.Copy)
                    act.activation(bt[:, :], A[3][:, 0:NS], ACT.Copy).then_inc(xt_made.sem, 1)
                    act.wait_ge(*z_raw(blk, r))
                    act.activation(tz[:, :], A[1][:, :], ACT.Tanh).then_inc(z_tanh.sem, 1)

                turned(0)
                yield
                for r in range(B):
                    act.wait_ge(*seg_raw(blk, 2 * r))
                    act.activation(seg[:, 0:512], A[0][:, :], ACT.Exp)
                    act.wait_ge(*seg_raw(blk, 2 * r + 1))
                    act.activation(seg[:, 512:1024], A[1][:, :], ACT.Exp).then_inc(seg_exp.sem, 1)
                    yield
                    yield
                    act.wait_ge(*yg_made(blk, r))
                    act.activation(gT[:, :], yg[:, :], ACT.Square, accum_out=yst[:, 0:1]
                                   ).then_inc(ysum_made.sem, 1)
                    yield
                    if r < B - 1:
                        turned(r + 1)
                        yield
                    act.wait_ge(*yg_turned(blk, r))
                    act.wait_ge(*ysum_made(blk, r))
                    act.activation(gT[:, :], A[0][:, :], ACT.Copy).then_inc(gT_made.sem, 1)
                    yield
                    yield

            def attn1(blk):
                yield
                norm(2, blk)
                yield
                act.wait_ge(*lg_v(blk))
                act.activation(lg[:, :], lg[:, :], ACT.Exp, scale=-1.0).then_inc(lg_e.sem, 1)
                act.wait_ge(*lg_b(blk))
                act.activation(la[:, :], la[:, :], ACT.Ln).then_inc(la_made.sem, 1)
                yield
                act.wait_ge(*cs_raw(blk))
                act.activation(le[:, 0, :, :], v3_(A[2][:, 64:128], B), ACT.Exp)
                act.activation(le[:, 1, :, :], v3_(A[2][:, 64:128], B), ACT.Exp, scale=-1.0)
                act.activation(le[:, 2, :, :], v3_(A[2][:, 128:192], B), ACT.Exp).then_inc(le_made.sem, 1)
                yield

                def values(r):
                    act.wait_ge(*v_raw(blk, r))
                    if r:
                        act.wait_ge(*ly_raw(blk, r - 1))
                        act.wait_ge(*lst_raw(blk, r - 1))
                    act.activation(v3(v1, LH)[:, :, 0:LD], v3_(A[1][:, 0:D], LH), ACT.Copy
                                   ).then_inc(v1_made.sem, 1)

                def q_exp(r):
                    act.wait_ge(*qneg_made(blk, r))
                    act.activation(qm[:, :], qm[:, :], ACT.Exp).then_inc(qexp_made.sem, 1)

                values(0)
                q_exp(0)
                yield
                for r in range(B):
                    act.wait_ge(*qk_turned(blk, r))
                    act.activation(qkT, v3_(A[0][:, :], 4), ACT.Copy).then_inc(qkT_made.sem, 1)
                    yield
                    yield
                    yield
                    if r < B - 1:
                        values(r + 1)
                        yield
                    act.wait_ge(*ly_turned(blk, r))
                    act.activation(lyT[:, :], A[2][:, 0:D], ACT.Copy).then_inc(lyT_made.sem, 1)
                    yield
                    if r < B - 1:
                        q_exp(r + 1)
                    yield

            def ffn(y, blk, following):
                for slot in FFN_SLOTS:
                    what, n = slot[0], slot[1:]
                    if slot == "down":
                        act.wait_ge(*lh_raw[y](blk))
                        act.activation(gl[:, :], F[3][:, :], ACT.Gelu, bias=ffn_c[y][:, C_DOWN:C_DOWN + 1]
                                       ).then_inc(gl_made[y].sem, 1)
                        act.activation(ghT, hT[1], ACT.Gelu).then_inc(gh_made[y].sem, 1)
                    elif what == "hidden":
                        for j in n:
                            act.wait_ge(*hid_raw[y](blk, j))
                            if j >= RING:
                                act.wait_ge(*exp_raw[y](blk, unit_of(j - RING)))
                            col = hidden_col(j)
                            act.activation(u[j % RING][:, :], F[j % 2][:, :], ACT.Gelu,
                                           bias=ffn_c[y][:, col:col + 1]).then_inc(u_made[y].sem, 1)
                    elif slot == ("out", 0, 0):
                        act.wait_ge(*rt_max[y](blk))
                        act.activation(rt[1][:, :], rt[0][:, :], ACT.Exp).then_inc(rt_exp[y].sem, 1)
                    elif slot == ("out", 0, B - 1):
                        act.wait_ge(*top_diff[y](blk))
                        act.activation(rm[2][:, :], rm[1][:, :], ACT.Tanh, scale=0.5).then_inc(top_tanh[y].sem, 1)
                    elif slot == "gates":
                        act.wait_ge(*gates_turned[y](blk))
                        act.activation(gatesT[:, :], F[0][0:GC, :], ACT.Copy).then_inc(gatesT_made[y].sem, 1)
                    elif slot == "turn_next" and following:
                        norm(*following)
                    elif slot == "turn":
                        act.wait_ge(*fo_turned[y](blk))
                        act.activation(foT[:, :], F[2][:, :], ACT.Copy).then_inc(foT_made[y].sem, 1)
                    yield

            walk(act, attn0, ffn, attn1, norm, setup_of)

        @block.vector
        def _(dve):
            made = [0]

            def setup(ins):
                made[0] += 1
                ins.then_inc(set_dve, 1)
                dve.wait_ge(set_dve, made[0])

            dve.wait_ge(masks_made, 1)
            dve.wait_ge(set_act, 1)
            setup(dve.tensor_scalar(c_t[:, :], c_t[:, :], 0.5, None, ALU.mult))
            setup(dve.scalar_tensor_tensor(c_s[:, :], c_s[:, :], 1.0, c_t[:, :], ALU.add, ALU.mult))
            assert made[0] == SET_C

            def modulation(y):
                setup(dve.tensor_copy(c_rep.rearrange("p (a b) -> p a b", a=KD * B),
                                      bc(v3(c_s, 2)[:, y, :].unsqueeze(2), P, KD * B, P)))
                assert made[0] == (SET_REP0, SET_REP1)[y]
                dve.wait_ge(set_pe, (MODC0, MODC1)[y])
                for s in range(2):
                    src = F[1][:, 16 * s:16 * s + 16].rearrange("p (w k b) -> p w k b", w=2, k=KD)
                    setup(dve.tensor_copy(mod_c[2 * y + s][:, 0, :, :], src[:, 0, :, :]))
                    setup(dve.tensor_scalar(mod_c[2 * y + s][:, 1, :, :], src[:, 1, :, :], 1.0, None, ALU.add))
                yield
                for s in range(2):
                    for h in range(2):
                        n = 2 * s + h
                        dve.wait_ge(set_pe, (MODC0, MODC1)[y] + 1 + n)
                        gb = gate_bc[2 * y + s][:, h * 2 * D:(h + 1) * 2 * D]
                        src = F[2 + h][:, :]
                        sign = u[4]
                        setup(dve.tensor_scalar(sign, src, 0.0, 2.0, ALU.is_ge, ALU.mult))
                        setup(dve.tensor_scalar(sign, sign, -1.0, None, ALU.add))
                        setup(dve.tensor_tensor(gb, sign, src, ALU.mult))
                        setup(dve.scalar_tensor_tensor(gb, gb, 0.25, sign, ALU.max, ALU.mult))
                        yield

            alone(modulation(0))
            dve.wait_ge(set_act, 2)
            setup(dve.tensor_scalar(a_neg[:, :], a_neg[:, :], -1.0, None, ALU.mult))
            for y in range(2):
                setup(dve.tensor_tensor(router_bias[y][:, :], rows[:, R_RB + 8 * y:R_RB + 8 * y + 8],
                                        rows[:, R_COST:R_COST + 8], ALU.subtract))
            setup(dve.tensor_scalar(mam_c[:, 0:C_NW], mam_c[:, 0:C_NW], 0.5, None, ALU.mult))
            dve.wait_ge(loaded["w_in"], 16)
            setup(dve.tensor_scalar(w_in[:, :, 0:DI], w_in[:, :, 0:DI], 0.5, None, ALU.mult))
            dve.wait_ge(loaded["w_out"], 16)
            for k in range(DI // P):
                setup(dve.tensor_scalar(w_out[:, k, :], w_out[:, k, :], mam_c[:, C_NW + k:C_NW + k + 1],
                                        None, ALU.mult))
            for y in range(2):
                setup(dve.tensor_reduce(parity[:, y:y + 1], v3(block8, LG // 2)[:, :, y], AX_X, ALU.add))
            assert made[0] == SET_ALL
            dve.wait_ge(set_done, 1)

            def setup_of(y):
                if y == 0:
                    yield from modulation(1)
                dve.wait_ge(loaded[f"ffn{y}"], 16)
                dve.wait_ge(set_act, 3 + y)
                if y:
                    dve.wait_ge(set_pe, CONST_READ0)
                for e in range(NE):
                    j = slice(FIRST[e], FIRST[e] + TILES[e])
                    setup(dve.tensor_scalar(gsel[:, j, e:e + 1], gb1[:, j].unsqueeze(2), -1.0, None, ALU.mult))
                setup(dve.tensor_copy(gsel[:, :, NE:GC], gb1[:, :].unsqueeze(2)))
                setup(dve.tensor_scalar(ffn_w[y][:, W_S2:W_S2 + L], ffn_w[y][:, W_S2:W_S2 + L], 0.1,
                                        None, ALU.mult))
                assert made[0] == (SET_SEL0, SET_SEL1)[y]
                yield
                dve.wait_ge(set_pe, (CONST_DONE0, CONST_DONE1)[y])
                setup(dve.tensor_copy(cw[y][:, :], F[0][0:GC, 0:L]))
                yield

            def carry_wait():
                dve.memset(spare[:, 0:1], 0.0)

            def rsqrt(blk, chain, y, v, tmp):
                yi, vi = y.bitcast(I32), v.bitcast(I32)
                chain.step(dve, blk, dve.tensor_scalar(yi, vi, 1, None, ALU.logical_shift_right))
                chain.step(dve, blk, dve.tensor_scalar(yi, yi, -1.0, float(0x5F3759DF), ALU.mult, ALU.add))
                for three in (3.0, 12.0, 768.0):
                    if y.shape[-1] == 1:
                        chain.step(dve, blk, dve.tensor_scalar(tmp, y, y, v, ALU.mult, ALU.mult))
                    else:
                        chain.step(dve, blk, dve.tensor_tensor(tmp, y, y, ALU.mult))
                        chain.step(dve, blk, dve.tensor_tensor(tmp, tmp, v, ALU.mult))
                    chain.step(dve, blk, dve.scalar_tensor_tensor(y, tmp, -three, y, ALU.add, ALU.mult))

            def norm(g, blk):
                norm_sums(g, blk)
                norm_root(g, blk)
                norm_rows(g, blk)

            def norm_sums(g, blk):
                s, chain = g % 2, dve_n[g]
                xg = v3(x_in_of[g], B)
                if g == 0:
                    dve.wait_ge(x_in.sem, blk * 16 + 16)
                else:
                    dve.wait_ge(*x_done[g](blk, B - 1))
                for r in range(B):
                    last = dve.bn_stats(v3(stats[s], B)[:, r, :], xg[:, r, :])
                chain.step(dve, blk, last)
                carry_wait()
                for r in range(B):
                    last = dve.bn_aggr(v3(mv[s], B)[:, r, :], v3(stats[s], B)[:, r, :])
                chain.step(dve, blk, last)
                chain.step(dve, blk, dve.tensor_scalar(var_e[s][:, :], v3(mv[s], B)[:, :, 1], 1e-05, None, ALU.add))

            def norm_root(g, blk):
                s, chain = g % 2, dve_n[g]
                rsqrt(blk, chain, rstd[s][:, :], var_e[s][:, :], rtmp[s][:, :])
                chain.step(dve, blk, dve.tensor_scalar(rstd[s][:, :], rstd[s][:, :], 1 / RSQRT_SCALE, None,
                                                       ALU.mult))

            def norm_rows(g, blk):
                s, chain = g % 2, dve_n[g]
                xg = v3(x_in_of[g], B)
                for r in range(B):
                    dve.tensor_scalar(v3(xn[s], B)[:, r, :], xg[:, r, :], v3(mv[s], B)[:, r, 0:1],
                                      rstd[s][:, r:r + 1], ALU.subtract, ALU.mult).then_inc(xn_made[g].sem, 1)
                chain.close()

            def residual(g, blk, bank, cols, r, n, tmp, chain):
                w = slice(r * D, (r + n) * D)
                chain.step(dve, blk, dve.tensor_tensor(tmp, bank[:, cols], gate_bc[g][:, w], ALU.mult))
                dve.tensor_tensor(x_of[g][:, w], x_of[g][:, w], tmp, ALU.add).then_inc(x_done[g + 1].sem, n)

            def attn0(blk):
                c = dve_a0
                norm(0, blk)
                yield
                yield
                dve.wait_ge(*dt_raw(blk))
                c.step(dve, blk, dve.tensor_tensor(v3(dt_v, B), v3_(A[2][:, 0:B * NH], B),
                                                   bc(rows[:, R_DT:R_DT + NH].unsqueeze(1), P, B, NH), ALU.add))
                dve.scalar_tensor_tensor(dt_n[:, :], dt_v[:, :], -1.0, dt_v[:, :], ALU.mult, ALU.min
                                         ).then_inc(dt_abs.sem, 1)
                yield
                for m in range(XM):
                    if m == 1:
                        dve.wait_ge(*dt_ln(blk))
                        c.step(dve, blk, dve.scalar_tensor_tensor(dt_s[:, :], dt_v[:, :], 0.0, dt_n[:, :],
                                                                  ALU.max, ALU.add))
                        dve.tensor_tensor(v3(dA, B), v3(dt_s, B), bc(a_neg[:, :].unsqueeze(1), P, B, NH),
                                          ALU.mult).then_inc(dA_made.sem, 1)
                    if m == 3:
                        dve.wait_ge(*dec_made(blk))
                        dve.tensor_tensor(dtd[:, :], dt_s[:, :], v3(dec, 3)[:, 0, :], ALU.mult
                                          ).then_inc(dtd_made.sem, 1)
                    dve.wait_ge(*xbc_in(blk, m))
                    dve.wait_ge(*tail_put(blk, m))
                    o = v3_(acc[m % 3], B)
                    src = raw[:, m % 2, :, :]
                    w = [mam_c[:, C_CW + m * CONV + k:C_CW + m * CONV + k + 1] for k in range(CONV - 1)]
                    for k in (0, 1):
                        c.step(dve, blk, dve.scalar_tensor_tensor(o, src[:, :, k:k + P], w[k], o,
                                                                  ALU.mult, ALU.add))
                    dve.scalar_tensor_tensor(o, src[:, :, 2:2 + P], w[2], o, ALU.mult, ALU.add
                                             ).then_inc(conv_made.sem, 1)
                    if m:
                        silu(blk, m - 1)
                    yield
                silu(blk, XM - 1)
                yield

                def decays(r):
                    h = slice(r * NH, (r + 1) * NH)
                    dve.wait_ge(*dA_made(blk))
                    if r:
                        dve.wait_ge(*seg_raw(blk, 2 * r - 1))
                    else:
                        dve.wait_ge(*tail_kept(blk, XM - 1))
                    dve.tensor_tensor(v3(va, NH), bc(upto[:, :].unsqueeze(1), P, NH, P),
                                      bc(dA[:, h].unsqueeze(2), P, NH, P), ALU.mult).then_inc(va_made.sem, 1)

                def turned(r):
                    h = slice(r * NH, (r + 1) * NH)
                    dve.wait_ge(*z_tanh(blk, r))
                    dve.scalar_tensor_tensor(sz[:, :], tz[:, :], 1.0, A[1][:, :], ALU.add, ALU.mult
                                             ).then_inc(sz_made.sem, 1)
                    dve.wait_ge(*xt_made(blk, r))
                    dve.tensor_tensor(cbm[:, :], A[3][:, NS:2 * NS], upto[:, :], ALU.mult).then_inc(cbm_made.sem, 1)
                    dve.tensor_tensor(v3(xdt, NH), v3(xt, NH), bc(dt_s[:, h].unsqueeze(2), P, NH, HD), ALU.mult)

                decays(0)
                turned(0)
                yield
                for r in range(B):
                    h = slice(r * NH, (r + 1) * NH)
                    dve.wait_ge(*cbm_made(blk, r))
                    dve.wait_ge(*seg_exp(blk, r))
                    dve.tensor_tensor(v3(seg, NH), v3(seg, NH), bc(cbm[:, :].unsqueeze(1), P, NH, P), ALU.mult
                                      ).then_inc(mh_made.sem, 1)
                    yield
                    dve.wait_ge(*yoff_raw(blk, r))
                    c.step(dve, blk, dve.tensor_tensor(v3(yg, NH), v3_(A[0][:, :], NH),
                                                       bc(v3(dec, 3)[:, 1, h].unsqueeze(2), P, NH, HD), ALU.mult))
                    dve.wait_ge(*xd_made(blk, r))
                    c.step(dve, blk, dve.tensor_tensor(yg[:, :], yg[:, :], xd[:, :], ALU.add))
                    yield
                    dve.wait_ge(*ydiag_raw(blk, r))
                    c.step(dve, blk, dve.tensor_tensor(yg[:, :], yg[:, :], A[2][:, :], ALU.add))
                    dve.tensor_tensor(yg[:, :], yg[:, :], sz[:, :], ALU.mult).then_inc(yg_made.sem, 1)
                    dve.wait_ge(*state_faded(blk, r))
                    dve.wait_ge(*dst_raw(blk, r))
                    dve.tensor_tensor(state[r][:, :], state[r][:, :], A[1][:, :], ALU.add
                                      ).then_inc(state_made.sem, 1)
                    if r < B - 1:
                        decays(r + 1)
                    yield
                    if r < B - 1:
                        turned(r + 1)
                        yield
                    dve.wait_ge(*ysum_made(blk, r))
                    c.step(dve, blk, dve.tensor_scalar(yst[:, 0:1], yst[:, 0:1], 1.0 / DI, 1e-05, ALU.mult, ALU.add))
                    rsqrt(blk, c, yst[:, 2:3], yst[:, 0:1], yst[:, 1:2])
                    yield
                    dve.wait_ge(*out0_raw(blk, r))
                    c.step(dve, blk, dve.tensor_scalar(res_a[:, :], A[3][:, 2 * NS:2 * NS + D], yst[:, 2:3],
                                                       1 / RSQRT_SCALE, ALU.mult, ALU.mult))
                    c.step(dve, blk, dve.tensor_tensor(res_a[:, :], res_a[:, :], A[2][:, 0:D], ALU.add))
                    w = slice(r * D, (r + 1) * D)
                    c.step(dve, blk, dve.tensor_tensor(res_a[:, :], res_a[:, :], gate_bc[0][:, w], ALU.mult))
                    dve.tensor_tensor(x_of[0][:, w], x_of[0][:, w], res_a[:, :], ALU.add).then_inc(x_done[1].sem, 1)
                    yield
                c.close()

            def silu(blk, m):
                dve.wait_ge(*conv_tanh(blk, m))
                dve.scalar_tensor_tensor(xs[:, m, :], v3(th, 2)[:, m % 2, :], 1.0, acc[m % 3],
                                         ALU.add, ALU.mult).then_inc(xs_made.sem, 1)

            def attn1(blk):
                c = dve_a1
                norm(2, blk)
                yield
                yield
                dve.wait_ge(*lg_raw(blk))
                dve.tensor_tensor(v3(lg, B), v3_(A[2][:, 0:B * LH], B),
                                  bc(rows[:, R_BG:R_BG + LH].unsqueeze(1), P, B, LH), ALU.add
                                  ).then_inc(lg_v.sem, 1)
                dve.wait_ge(*lg_e(blk))
                c.step(dve, blk, dve.tensor_scalar(la[:, :], lg[:, :], 1.0, None, ALU.add))
                c.step(dve, blk, dve.reciprocal(la[:, :], la[:, :]))
                dve.tensor_scalar(la[:, :], la[:, :], 0.8, 0.9995, ALU.max, ALU.min).then_inc(lg_b.sem, 1)
                yield
                dve.wait_ge(*le_made(blk))
                dve.wait_ge(rope_in.sem, blk * 16 + 16)
                yield

                def turn_qk(r):
                    dve.wait_ge(*qk_raw(blk, r))
                    half = LD // 2
                    both = A[0][:, :].rearrange("p (h t e) -> p (h t) e", t=2, e=half)
                    cos = bc(rope[:, 0, :].unsqueeze(1), P, 4 * LH, half)
                    sin = bc(rope[:, 1, :].unsqueeze(1), P, 4 * LH, half)
                    dve.tensor_tensor(v3(qr1, 4 * LH), both, cos, ALU.mult)
                    c.step(dve, blk, dve.tensor_tensor(v3(qr2, 4 * LH), both, sin, ALU.mult))
                    t1, t2, o = (v4(t, 2 * LH, 2) for t in (qr1, qr2, qk))
                    dve.tensor_tensor(o[:, :, 0, :], t1[:, :, 0, :], t2[:, :, 1, :], ALU.subtract)
                    c.step(dve, blk, dve.tensor_tensor(o[:, :, 1, :], t2[:, :, 0, :], t1[:, :, 1, :], ALU.add))
                    dve.tensor_scalar(qm[:, :], qk[:, :], 0.0, None, ALU.min).then_inc(qneg_made.sem, 1)

                def scale_qk(r):
                    dve.wait_ge(*qexp_made(blk, r))
                    c.step(dve, blk, dve.scalar_tensor_tensor(qk[:, :], qk[:, :], 0.0, qm[:, :], ALU.max, ALU.add))
                    for n in range(2):
                        q = slice(n * D, (n + 1) * D)
                        last = dve.tensor_tensor(v3_(qk[:, q], LH), v3_(qk[:, q], LH),
                                                 bc(le[:, n, r, :].unsqueeze(2), P, LH, LD), ALU.mult)
                    last.then_inc(qs_made.sem, 1)

                turn_qk(0)
                scale_qk(0)
                yield
                for r in range(B):
                    dve.wait_ge(*qkT_made(blk, r))
                    for n in range(2):
                        last = dve.tensor_tensor(qpar[:, n, :, :], bc(qkT[:, n, :].unsqueeze(1), P, 2, P),
                                                 bc(parity[:, :].unsqueeze(2), P, 2, P), ALU.mult)
                    last.then_inc(qpar_made.sem, 1)
                    c.step(dve, blk, dve.tensor_tensor(v3(lbt, 2), v3_(le[:, 2, r, :], 2),
                                                       bc(block8[:, :].unsqueeze(1), P, 2, LG), ALU.mult))
                    yield
                    dve.wait_ge(*att_raw(blk, r))
                    for k in range(4):
                        dve.tensor_tensor(v3(am[k], 4), v3_(A[k][:, :], 4),
                                          bc(upto[:, :].unsqueeze(1), P, 4, P), ALU.mult).then_inc(am_made.sem, 1)
                    yield
                    dve.wait_ge(*ly_raw(blk, r))
                    num = A[0][:, 0:LH * EXT].rearrange("p (h e) -> p h e", h=LH)
                    c.step(dve, blk, dve.tensor_scalar(lden[:, :].unsqueeze(2), num[:, :, LD:EXT], 1e-06, None, ALU.add))
                    c.step(dve, blk, dve.reciprocal(lden[:, :], lden[:, :]))
                    dve.tensor_tensor(v3(ly, LH), num[:, :, 0:LD], bc(lden[:, :].unsqueeze(2), P, LH, LD),
                                      ALU.mult).then_inc(ly_made.sem, 1)
                    dve.wait_ge(*lst_raw(blk, r))
                    sums = A[1][:, 0:2 * LG * EXT]
                    c.step(dve, blk, dve.tensor_tensor(v3(ltm, 2), lst[r], v3_(sums, 2), ALU.add))
                    dve.tensor_tensor(lst[r].rearrange("p g (h e) -> p (g h) e", e=EXT), v3(ltm, 2 * LG),
                                      bc(lbt[:, :].unsqueeze(2), P, 2 * LG, EXT), ALU.mult).then_inc(lst_made.sem, 1)
                    yield
                    if r < B - 1:
                        turn_qk(r + 1)
                        yield
                    yield
                    if r < B - 1:
                        scale_qk(r + 1)
                    dve.wait_ge(*out2_raw(blk, r))
                    if r == 0:
                        dve.wait_ge(*copied[2](blk, B - 1))
                    residual(2, blk, A[3], slice(0, D), r, 1, res_a[:, :], c)
                    yield
                c.close()

            def ffn(y, blk, following):
                g, c = 1 + 2 * y, dve_f[y]
                e3, p3 = v3(rt[0], B), v3(rt[1], B)

                def logits():
                    dve.wait_ge(*logit_raw[y](blk))
                    c.step(dve, blk, dve.tensor_tensor(e3, v3_(F[2][:, 0:B * NE], B),
                                                       bc(router_bias[y][:, :].unsqueeze(1), P, B, NE), ALU.add))
                    c.step(dve, blk, dve.tensor_reduce(rm[0][:, :], e3, AX_X, ALU.max))
                    dve.tensor_tensor(e3, e3, bc(rm[0][:, :].unsqueeze(2), P, B, NE), ALU.subtract
                                      ).then_inc(rt_max[y].sem, 1)

                def top_two():
                    dve.wait_ge(*rt_exp[y](blk))
                    c.step(dve, blk, dve.tensor_reduce(rm[0][:, :], p3, AX_X, ALU.add))
                    c.step(dve, blk, dve.reciprocal(rm[0][:, :], rm[0][:, :]))
                    c.step(dve, blk, dve.tensor_tensor(p3, p3, bc(rm[0][:, :].unsqueeze(2), P, B, NE), ALU.mult))
                    carry_wait()
                    for r in range(B):
                        last = dve.max(p8[:, r, :], p3[:, r, :])
                    c.step(dve, blk, last)
                    dve.tensor_tensor(rm[1][:, :], p8[:, :, 1], p8[:, :, 0], ALU.subtract
                                      ).then_inc(top_diff[y].sem, 1)
                    for r in range(B):
                        last = dve.max_index(i8[:, r, :], p8[:, r, :], p3[:, r, :])
                    c.step(dve, blk, last)
                    c.step(dve, blk, dve.tensor_copy(i8f, i8[:, :, 0:2]))

                def make_gates():
                    dve.wait_ge(*top_tanh[y](blk))
                    dve.tensor_scalar(g2[:, :, 0], rm[2][:, :], -0.5, 0.5, ALU.mult, ALU.add)
                    c.step(dve, blk, dve.tensor_scalar(g2[:, :, 1], rm[2][:, :], 0.5, 0.5, ALU.mult, ALU.add))
                    for n, t in ((0, rt[0]), (1, rt[2])):
                        last = dve.tensor_tensor(v3(t, B), bc(iota8[:, :].unsqueeze(1), P, B, NE),
                                                 bc(i8f[:, :, n:n + 1], P, B, NE), ALU.is_equal)
                    c.step(dve, blk, last)
                    for n, t in ((0, rt[0]), (1, rt[2])):
                        last = dve.tensor_tensor(v3(t, B), v3(t, B), bc(g2[:, :, n:n + 1], P, B, NE), ALU.mult)
                    c.step(dve, blk, last)
                    dve.tensor_tensor(gates[:, :, 0:NE], e3, v3(rt[2], B), ALU.add).then_inc(gates_made[y].sem, 1)

                def weigh(n):
                    dve.wait_ge(*exp_raw[y](blk, n))
                    if n == 0:
                        dve.wait_ge(*gates_made[y](blk))
                    else:
                        dve.wait_ge(*fo_made[y](blk, n - 1))
                    e, src = UNITS[n], F[2 + n % 2]
                    if e == SHARED:
                        dve.tensor_tensor(fo[:, :], fo[:, :], src[:, :], ALU.add).then_inc(fo_made[y].sem, 1)
                        return
                    for r in range(B):
                        w = slice(r * L, (r + 1) * L)
                        if n == 0:
                            last = dve.tensor_scalar(fo[:, w], src[:, w], gates[:, r, e:e + 1], None, ALU.mult)
                        else:
                            last = dve.scalar_tensor_tensor(fo[:, w], src[:, w], gates[:, r, e:e + 1],
                                                            fo[:, w], ALU.mult, ALU.add)
                    last.then_inc(fo_made[y].sem, 1)

                weighed = 0
                for k, slot in enumerate(FFN_SLOTS):
                    if k and FFN_SLOTS[k - 1][0] == "out" and FFN_SLOTS[k - 1][2] == B - 1:
                        n = FFN_SLOTS[k - 1][1]
                        if n == 0:
                            make_gates()
                        weigh(n)
                    if slot == ("hidden", 2, 3):
                        logits()
                    elif slot == ("out", 0, 1):
                        top_two()
                    elif slot == "norm_sums" and following:
                        norm_sums(*following)
                    elif slot == "norm_root" and following:
                        norm_root(*following)
                    elif slot == "norm_rows" and following:
                        norm_rows(*following)
                    elif slot == "up":
                        for n in range(2):
                            dve.wait_ge(*outf_raw[y](blk, n))
                            if n == 0:
                                dve.wait_ge(*copied[g](blk, B - 1))
                            residual(g, blk, F[n], slice(0, 2 * D), 2 * n, 2, res_f[n][:, :], c)
                    yield
                c.close()

            walk(dve, attn0, ffn, attn1, norm, setup_of)

        @block.tensor
        def _(pe):
            made = [0]

            def setup(ins):
                made[0] += 1
                ins.then_inc(set_pe, 1)

            def modulation(y):
                pe.wait_ge(loaded[f"mod{y}"], 16)
                pe.wait_ge(set_dve, (SET_REP0, SET_REP1)[y])
                wm = v3_(wmod[y][:, :], KD)
                cs = v3(c_s, 2)[:, y, :].rearrange("p (k b) -> p k b", k=KD)
                for s in range(2):
                    for w in range(2):
                        for kh in range(KD):
                            o = 16 * s + 8 * w + B * kh
                            c0 = (3 * s + w) * D + kh * P
                            for k in range(KD):
                                last = pe.matmul(F[1][:, o:o + B], wm[:, k, c0:c0 + P], cs[:, k, :],
                                                 start=(k == 0), stop=(k == KD - 1))
                setup(last)
                yield
                rep = c_rep.rearrange("p (k b t) -> p k b t", k=KD, b=B)
                for s in range(2):
                    for h in range(2):
                        if s:
                            pe.wait_ge(set_dve, (SET_REP0, SET_REP1)[y] + 4 + 4 * (h + 1))
                        for b in range(2):
                            for k in range(KD):
                                last = pe.matmul(F[2 + h][:, b * D:(b + 1) * D], rep[:, k, 2 * h + b, :],
                                                 wm[:, k, (3 * s + 2) * D:(3 * s + 3) * D],
                                                 start=(k == 0), stop=(k == KD - 1))
                        setup(last)
                        yield
                assert made[0] == (MOD_READ0, MOD_READ1)[y]

            alone(modulation(0))
            pe.wait_ge(set_dve, SET_ALL)

            def setup_of(y):
                if y == 0:
                    yield from modulation(1)
                yield
                pe.wait_ge(set_dve, (SET_SEL0, SET_SEL1)[y])
                for j in range(NT):
                    last = pe.matmul(F[0][0:GC, 0:L], gsel[:, j, :], ffn_w[y][:, W_E2 + j * L:W_E2 + (j + 1) * L],
                                     start=(j == 0), stop=False)
                setup(last)
                setup(pe.matmul(F[0][0:GC, 0:L], b2sel[:, :], b2rows[y][:, :], start=False, stop=True))
                assert made[0] == (CONST_DONE0, CONST_DONE1)[y]
                pe.wait_ge(set_dve, (SET_SEL0, SET_SEL1)[y] + 1)
                if y == 0:
                    pe.wait_ge(loaded["lin"], 16)
                yield

            def norm(g, blk):
                s = g % 2
                bank = A if s == 0 else F
                for r in range(B):
                    pe.wait_ge(*xn_made[g](blk, r))
                    for k in range(KD):
                        last = pe.transpose(bank[k][:, r * P:(r + 1) * P], v3(xn[s], B)[:, r, k * P:(k + 1) * P],
                                            ident[:, :])
                last.then_inc(xn_turned[g].sem, 1)

            def over_d(dst, lhs, rhs):
                for k in range(KD):
                    last = pe.matmul(dst, lhs(k), rhs(k), start=(k == 0), stop=(k == KD - 1))
                return last

            def attn0(blk):
                yield
                norm(0, blk)
                yield
                h = hT[0]
                for r in range(B):
                    pe.wait_ge(*hT_made[0](blk, r))
                    last = over_d(A[2][:, r * NH:(r + 1) * NH], lambda k: h[:, k, r * P:(r + 1) * P],
                                  lambda k: w_in[:, k, DIN - NH:DIN])
                last.then_inc(dt_raw.sem, 1)
                yield
                for m in range(XM):
                    if m == 2:
                        pe.wait_ge(*dA_made(blk))
                        for n, a in enumerate((after, upto, ones)):
                            last = pe.matmul(A[2][:, (1 + n) * B * NH:(2 + n) * B * NH], a[:, :], dA[:, :],
                                             start=True, stop=True)
                        last.then_inc(dec_raw.sem, 1)
                    if m == 3:
                        pe.wait_ge(*dec_made(blk))
                    if m >= 4:
                        pe.wait_ge(*xbc_in(blk, m - 4))
                    over_d(A[(m + 3) % 4][:, :], lambda k: w_in[:, k, DI + m * P:DI + (m + 1) * P],
                           lambda k: h[:, k, :]).then_inc(xbc_raw.sem, 1)
                    yield
                yield
                pe.wait_ge(*xs_made(blk, XM - 1))

                def turned(r):
                    t = slice(r * P, (r + 1) * P)
                    if r:
                        pe.wait_ge(*yg_made(blk, r - 1))
                    if r >= 2:
                        pe.wait_ge(*x_done[1](blk, r - 2))
                    for m in range(4):
                        pe.transpose(A[2][:, m * P:(m + 1) * P], xs[:, m, t], ident[:, :])
                    pe.transpose(A[3][:, 0:NS], xs[:, 4, t], ident[:, :])
                    pe.matmul(A[3][:, NS:2 * NS], xs[:, 4, t], xs[:, 5, t], start=True, stop=True
                              ).then_inc(xb_turned.sem, 1)
                    if r:
                        pe.wait_ge(*state_made(blk, r - 1))
                    over_d(A[1][:, :], lambda k: h[:, k, t], lambda k: w_in[:, k, 0:DI]).then_inc(z_raw.sem, 1)

                turned(0)
                yield
                for r in range(B):
                    t = slice(r * P, (r + 1) * P)
                    pe.wait_ge(*va_made(blk, r))
                    for k in range(2):
                        if k:
                            pe.wait_ge(*sz_made(blk, r))
                        pe.matmul(A[k][:, :], after[:, :], va[:, k * 512:(k + 1) * 512], start=True, stop=True
                                  ).then_inc(seg_raw.sem, 1)
                    yield
                    pe.wait_ge(*seg_exp(blk, r))
                    wait_before(pe, state_made, blk, r)
                    pe.matmul(A[0][:, :], xs[:, 5, t], state[r][:, :], start=True, stop=True
                              ).then_inc(yoff_raw.sem, 1)
                    pe.wait_ge(*xdt_made(blk, r))
                    pe.matmul(A[1][:, :], bt[:, :], xdec[:, :], start=True, stop=True).then_inc(dst_raw.sem, 1)
                    yield
                    pe.wait_ge(*mh_made(blk, r))
                    if r:
                        pe.wait_ge(*x_done[1](blk, r - 1))
                    for q in range(NH):
                        last = pe.matmul(A[2][:, q * HD:(q + 1) * HD], v3(seg, NH)[:, q, :],
                                         xdt[:, q * HD:(q + 1) * HD], start=True, stop=True)
                    last.then_inc(ydiag_raw.sem, 1)
                    yield
                    if r < B - 1:
                        turned(r + 1)
                        yield
                    pe.wait_ge(*yg_made(blk, r))
                    for m in range(4):
                        last = pe.transpose(A[0][:, m * P:(m + 1) * P], yg[:, m * P:(m + 1) * P], ident[:, :])
                    last.then_inc(yg_turned.sem, 1)
                    yield
                    pe.wait_ge(*gT_made(blk, r))
                    if r < B - 1:
                        pe.wait_ge(*xt_made(blk, r + 1))
                        pe.wait_ge(*cbm_made(blk, r + 1))
                    else:
                        pe.wait_ge(*x_done[1](blk, r - 1))
                    o = A[3][:, 2 * NS:2 * NS + D]
                    for m in range(4):
                        pe.matmul(o, gT[:, m * P:(m + 1) * P], w_out[:, m, :], start=(m == 0), stop=(m == 3))
                    for k in range(KD):
                        last = pe.matmul(A[2][:, k * P:(k + 1) * P], h[:, k, t], ident[:, :], start=True, stop=True)
                    last.then_inc(out0_raw.sem, 1)
                    yield

            def attn1(blk):
                yield
                norm(2, blk)
                yield
                h = hT[0]
                wq = v3_(lin_w[:, W_QK:W_V], KD)
                wv = v3_(lin_w[:, W_V:W_G], KD)
                wg = v3_(lin_w[:, W_G:W_O], KD)
                wo = v3_(lin_w[:, W_O:W_LIN], KD)
                for r in range(B):
                    pe.wait_ge(*hT_made[2](blk, r))
                    last = over_d(A[2][:, r * LH:(r + 1) * LH], lambda k: h[:, k, r * P:(r + 1) * P],
                                  lambda k: wg[:, k, :])
                last.then_inc(lg_raw.sem, 1)
                yield
                pe.wait_ge(*la_made(blk))
                for n, m in enumerate((upto, ones)):
                    last = pe.matmul(A[2][:, (1 + n) * 64:(2 + n) * 64], m[:, :], la[:, :], start=True, stop=True)
                last.then_inc(cs_raw.sem, 1)
                yield
                pe.wait_ge(*le_made(blk))

                def project(r):
                    t = slice(r * P, (r + 1) * P)
                    if r:
                        pe.wait_ge(*ly_made(blk, r - 1))
                        pe.wait_ge(*lst_made(blk, r - 1))
                    over_d(A[0][:, :], lambda k: h[:, k, t], lambda k: wq[:, k, :]).then_inc(qk_raw.sem, 1)
                    over_d(A[1][:, 0:D], lambda k: h[:, k, t], lambda k: wv[:, k, :]).then_inc(v_raw.sem, 1)

                project(0)
                yield
                for r in range(B):
                    pe.wait_ge(*qs_made(blk, r))
                    for m in range(4):
                        last = pe.transpose(A[0][:, m * P:(m + 1) * P], qk[:, m * P:(m + 1) * P], ident[:, :])
                    last.then_inc(qk_turned.sem, 1)
                    yield
                    pe.wait_ge(*qkT_made(blk, r))
                    pe.wait_ge(*qpar_made(blk, r))
                    pe.wait_ge(*v1_made(blk, r))
                    if r:
                        pe.wait_ge(*x_done[3](blk, r - 1))
                    for n in range(2):
                        for q in range(4):
                            last = pe.matmul(A[q][:, n * D:(n + 1) * D], qkT[32 * q:32 * q + 32, 2 + n, :],
                                             qpar[32 * q:32 * q + 32, n, :, :], start=True, stop=True)
                    last.then_inc(att_raw.sem, 1)
                    yield
                    pe.wait_ge(*am_made(blk, 4 * r))
                    wait_before(pe, lst_made, blk, r)
                    for n in range(2):
                        o = n * LG * EXT
                        pe.matmul(A[0][:, o:o + LG * EXT], qkT[:, n, :], lst[r][:, n, :], start=(n == 0), stop=False,
                                  skip_group_check=True)
                    for q in range(4):
                        if q:
                            pe.wait_ge(*am_made(blk, 4 * r + q))
                        for n in range(2):
                            for j in range(2):
                                hd = LG * n + 2 * q + j
                                last = pe.matmul(A[0][:, hd * EXT:(hd + 1) * EXT],
                                                 am[q][:, n * D + j * P:n * D + (j + 1) * P],
                                                 v3(v1, LH)[:, hd, :], start=False, stop=(hd == LH - 1),
                                                 skip_group_check=True)
                    last.then_inc(ly_raw.sem, 1)
                    for n in range(2):
                        o = n * LG * EXT
                        last = pe.matmul(A[1][:, o:o + LG * EXT], qk[:, D + n * P:D + (n + 1) * P],
                                         v1[:, o:o + LG * EXT], start=True, stop=True)
                    last.then_inc(lst_raw.sem, 1)
                    yield
                    if r < B - 1:
                        project(r + 1)
                        yield
                    pe.wait_ge(*ly_made(blk, r))
                    for m in range(2):
                        last = pe.transpose(A[2][:, m * P:(m + 1) * P], ly[:, m * P:(m + 1) * P], ident[:, :])
                    last.then_inc(ly_turned.sem, 1)
                    yield
                    pe.wait_ge(*lyT_made(blk, r))
                    over_d(A[3][:, 0:D], lambda k: lyT[:, k * P:(k + 1) * P], lambda k: wo[:, k, :]
                           ).then_inc(out2_raw.sem, 1)
                    yield

            def ffn(y, blk, following):
                g = 1 + 2 * y
                w = ffn_w[y]
                h = hT[1]
                for slot in FFN_SLOTS:
                    if slot == "down":
                        pe.wait_ge(*hT_made[g](blk, B - 1))
                        for r in range(B):
                            last = over_d(F[2][:, r * NE:(r + 1) * NE], lambda k: h[:, k, r * P:(r + 1) * P],
                                          lambda k: w[:, W_ROUT + k * NE:W_ROUT + (k + 1) * NE])
                        last.then_inc(logit_raw[y].sem, 1)
                        over_d(F[3][:, :], lambda k: w[:, W_DOWN + k * L:W_DOWN + (k + 1) * L],
                               lambda k: h[:, k, :]).then_inc(lh_raw[y].sem, 1)
                    elif slot[0] == "hidden":
                        for j in slot[1:]:
                            if j == 0:
                                pe.wait_ge(*gl_made[y](blk))
                                if y == 1 and not (isinstance(blk, int) and blk == NBLK - 1):
                                    pe.wait_ge(*x_done[2](blk + 1, B - 1))
                                elif y == 1:
                                    pe.wait_ge(*x_done[4](blk - 1, B - 1))
                                elif not (isinstance(blk, int) and blk == 0):
                                    pe.wait_ge(*x_done[4](blk - 2, B - 1))
                            if j >= 2:
                                pe.wait_ge(*u_made[y](blk, j - 2))
                            c0 = hidden_w(j)
                            pe.matmul(F[j % 2][:, :], w[:, c0:c0 + P], gl[:, :], start=True, stop=True
                                      ).then_inc(hid_raw[y].sem, 1)
                    elif slot == "gates":
                        pe.wait_ge(*gates_made[y](blk))
                        pe.wait_ge(*u_made[y](blk, 4))
                        for r in range(B):
                            last = pe.transpose(F[0][0:GC, r * P:(r + 1) * P], gates[:, r, :], ident[:, :])
                        last.then_inc(gates_turned[y].sem, 1)
                    elif slot[0] == "out":
                        n, r = slot[1:]
                        shared = UNITS[n] == SHARED
                        js = range(UNIT_FIRST[n], UNIT_FIRST[n] + UNIT_TILES[n])
                        if r == 0:
                            if n == 0:
                                pe.wait_ge(*rt_max[y](blk))
                            if n >= 2:
                                pe.wait_ge(*fo_made[y](blk, n - 2))
                            if shared:
                                pe.wait_ge(*gatesT_made[y](blk))
                            pe.wait_ge(*u_made[y](blk, js[-1]))
                        t = slice(r * P, (r + 1) * P)
                        for j in js:
                            c0 = out_w(j)
                            last = pe.matmul(F[2 + n % 2][:, t], u[j % RING][:, t], w[:, c0:c0 + L],
                                             start=(j == js[0]), stop=(j == js[-1] and not shared))
                        if shared:
                            last = pe.matmul(F[2 + n % 2][:, t], gatesT[:, t], cw[y][:, :], start=False, stop=True)
                        if r == B - 1:
                            last.then_inc(exp_raw[y].sem, 1)
                    elif slot == "turn_next":
                        pe.wait_ge(*u_made[y](blk, NT))
                        if following:
                            norm(*following)
                    elif slot == "core":
                        if following:
                            pe.wait_ge(*hT_made[following[0]](following[1], B - 1))
                        pe.wait_ge(*gh_made[y](blk))
                        for r in range(B):
                            t = slice(r * P, (r + 1) * P)
                            o = F[r // 2][:, r % 2 * D:(r % 2 + 1) * D]
                            for k in range(KD):
                                pe.matmul(o, ghT[:, k, t], w[:, W_CORE + k * D:W_CORE + (k + 1) * D],
                                          start=(r % 2 == 0 and k == 0), stop=False,
                                          skip_group_check=True)
                    elif slot == "turn":
                        pe.wait_ge(*fo_made[y](blk, NE))
                        for r in range(B):
                            last = pe.transpose(F[2][:, r * P:(r + 1) * P], fo[:, r * P:(r + 1) * P], ident[:, :])
                        last.then_inc(fo_turned[y].sem, 1)
                    elif slot == "up":
                        pe.wait_ge(*foT_made[y](blk))
                        for r in range(B):
                            t = slice(r * P, (r + 1) * P)
                            o = F[r // 2][:, r % 2 * D:(r % 2 + 1) * D]
                            last = pe.matmul(o, foT[:, t], w[:, W_UP:W_UP + D], start=False, stop=True,
                                             skip_group_check=True)
                            if r % 2:
                                last.then_inc(outf_raw[y].sem, 1)
                    yield

            walk(pe, attn0, ffn, attn1, norm, setup_of)


def v3_(ap, a):
    return ap.rearrange("p (a b) -> p a b", a=a)


def unit_of(j):
    return max(n for n in range(len(UNITS)) if UNIT_FIRST[n] <= j)


def expert_tile(j):
    n = unit_of(j)
    return None if UNITS[n] == SHARED else FIRST[UNITS[n]] + j - UNIT_FIRST[n]


def hidden_col(j):
    t = expert_tile(j)
    return C_S1 if t is None else C_B1 + t


def hidden_w(j):
    t = expert_tile(j)
    return W_S1 if t is None else W_E1 + t * P


def out_w(j):
    t = expert_tile(j)
    return W_S2 if t is None else W_E2 + t * L


def ffn_slots():
    slots = []
    for step in FFN_ORDER:
        if isinstance(step, str):
            slots.append(step)
        elif isinstance(step, tuple):
            slots.append(("hidden", *step))
        else:
            slots += [("out", UNITS.index(step), r) for r in range(B)]
    return slots


FFN_SLOTS = ffn_slots()

AHEAD0 = [0, 5, 2, 4, 5, 1, 1, 1, 2, 0, 4,
          1, 3, 2, 2, 2, 0,
          0, 3, 0, 3, 1, 1,
          0, 4, 0, 3, 0, 2,
          0, 0, 0, 2, 1]
AHEAD1 = [0, 4, 3, 8, 3,
          4, 1, 1, 7, 0, 0,
          3, 2, 2, 0, 0, 0,
          3, 3, 4, 3, 0, 1,
          1, 1, 1, 0, 1]

SETUP_SLOTS = [7, 2]
SETUP_AHEAD0 = [0, 0, 0, 1] * 7 + [0] * (len(AHEAD0) - 28)
SETUP_AHEAD1 = [0, 0, 1, 0, 1] + [0] * (len(AHEAD1) - 5)

NSMALL = 9
SET_C = 2
SET_REP0 = SET_C + 1
SET_ALL = SET_REP0 + 4 + 16 + 1 + 2 + 1 + 1 + DI // P + 2
SET_REP1 = SET_ALL + 1
SET_SEL0 = SET_REP1 + 4 + 16 + NE + 2
SET_SEL1 = SET_SEL0 + 1 + NE + 2
MODC0 = 1
MOD_READ0 = MODC0 + 4
MODC1 = MOD_READ0 + 1
MOD_READ1 = MODC1 + 4
CONST_READ0, CONST_DONE0 = MOD_READ1 + 1, MOD_READ1 + 2
CONST_DONE1 = CONST_DONE0 + 2


def kernel(**inputs):
    import concourse.bacc as bacc
    from concourse.bass_utils import run_bass_kernel_spmd as run

    f = {k: np.ascontiguousarray(v) for k, v in inputs.items()}

    def halves(w):
        return w.reshape(w.shape[0] // P, P, w.shape[1]).transpose(1, 0, 2).reshape(P, -1)

    def over_p(*vecs):
        row = np.concatenate([v.reshape(1, -1) for v in vecs], 1)
        return np.ascontiguousarray(np.broadcast_to(row, (P, row.shape[1])))

    arrays = {"x": f["L0_attn_x"]}
    arrays["w_in"] = halves(f["L0_attn_w_in"]).reshape(P, KD, DIN)
    arrays["w_out"] = halves(f["L0_attn_w_out"]).reshape(P, DI // P, D)
    conv_w = f["L0_attn_conv_w"].reshape(XM, P, CONV).transpose(1, 0, 2).reshape(P, XM * CONV)
    arrays["mam_c"] = np.concatenate([conv_w, f["L0_attn_conv_b"].reshape(XM, P).T,
                                      f["L0_attn_norm_w"].reshape(DI // P, P).T], 1)
    cost = np.array([2 * L * h for h in HID], np.float32) * np.float32(COST_LAMBDA)
    arrays["rows"] = over_p(f["L0_attn_dt_bias"], f["L0_attn_A_log"], f["L0_attn_D"], f["L1_attn_bg"],
                            f["L0_ffn_router_b"], f["L1_ffn_router_b"], cost)
    arrays["c_t"] = np.concatenate([f[f"L{y}_c"].reshape(B, KD, P).transpose(2, 1, 0).reshape(P, -1)
                                    for y in range(2)], 1)
    for y in range(2):
        g = {k[len(f"L{y}_ffn_"):]: v for k, v in f.items() if k.startswith(f"L{y}_ffn_")}
        arrays[f"ffn_w{y}"] = np.concatenate(
            [halves(g["down_w"]), g["up_w"], halves(g["core_w"]), halves(g["router_w"]), g["shared_w1"],
             g["shared_w2"]] + [g[f"e{e}_w1"] for e in range(NE)] + [halves(g[f"e{e}_w2"]) for e in range(NE)], 1)
        arrays[f"ffn_c{y}"] = np.concatenate(
            [g["down_b"].reshape(P, 1), g["shared_b1"].reshape(P, 1)]
            + [g[f"e{e}_b1"].reshape(-1, P).T for e in range(NE)], 1)
        arrays[f"b2rows{y}"] = np.stack([g[f"e{e}_b2"] for e in range(NE)] + [g["shared_b2"]], 0)
        arrays[f"wmod{y}"] = halves(f[f"L{y}_wmod"])
    arrays["ub"] = over_p(f["L0_ffn_up_b"], f["L1_attn_bo"], f["L1_ffn_up_b"])
    arrays["ub2"] = over_p(f["L0_ffn_core_b"], np.zeros(D, np.float32), f["L1_ffn_core_b"])
    arrays["lin_w"] = np.concatenate([halves(np.concatenate([f["L1_attn_Wq"], f["L1_attn_Wk"]], 1)),
                                      halves(f["L1_attn_Wv"]), halves(f["L1_attn_Wg"]),
                                      halves(f["L1_attn_Wo"])], 1)
    half = LD // 2
    inv = (1.0 / np.float32(10000.0) ** (np.arange(half, dtype=np.float32) / np.float32(half))).astype(np.float32)
    ang = np.arange(T, dtype=np.float32)[:, None] * inv[None, :]
    arrays["rope"] = np.concatenate([np.cos(ang), np.sin(ang)], 1).astype(np.float32)

    nc = bacc.Bacc("TRN2", target_bir_lowering=False, num_devices=1)
    dram = {}
    arrays = {k: np.ascontiguousarray(v) for k, v in arrays.items()}
    for k, v in arrays.items():
        dram[k] = nc.dram_tensor(f"in_{k}", list(v.shape), F32, kind="ExternalInput").ap()
    out = nc.dram_tensor("out", [B, T, D], F32, kind="ExternalOutput").ap()
    program(nc, dram, out)
    r = run(nc, [{f"in_{k}": v for k, v in arrays.items()}], core_ids=[0])
    return r.results[0]["out"]
```
